# Optimizing a Trainium2 kernel written in Bass

```python
import numpy as np
import jax
import jax.numpy as jnp

def _softmax(x, axis=-1):
    return jax.nn.softmax(x, axis=axis)
def _gelu(x):
    return jax.nn.gelu(x, approximate=True)
def _silu(x):
    return jax.nn.silu(x)
def _sigmoid(x):
    return jax.nn.sigmoid(x)
def _layernorm(x, axis=-1, eps=1e-5):
    m = jnp.mean(x, axis=axis, keepdims=True)
    v = jnp.var(x, axis=axis, keepdims=True)
    return (x - m) / jnp.sqrt(v + eps)
def _scatter_add(tgt, idx, src, axis=0):
    return tgt.at[idx].add(src)
def _segment_sum(src, seg, n):
    return jax.ops.segment_sum(src, seg, n)

kernel_name = 'mk_vit_tower_cls_d1_tok_img256_2c6c84'

def setup_inputs(seed: int = 0):
    np.random.seed(seed)
    _w = jnp.asarray
    def _rec_inputs():
        import jax
        import jax.numpy as jnp
        _rk = jax.random.key(seed)
        x = (-0.000392918 + 0.999932 * jax.random.normal(jax.random.fold_in(_rk, 1), (2, 64, 64, 256), jnp.float32))
        cls_tok = 0.02 * jax.random.normal(jax.random.fold_in(_rk, 5), (1, 1, 256), jnp.float32)
        return x, cls_tok
    x, cls_tok = _rec_inputs()
    def _L0_tok_setup():
        import jax, jax.numpy as jnp
        import numpy as np
        from jax import lax
        BN_EPS = 1e-05
        key = jax.random.key(seed)
        ks = jax.random.split(key, 9)
        B, H, W, C = (16, 64, 64, 256)
        return {'x': jax.random.normal(ks[0], (B, H, W, C), dtype=jnp.float32), 'bn_gamma': jax.random.uniform(ks[1], (C,), dtype=jnp.float32, minval=0.5, maxval=1.5), 'bn_beta': jax.random.normal(ks[2], (C,), dtype=jnp.float32) * 0.1, 'bn_mean': jax.random.normal(ks[3], (C,), dtype=jnp.float32) * 0.1, 'bn_var': jax.random.uniform(ks[4], (C,), dtype=jnp.float32, minval=0.5, maxval=1.5), 'conv_w': jax.random.normal(ks[5], (C, 1, 3, 3), dtype=jnp.float32) * (1.0 / 3.0), 'conv_b': jax.random.normal(ks[6], (C,), dtype=jnp.float32) * 0.1, 'lin_w': jax.random.normal(ks[7], (C, C), dtype=jnp.float32) * (1.0 / np.sqrt(C)), 'lin_b': jax.random.normal(ks[8], (C,), dtype=jnp.float32) * 0.1}
    _L0_tok_all = _L0_tok_setup()
    _L0_tok_in = {k: v for k, v in _L0_tok_all.items() if k in ('bn_gamma', 'bn_beta', 'bn_mean', 'bn_var', 'conv_w', 'conv_b', 'lin_w', 'lin_b', )}
    del _L0_tok_all

    def _L0_attn_setup():
        import jax, jax.numpy as jnp
        import numpy as np
        key = jax.random.key(seed)
        ks = jax.random.split(key, 4)
        B, S, D = (4, 4096, 256)
        x = jax.random.normal(ks[0], (B, S, D), dtype=jnp.float32)
        Wq = jax.random.normal(ks[1], (D, D), dtype=jnp.float32) * 0.02
        Wk = jax.random.normal(ks[2], (D, D), dtype=jnp.float32) * 0.02
        Wv = jax.random.normal(ks[3], (D, D), dtype=jnp.float32) * 0.02
        bq = jnp.zeros((D,), dtype=jnp.float32)
        bk = jnp.zeros((D,), dtype=jnp.float32)
        bv = jnp.zeros((D,), dtype=jnp.float32)
        return {'x': x, 'Wq': Wq, 'bq': bq, 'Wk': Wk, 'bk': bk, 'Wv': Wv, 'bv': bv}
    _L0_attn_all = _L0_attn_setup()
    _L0_attn_in = {k: v for k, v in _L0_attn_all.items() if k in ('Wq', 'bq', 'Wk', 'bk', 'Wv', 'bv', )}
    del _L0_attn_all

    def _L0_ffn_setup():
        import math
        import jax, jax.numpy as jnp
        import numpy as np
        CAPACITY_FACTOR = 1.25
        key = jax.random.key(seed)
        ks = jax.random.split(key, 5)
        B, L, D, F, E = (8, 8192, 256, 1024, 8)
        h = jax.random.normal(ks[0], (B, L, D), dtype=jnp.float32)
        gate_w = jax.random.normal(ks[1], (D, E), dtype=jnp.float32) * 0.02
        gate_b = jnp.zeros((E,), dtype=jnp.float32)
        w1 = jax.random.normal(ks[2], (E, D, F), dtype=jnp.float32) * (1.0 / math.sqrt(D))
        b1 = jnp.zeros((E, F), dtype=jnp.float32)
        w2 = jax.random.normal(ks[3], (E, F, D), dtype=jnp.float32) * (1.0 / math.sqrt(F))
        b2 = jnp.zeros((E, D), dtype=jnp.float32)
        return {'h': h, 'gate_w': gate_w, 'gate_b': gate_b, 'w1': w1, 'b1': b1, 'w2': w2, 'b2': b2}
    _L0_ffn_all = _L0_ffn_setup()
    _L0_ffn_in = {k: v for k, v in _L0_ffn_all.items() if k in ('gate_w', 'gate_b', 'w1', 'b1', 'w2', 'b2', )}
    del _L0_ffn_all

    return {
        "x": x,
        "cls_tok": cls_tok,
        "L0_tok_bn_gamma": _L0_tok_in["bn_gamma"],
        "L0_tok_bn_beta": _L0_tok_in["bn_beta"],
        "L0_tok_bn_mean": _L0_tok_in["bn_mean"],
        "L0_tok_bn_var": _L0_tok_in["bn_var"],
        "L0_tok_conv_w": _L0_tok_in["conv_w"],
        "L0_tok_conv_b": _L0_tok_in["conv_b"],
        "L0_tok_lin_w": _L0_tok_in["lin_w"],
        "L0_tok_lin_b": _L0_tok_in["lin_b"],
        "L0_attn_Wq": _L0_attn_in["Wq"],
        "L0_attn_bq": _L0_attn_in["bq"],
        "L0_attn_Wk": _L0_attn_in["Wk"],
        "L0_attn_bk": _L0_attn_in["bk"],
        "L0_attn_Wv": _L0_attn_in["Wv"],
        "L0_attn_bv": _L0_attn_in["bv"],
        "L0_ffn_gate_w": _L0_ffn_in["gate_w"],
        "L0_ffn_gate_b": _L0_ffn_in["gate_b"],
        "L0_ffn_w1": _L0_ffn_in["w1"],
        "L0_ffn_b1": _L0_ffn_in["b1"],
        "L0_ffn_w2": _L0_ffn_in["w2"],
        "L0_ffn_b2": _L0_ffn_in["b2"],
    }

def reference(x, cls_tok, L0_tok_bn_gamma, L0_tok_bn_beta, L0_tok_bn_mean, L0_tok_bn_var, L0_tok_conv_w, L0_tok_conv_b, L0_tok_lin_w, L0_tok_lin_b, L0_attn_Wq, L0_attn_bq, L0_attn_Wk, L0_attn_bk, L0_attn_Wv, L0_attn_bv, L0_ffn_gate_w, L0_ffn_gate_b, L0_ffn_w1, L0_ffn_b1, L0_ffn_w2, L0_ffn_b2):
    import jax
    import jax.numpy as jnp
    def _L0_tok_ref(x, bn_gamma, bn_beta, bn_mean, bn_var, conv_w, conv_b, lin_w, lin_b):
        import jax, jax.numpy as jnp
        import numpy as np
        from jax import lax
        BN_EPS = 1e-05
        x = jnp.transpose(x, (0, 3, 1, 2))
        B, C, H, W = x.shape
        scale = bn_gamma / jnp.sqrt(bn_var + BN_EPS)
        shift = bn_beta - bn_mean * scale
        xn = x * scale[None, :, None, None] + shift[None, :, None, None]
        y = lax.conv_general_dilated(xn, conv_w, window_strides=(1, 1), padding='SAME', feature_group_count=C, dimension_numbers=('NCHW', 'OIHW', 'NCHW')) + conv_b[None, :, None, None]
        y = jnp.transpose(y.reshape(B, C, H * W), (0, 2, 1))
        return jnp.einsum('bnc,dc->bnd', y, lin_w) + lin_b

    def _L0_attn_ref(x, Wq, bq, Wk, bk, Wv, bv):
        import jax, jax.numpy as jnp
        import numpy as np
        Q = jnp.einsum('bsd,de->bse', x, Wq) + bq
        K = jnp.einsum('bsd,de,->bse'.replace(',->', '->'), x, Wk) + bk
        V = jnp.einsum('bsd,de->bse', x, Wv) + bv
        scale = 1.0 / jnp.sqrt(jnp.asarray(Q.shape[-1], dtype=jnp.float32))
        scores = jnp.einsum('bqd,bkd->bqk', Q, K) * scale
        weights = jax.nn.softmax(scores, axis=-1)
        return jnp.einsum('bqk,bkd->bqd', weights, V)

    def _L0_ffn_ref(h, gate_w, gate_b, w1, b1, w2, b2):
        import math
        import jax, jax.numpy as jnp
        import numpy as np
        CAPACITY_FACTOR = 1.25
        B, L, D = h.shape
        E = gate_w.shape[1]
        T = B * L
        C = max(1, math.ceil(CAPACITY_FACTOR * T / E))
        x = h.reshape(T, D)
        logits = x @ gate_w + gate_b
        probs = jax.nn.softmax(logits, axis=-1)
        idx = jnp.argmax(probs, axis=-1)
        prb = jnp.take_along_axis(probs, idx[:, None], axis=1)[:, 0]
        one_hot = jax.nn.one_hot(idx, E, dtype=jnp.float32)
        pos = (jnp.cumsum(one_hot, axis=0) * one_hot).sum(-1).astype(jnp.int32) - 1
        kept = pos < C
        pos_safe = jnp.where(kept, pos, C)
        buf = jnp.zeros((E, C, D), dtype=h.dtype).at[idx, pos_safe].set(x, mode='drop')
        hmid = jax.nn.relu(jnp.einsum('ecd,edf->ecf', buf, w1) + b1[:, None, :])
        ybuf = jnp.einsum('ecf,efd->ecd', hmid, w2) + b2[:, None, :]
        pos_g = jnp.minimum(pos, C - 1)
        y_tok = ybuf[idx, pos_g] * (prb * kept)[:, None]
        y = y_tok.reshape(B, L, D)
        y = jnp.nan_to_num(y, nan=0.0, posinf=10000.0, neginf=-10000.0)
        return y

    h = _L0_tok_ref(x, L0_tok_bn_gamma, L0_tok_bn_beta, L0_tok_bn_mean, L0_tok_bn_var, L0_tok_conv_w, L0_tok_conv_b, L0_tok_lin_w, L0_tok_lin_b)
    h = jnp.concatenate([jnp.broadcast_to(cls_tok, (h.shape[0], 1, h.shape[2])), h], axis=1)
    h = h + _L0_attn_ref(_layernorm(h, axis=-1), L0_attn_Wq, L0_attn_bq, L0_attn_Wk, L0_attn_bk, L0_attn_Wv, L0_attn_bv)
    h = h + _L0_ffn_ref(_layernorm(h, axis=-1), L0_ffn_gate_w, L0_ffn_gate_b, L0_ffn_w1, L0_ffn_b1, L0_ffn_w2, L0_ffn_b2)
    return h


_drawn_inputs = setup_inputs


def setup_inputs(seed=0):
    import zlib

    import numpy as np

    out = dict(_drawn_inputs(seed))
    spreads = {'L0_attn_bq': (0.0, 0.8),
     'L0_attn_bk': (0.0, 2.0),
     'L0_attn_bv': (0.0, 0.1),
     'L0_ffn_gate_b': (0.0, 0.1),
     'L0_ffn_b1': (0.0, 0.635),
     'L0_ffn_b2': (0.0, 0.448)}
    factors = {'cls_tok': 172.677, 'L0_attn_Wq': 6.379, 'L0_attn_Wk': 7.384}
    for name, (base, spread) in spreads.items():
        noise = np.random.default_rng([zlib.crc32(name.encode()), seed]).standard_normal(out[name].shape)
        drawn = base * np.exp(spread * noise) if base else spread * noise
        out[name] = jnp.asarray(drawn.astype(out[name].dtype))
    for name, factor in factors.items():
        out[name] = (out[name] * factor).astype(out[name].dtype)
    return out
```

```python
import concourse.bass as bass
from concourse import mybir

F32, F16, I32 = mybir.dt.float32, mybir.dt.float16, mybir.dt.int32
ALU, ACT, AX = mybir.AluOpType, mybir.ActivationFunctionType, mybir.AxisListType

B, IMG, D, E, F = 2, 64, 256, 8, 1024
P = 128
NP = IMG * IMG
N = NP + 1
T = B * N
DC, FC = D // P, F // P
CAP = -(-5 * T // (4 * E))
GT = -(-CAP // P)
STRIDE = GT * P
QB = 512
NQB = NP // QB
SUB = QB // P
KT = NP // P + 1
LAST = KT - 1
ROWS8 = QB // IMG
PW = IMG + 2
VW = D + 1
ROW = 2 * D + 1
A_SCALE, P_SCALE, TOP = 2.0 ** 10, 2.0 ** 14, 2.0 ** 13
NONE = T
BIG = float(2 ** 20)
EPS = 1e-5


class Names:
    pass


def semaphores(nc, names):
    return [nc.alloc_semaphore(n) for n in names.split()]


def clear(nc, s):
    with nc.Block() as block:
        @block.gpsimd
        def _(pool):
            for handle in s.handles:
                pool.sem_clear(handle)


def setup(nc, g, a):
    s = Names()
    (s.w_in, s.c_made, s.w0_max, s.w0_red, s.sc_made, s.w0_hi) = \
        s.handles = semaphores(nc, "w_in c_made w0_max w0_red sc_made w0_hi")
    W = (a["L0_attn_Wq"], a["L0_attn_Wk"], a["L0_attn_Wv"])
    with nc.Block() as block:
        @block.sync
        def _(sp):
            for i in range(3):
                sp.dma_start(g.w_raw[:, i], W[i].rearrange("(c p) e -> p c e", p=P)).then_inc(s.w_in, 16)
            sp.dma_start(g.lin_t[:], a["lin_wT"].rearrange("(c p) d -> p c d", p=P)).then_inc(s.w_in, 16)
            sp.dma_start(g.gate_w[:], a["L0_ffn_gate_w"].rearrange("(c p) e -> p c e", p=P)).then_inc(s.w_in, 16)
            sp.dma_start(g.taps[:], a["conv_taps"].rearrange("(c p) k -> p c k", p=P)).then_inc(s.w_in, 16)
            with nc.allow_non_contiguous_dma(reason="vectors of 256 onto the partitions"):
                for i, n in enumerate(("L0_tok_bn_gamma", "L0_tok_bn_beta", "L0_tok_bn_mean", "L0_tok_bn_var",
                                       "L0_tok_conv_b", "L0_attn_bq", "L0_attn_bk", "L0_attn_bv")):
                    sp.dma_start(g.vecs[:, i], a[n].rearrange("(c p) -> p c", p=P)).then_inc(s.w_in, 16)
            for dst, n in ((g.lin_b, "L0_tok_lin_b"), (g.bv, "L0_attn_bv"), (g.gate_b, "L0_ffn_gate_b")):
                sp.dma_start(dst[:], a[n].rearrange("(a n) -> a n", a=1).to_broadcast((P, a[n].shape[0])))\
                    .then_inc(s.w_in, 16)
            sp.wait_ge(s.c_made, 1)
            sp.dma_start(g.table.rearrange("(p n) a -> p (n a)", p=P), g.none_i[:]).then_inc(s.w_in, 16)
            sp.dma_start(g.rows[T:T + 1, :], g.zrow[0:1, :]).then_inc(s.w_in, 16)
            sp.wait_ge(s.w_in, 16 * 19)

        @block.gpsimd
        def _(pool):
            pool.memset(g.ones[:], 1.0)
            pool.memset(g.none_f[:], float(NONE))
            pool.memset(g.zrow[:], 0.0)
            pool.memset(g.ident[:], 0.0)
            pool.memset(g.expo[:], -0.5)
            pool.memset(g.carry[:], 0.0)
            pool.memset(g.ones16[:], 1.0)
            pool.iota(g.iota_i[:], [[P, SUB]], base=0, channel_multiplier=1)
            pool.iota(g.weight_i[:], [[0, SUB], [-1, E]], base=E, channel_multiplier=0)
            pool.iota(g.base_i[:], [[0, SUB], [STRIDE, E]], base=-1, channel_multiplier=0)
            pool.drain()
            pool.affine_select(out=g.ident[:], in_=g.ident[:], compare_op=ALU.not_equal, fill=1.0, base=0,
                               pattern=[[-1, P]], channel_multiplier=1)
            pool.affine_select(out=g.upper[:], in_=g.ones16[:], compare_op=ALU.is_ge, fill=0.0, base=0,
                               pattern=[[1, P]], channel_multiplier=-1)
            pool.tensor_copy(g.none_i[:], g.none_f[:])
            pool.tensor_copy(g.tok_f[:], g.iota_i[:])
            pool.tensor_copy(g.weight[:], g.weight_i[:])
            pool.tensor_copy(g.slot0[:], g.base_i[:])
            pool.drain().then_inc(s.c_made, 1)
            pool.wait_ge(s.w0_max, 1)
            pool.partition_all_reduce(g.mx[:, 0:6], g.mx[:, 0:6], P, bass.bass_isa.ReduceOp.max).then_inc(s.w0_red, 1)
            pool.wait_ge(s.sc_made, 1)
            pool.tensor_tensor(g.bn_r[:], g.bn_v[:], g.expo[:, 0:DC], ALU.pow)
            pool.drain().then_inc(s.w0_red, 1)

        @block.vector
        def _(dve):
            dve.wait_ge(s.w_in, 16 * 19)
            for i in range(3):
                nc.vector.tensor_reduce(g.mx[:, i:i + 1], g.w_raw[:, i], axis=AX.XY, op=ALU.max,
                                        apply_absolute_value=True)
                nc.vector.tensor_reduce(g.mx[:, 3 + i:4 + i], g.vecs[:, 5 + i], axis=AX.X, op=ALU.max,
                                        apply_absolute_value=True)
            nc.vector.tensor_scalar(g.bn_v[:], g.vecs[:, 3], EPS, None, ALU.add)
            dve.drain().then_inc(s.w0_max, 1)
            dve.wait_ge(s.w0_red, 1)
            nc.vector.scalar_tensor_tensor(out=g.mx[:, 3:6], in0=g.mx[:, 0:3], scalar=float(D), in1=g.mx[:, 3:6],
                                           op0=ALU.mult, op1=ALU.add)
            dve.drain()
            scale_of(nc, dve, g.sc[:, 0:6], g.isc[:, 0:6], g.mx[:, 0:6])
            nc.vector.tensor_tensor(g.ratio[:], g.sc[:, 3:6], g.isc[:, 0:3], ALU.mult)
            nc.vector.tensor_tensor(g.score[:], g.isc[:, 3:4], g.isc[:, 4:5], ALU.mult)
            dve.drain()
            nc.vector.tensor_scalar(g.ratio[:], g.ratio[:], 1.0 / A_SCALE, None, ALU.mult)
            nc.vector.tensor_scalar(g.score[:], g.score[:], float(D) ** -0.5, None, ALU.mult)
            for i in range(2):
                nc.vector.tensor_scalar(g.bqk[:, i], g.vecs[:, 5 + i], g.sc[:, 3 + i:4 + i], None, ALU.mult)
            dve.drain().then_inc(s.sc_made, 1)
            dve.wait_ge(s.w0_red, 2)
            nc.vector.tensor_tensor(g.bn_s[:], g.vecs[:, 0], g.bn_r[:], ALU.mult)
            dve.drain()
            nc.vector.tensor_tensor(g.bn_h[:], g.vecs[:, 2], g.bn_s[:], ALU.mult)
            dve.drain()
            nc.vector.tensor_tensor(g.bn_h[:], g.vecs[:, 1], g.bn_h[:], ALU.subtract)
            dve.wait_ge(s.w0_hi, 1)
            for i in range(3):
                nc.vector.scalar_tensor_tensor(out=g.w_lo[:, i], in0=g.w_raw[:, i], scalar=g.sc[:, i:i + 1],
                                               in1=g.w_hi[:, i], op0=ALU.mult, op1=ALU.subtract)

        @block.scalar
        def _(act):
            act.wait_ge(s.sc_made, 1)
            for i in range(3):
                last = nc.scalar.activation(g.w_hi[:, i], g.w_raw[:, i], ACT.Copy, scale=g.sc[:, i:i + 1])
            last.then_inc(s.w0_hi, 1)


def scale_of(nc, dve, scale, inverse, bound):
    nc.vector.tensor_scalar(inverse, bound, 2.0 ** -30, 2.0 ** 60, ALU.max, ALU.min)
    dve.drain()
    nc.vector.tensor_scalar(inverse.bitcast(I32), inverse.bitcast(I32), 0x7F800000, None, ALU.bitwise_and)
    dve.drain()
    nc.vector.reciprocal(scale, inverse)
    dve.drain()
    nc.vector.tensor_scalar(scale, scale, TOP, None, ALU.mult)
    nc.vector.tensor_scalar(inverse, inverse, 1.0 / TOP, None, ALU.mult)
    dve.drain()


def wait(engine, semaphore, value):
    if not isinstance(value, int) or value > 0:
        engine.wait_ge(semaphore, value)


def settle(g, engine):
    engine.sem_inc(g.settled, 1)


def tokenizer(nc, g, a, b, s):
    ps, xp = g.ps, g.xp

    def projected(m, i, parts):
        w, c = m // 2, m % 2
        if w < 2:
            return parts[w][:, c, bass.ds(i * QB, QB)], g.p_f[:, m % 2]
        return parts[2][:, bass.ds(i * SUB + 2 * c, 2), 0:D], g.p_f[:, m % 2].rearrange("p (t d) -> p t d", d=D)

    with nc.Block() as block:
        @block.sync
        def _(sp):
            def load(i):
                wait(sp, s.xn, i)
                sp.dma_start(g.x_in[:], a["xT"][b, :, bass.ds(i * QB, QB)].rearrange("(c p) n -> p c n", p=P))\
                    .then_inc(s.x_in, 16)

            def store(i):
                wait(sp, s.h_made, i + 1)
                sp.dma_start(g.h_res[b, bass.ds(i * QB, QB), :].rearrange("(t p) d -> p t d", p=P), g.h[:])\
                    .then_inc(s.h_out, 16)

            load(0)
            with sp.Fori(1, NQB) as i:
                load(i)
            with sp.Fori(0, NQB) as i:
                store(i)
            sp.wait_ge(s.h_out, 16 * NQB)

        @block.scalar
        def _(act):
            nc.scalar.activation(g.warm[:], g.ones[:, 0:1], ACT.Exp)
            act.wait_ge(s.cleared, 1)
            with act.Fori(0, NQB) as i:
                act.wait_ge(s.x_in, i * 16 + 16)
                for c in range(DC):
                    last = nc.scalar.activation(xp[:, c, bass.ds(i * ROWS8 + 1, ROWS8), 1:1 + IMG],
                                                g.x_in[:, c].rearrange("p (r w) -> p r w", w=IMG), ACT.Identity,
                                                scale=g.bn_s[:, c:c + 1], bias=g.bn_h[:, c:c + 1])
                act.drain().then_inc(s.xn, 1)

            def project(i):
                act.wait_ge(s.aT, i + 1)
                wait(act, s.proj, i * 6)
                nc.scalar.activation(g.a_hi[:], ps[:, 2:4], ACT.Copy, scale=A_SCALE).then_inc(s.a_hi, 1)
                for m in range(6):
                    act.wait_ge(s.proj, i * 6 + m + 1)
                    wait(act, s.p_lo, i * 6 + m - 1)
                    bias = g.bqk[:, m // 2, m % 2:m % 2 + 1] if m < 4 else 0.0
                    nc.scalar.activation(g.p_f[:, m % 2], ps[:, 4 + m % 4], ACT.Identity,
                                         scale=g.ratio[:, m // 2:m // 2 + 1], bias=bias)
                    act.drain().then_inc(s.p_f, 1)
                    out, src = projected(m, i, (g.q_hi, g.k_hi, g.v_hi))
                    nc.scalar.activation(out, src, ACT.Copy).then_inc(s.p_hi, 1)

            project(0)
            with act.Fori(1, NQB) as i:
                project(i)

        @block.gpsimd
        def _(pool):
            def root(i):
                pool.wait_ge(s.var, i + 1)
                pool.tensor_tensor(g.rstd[:], g.var[:], g.expo[:, 0:SUB], ALU.pow).then_inc(s.rstd, 1)

            def low(i):
                for m in range(6):
                    pool.wait_ge(s.p_hi, i * 6 + m + 1)
                    out, src = projected(m, i, (g.q_lo, g.k_lo, g.v_lo))
                    hi, _ = projected(m, i, (g.q_hi, g.k_hi, g.v_hi))
                    pool.tensor_tensor(out, src, hi, ALU.subtract).then_inc(s.p_lo, 1)

            root(0)
            root(1)
            with pool.Fori(2, NQB) as i:
                low(i - 2)
                root(i)
            low(NQB - 2)
            low(NQB - 1)

        @block.tensor
        def _(pe):
            def linear(i):
                pe.wait_ge(s.y_t, i + 1)
                wait(pe, s.h_made, i)
                for t in range(SUB):
                    for c in range(DC):
                        last = nc.tensor.matmul(ps[:, t // 2, (t % 2) * D:(t % 2 + 1) * D],
                                                g.y_t[:, c, t * P:(t + 1) * P], g.lin_t[:, c],
                                                start=c == 0, stop=c == DC - 1)
                last.then_inc(s.lin, 1)

            def turn(i):
                pe.wait_ge(s.a, i + 1)
                wait(pe, s.a_lo, i)
                for c in range(DC):
                    for t in range(SUB):
                        last = nc.tensor.transpose(ps[:, 2 + c, t * P:(t + 1) * P], g.a[:, t, c * P:(c + 1) * P],
                                                   g.ident[:])
                last.then_inc(s.aT, 1)

            def project(i):
                pe.wait_ge(s.a_lo, i + 1)
                for m in range(6):
                    wait(pe, s.p_f, i * 6 + m - 1)
                    w, c, out = m // 2, m % 2, ps[:, 4 + m % 4]
                    for t in range(1 if w < 2 else 2):
                        n = 0
                        for k in range(DC):
                            for x, y in ((g.w_hi, g.a_hi), (g.w_hi, g.a_lo), (g.w_lo, g.a_hi)):
                                if w < 2:
                                    last = nc.tensor.matmul(out, x[:, w, k, c * P:(c + 1) * P], y[:, k],
                                                            start=n == 0, stop=n == 5)
                                else:
                                    last = nc.tensor.matmul(out[:, t * D:(t + 1) * D],
                                                            y[:, k, (2 * c + t) * P:(2 * c + t + 1) * P], x[:, w, k],
                                                            start=n == 0, stop=n == 5)
                                n += 1
                    last.then_inc(s.proj, 1)

            linear(0)
            linear(1)
            turn(0)
            linear(2)
            turn(1)
            project(0)
            with pe.Fori(3, NQB) as i:
                linear(i)
                turn(i - 1)
                project(i - 2)
            turn(NQB - 1)
            project(NQB - 2)
            project(NQB - 1)

        @block.vector
        def _(dve):
            nc.vector.memset(xp[:], 0.0)
            dve.drain().then_inc(s.cleared, 1)
            nc.vector.memset(g.v_hi[:, :, D:VW], 1.0)

            def conv(i, last=False):
                dve.wait_ge(s.xn, NQB if last else i + 2)
                wait(dve, s.lin, i)
                for k in range(9):
                    for c in range(DC):
                        view = xp[:, c, bass.ds(i * ROWS8 + k // 3, ROWS8), k % 3:k % 3 + IMG]
                        out = g.y_t[:, c].rearrange("p (r w) -> p r w", w=IMG)
                        if k == 0:
                            nc.vector.tensor_scalar(out, view, g.taps[:, c, 0:1], g.vecs[:, 4, c:c + 1],
                                                    ALU.mult, ALU.add)
                        else:
                            nc.vector.scalar_tensor_tensor(out=out, in0=view, scalar=g.taps[:, c, k:k + 1], in1=out,
                                                           op0=ALU.mult, op1=ALU.add)
                    dve.drain()
                dve.drain().then_inc(s.y_t, 1)

            def rows(i):
                dve.wait_ge(s.lin, i + 1)
                wait(dve, s.h_out, i * 16)
                for t in range(SUB):
                    nc.vector.tensor_tensor(g.h[:, t], ps[:, t // 2, (t % 2) * D:(t % 2 + 1) * D], g.lin_b[:], ALU.add)
                dve.drain().then_inc(s.h_made, 1)
                stats(nc, dve, g, g.h, SUB)
                dve.drain().then_inc(s.var, 1)

            def norm(i):
                dve.wait_ge(s.rstd, i + 1)
                wait(dve, s.aT, i)
                for t in range(SUB):
                    nc.vector.tensor_scalar(g.a[:, t], g.h[:, t], g.mv[:, t, 0:1], g.rstd[:, t:t + 1],
                                            ALU.subtract, ALU.mult)
                dve.drain().then_inc(s.a, 1)

            def low(i):
                dve.wait_ge(s.a_hi, i + 1)
                nc.vector.scalar_tensor_tensor(out=g.a_lo[:], in0=ps[:, 2:4], scalar=A_SCALE, in1=g.a_hi[:],
                                               op0=ALU.mult, op1=ALU.subtract)
                dve.drain().then_inc(s.a_lo, 1)

            conv(0)
            rows(0)
            conv(1)
            norm(0)
            with dve.Fori(2, NQB - 1) as i:
                rows(i - 1)
                low(i - 2)
                conv(i)
                norm(i - 1)
            rows(NQB - 2)
            low(NQB - 3)
            conv(NQB - 1, last=True)
            norm(NQB - 2)
            rows(NQB - 1)
            low(NQB - 2)
            norm(NQB - 1)
            low(NQB - 1)


def stats(nc, dve, g, x, nt, np_=P):
    for t in range(nt):
        nc.vector.bn_stats(g.st[0:np_, t], x[0:np_, t])
    dve.drain()
    for t in range(nt):
        nc.vector.bn_aggr(g.mv[0:np_, t], g.st[0:np_, t])
    dve.drain()
    nc.vector.tensor_scalar(g.var[0:np_, 0:nt], g.mv[0:np_, 0:nt, 1], EPS, None, ALU.add)


def class_token(nc, g, a, b, s):
    ps = g.ps

    def step(engine, n):
        engine.drain().then_inc(s.step, 1)

    with nc.Block() as block:
        @block.sync
        def _(sp):
            sp.dma_start(g.h[0:1, 0], a["cls_tok"][0]).then_inc(s.x_in, 16)

        @block.gpsimd
        def _(pool):
            pool.wait_ge(s.step, 1)
            pool.tensor_tensor(g.rstd[0:1, 0:1], g.var[0:1, 0:1], g.expo[0:1, 0:1], ALU.pow)
            step(pool, 2)
            pool.tensor_tensor(g.hb[0:1, 0], g.h[0:1, 0], g.bv[0:1], ALU.add)
            pool.drain().then_inc(s.hb, 1)
            ep_pool_root(nc, g, s, pool, 0, 1, 1)
            ep_pool_table(nc, g, s, pool, 0, 1)

        @block.vector
        def _(dve):
            dve.wait_ge(s.x_in, 16 * (NQB + 1))
            stats(nc, dve, g, g.h, 1, 1)
            step(dve, 1)
            dve.wait_ge(s.step, 2)
            nc.vector.tensor_scalar(g.a[0:1, 0], g.h[0:1, 0], g.mv[0:1, 0, 0:1], g.rstd[0:1, 0:1],
                                    ALU.subtract, ALU.mult)
            step(dve, 3)
            dve.wait_ge(s.step, 5)
            nc.vector.scalar_tensor_tensor(out=g.a_lo[:, :, 0:1], in0=ps[:, 2:4, 0:1], scalar=A_SCALE,
                                           in1=g.a_hi[:, :, 0:1], op0=ALU.mult, op1=ALU.subtract)
            step(dve, 6)
            dve.wait_ge(s.step, 8)
            for w, (hi, lo) in enumerate(((g.q_hi, g.q_lo), (g.k_hi, g.k_lo))):
                nc.vector.tensor_tensor(lo[:, :, NP], g.p_f[:, 0, 2 * w:2 * w + 2], hi[:, :, NP], ALU.subtract)
            nc.vector.tensor_tensor(g.v_lo[0:1, LAST], g.p_f[0:1, 1, 0:D], g.v_hi[0:1, LAST, 0:D], ALU.subtract)
            step(dve, 9)
            dve.wait_ge(s.step, 10)
            nc.vector.tensor_copy(g.c_s[:, 0:LAST], ps[:, 6, 0:LAST])
            nc.vector.tensor_copy(g.c_s[0:1, LAST:KT], ps[0:1, 6, LAST:KT])
            dve.drain()
            nc.vector.reduce_max(g.c_m[:], g.c_s[:, 0:LAST], axis=AX.X)
            dve.drain()
            nc.vector.tensor_tensor(g.c_m[0:1], g.c_m[0:1], g.c_s[0:1, LAST:KT], ALU.max)
            step(dve, 11)
            dve.wait_ge(s.step, 12)
            nc.vector.reduce_max(g.c_m1[0:1], ps[0:1, 7, 0:P], axis=AX.X)
            step(dve, 13)
            dve.wait_ge(s.step, 14)
            nc.vector.tensor_copy(g.c_m[:], ps[:, 7, P:P + 1])
            dve.drain()
            nc.vector.tensor_scalar(g.c_s[:, 0:LAST], g.c_s[:, 0:LAST], g.c_m[:], None, ALU.subtract)
            nc.vector.tensor_scalar(g.c_s[0:1, LAST:KT], g.c_s[0:1, LAST:KT], g.c_m[0:1], None, ALU.subtract)
            step(dve, 15)
            dve.wait_ge(s.step, 16)
            nc.vector.scalar_tensor_tensor(out=g.c_lo[:, 0:LAST], in0=g.c_s[:, 0:LAST], scalar=P_SCALE,
                                           in1=g.c_hi[:, 0:LAST], op0=ALU.mult, op1=ALU.subtract)
            nc.vector.scalar_tensor_tensor(out=g.c_lo[0:1, LAST:KT], in0=g.c_s[0:1, LAST:KT], scalar=P_SCALE,
                                           in1=g.c_hi[0:1, LAST:KT], op0=ALU.mult, op1=ALU.subtract)
            step(dve, 17)
            dve.wait_ge(s.step, 18)
            ep_evacuate(nc, g, s, dve, 0, 1, 1)
            ep_stats(nc, g, s, dve, 0, 1, 1)
            ep_norm(nc, g, s, dve, 0, 1, 1)
            ep_route(nc, g, s, dve, 0, 1, 1)
            ep_slots(nc, g, s, dve, 0, 1, 1)

        @block.scalar
        def _(act):
            nc.scalar.activation(g.warm[:], g.ones[:, 0:1], ACT.Exp)
            act.wait_ge(s.step, 4)
            nc.scalar.activation(g.a_hi[:, :, 0:1], ps[:, 2:4, 0:1], ACT.Copy, scale=A_SCALE)
            step(act, 5)
            act.wait_ge(s.step, 7)
            for m in range(4):
                nc.scalar.activation(g.p_f[:, 0, m:m + 1], ps[:, 4, m:m + 1], ACT.Identity,
                                     scale=g.ratio[:, m // 2:m // 2 + 1], bias=g.bqk[:, m // 2, m % 2:m % 2 + 1])
            nc.scalar.activation(g.p_f[0:1, 1, 0:D], ps[0:1, 5, 0:D], ACT.Copy, scale=g.ratio[0:1, 2:3])
            act.drain()
            nc.scalar.activation(g.q_hi[:, :, NP], g.p_f[:, 0, 0:2], ACT.Copy)
            nc.scalar.activation(g.k_hi[:, :, NP], g.p_f[:, 0, 2:4], ACT.Copy)
            nc.scalar.activation(g.v_hi[0:1, LAST, 0:D], g.p_f[0:1, 1, 0:D], ACT.Copy)
            step(act, 8)
            act.wait_ge(s.step, 15)
            nc.scalar.activation(g.c_s[:, 0:LAST], g.c_s[:, 0:LAST], ACT.Exp, scale=g.score[:])
            nc.scalar.activation(g.c_s[0:1, LAST:KT], g.c_s[0:1, LAST:KT], ACT.Exp, scale=g.score[0:1])
            act.drain()
            nc.scalar.activation(g.c_hi[:, 0:LAST], g.c_s[:, 0:LAST], ACT.Copy, scale=P_SCALE)
            nc.scalar.activation(g.c_hi[0:1, LAST:KT], g.c_s[0:1, LAST:KT], ACT.Copy, scale=P_SCALE)
            step(act, 16)
            ep_columns(nc, g, s, act, 0, 0, 1, 1)
            ep_columns(nc, g, s, act, 0, 1, 1, 1)
            ep_exp(nc, g, s, act, 0, 1, 1)

        @block.tensor
        def _(pe):
            pe.wait_ge(s.step, 3)
            for c in range(DC):
                nc.tensor.transpose(ps[:, 2 + c, 0:1], g.a[0:1, 0, c * P:(c + 1) * P], g.ident[0:1, 0:1])
            step(pe, 4)
            pe.wait_ge(s.step, 6)
            for m in range(4):
                products(nc, ps[:, 4, m:m + 1], [(g.w_hi[:, m // 2, k, m % 2 * P:(m % 2 + 1) * P],
                                                  g.w_lo[:, m // 2, k, m % 2 * P:(m % 2 + 1) * P],
                                                  g.a_hi[:, k, 0:1], g.a_lo[:, k, 0:1]) for k in range(DC)])
            products(nc, ps[0:1, 5, 0:D], [(g.a_hi[:, k, 0:1], g.a_lo[:, k, 0:1], g.w_hi[:, 2, k], g.w_lo[:, 2, k])
                                           for k in range(DC)])
            step(pe, 7)
            pe.wait_ge(s.step, 9)
            with pe.Fori(0, LAST) as t:
                keys = bass.ds(t * P, P)
                products(nc, ps[:, 6, bass.ds(t, 1)], [(g.k_hi[:, k, keys], g.k_lo[:, k, keys],
                                                        g.q_hi[:, k, NP:N], g.q_lo[:, k, NP:N]) for k in range(DC)])
            products(nc, ps[0:1, 6, LAST:KT], [(g.k_hi[:, k, NP:N], g.k_lo[:, k, NP:N],
                                                g.q_hi[:, k, NP:N], g.q_lo[:, k, NP:N]) for k in range(DC)])
            step(pe, 10)
            pe.wait_ge(s.step, 11)
            nc.tensor.transpose(ps[0:1, 7, 0:P], g.c_m[:], g.ident[:])
            step(pe, 12)
            pe.wait_ge(s.step, 13)
            nc.tensor.matmul(ps[:, 7, P:P + 1], g.ones[0:1, :], g.c_m1[0:1], start=True, stop=True)
            step(pe, 14)
            pe.wait_ge(s.step, 17)

            def values(t, np_, first, last):
                at = bass.ds(t, 1)
                v, vl = g.v_hi[0:np_, t, :], g.v_lo[0:np_, t, :]
                nc.tensor.matmul(ps[0:1, 0, 0:VW], g.c_hi[0:np_, at], v, start=first, stop=False)
                nc.tensor.matmul(ps[0:1, 0, 0:D], g.c_hi[0:np_, at], vl, start=False, stop=False)
                nc.tensor.matmul(ps[0:1, 0, 0:VW], g.c_lo[0:np_, at], v, start=False, stop=last)

            values(0, P, True, False)
            with pe.Fori(1, LAST) as t:
                values(t, P, False, False)
            values(LAST, 1, False, True)
            step(pe, 18)
            ep_turn(nc, g, s, pe, 0, 0, 1, 1)
            ep_turn(nc, g, s, pe, 0, 1, 1, 1)
            ep_logits(nc, g, s, pe, 0, 1, 1)
            ep_prefix(nc, g, s, pe, 0, 1, 1)

    with nc.Block() as block:
        @block.sync
        def _(sp):
            sp.dma_start(a["out"][b, 0:1, :], g.row[0:1, 0, D:2 * D]).then_inc(s.o_out, 16)
            sp.dma_start(g.rows[bass.ds(b * N, 1), :], g.row[0:1, 0]).then_inc(s.r_out, 16)
            sp.wait_ge(s.o_out, 16)
            sp.wait_ge(s.r_out, 16)


def products(nc, out, parts, start=True, stop=True):
    for i, (x_hi, x_lo, y_hi, y_lo) in enumerate(parts):
        nc.tensor.matmul(out, x_hi, y_hi, start=start and i == 0, stop=False)
        nc.tensor.matmul(out, x_hi, y_lo, start=False, stop=False)
        last = nc.tensor.matmul(out, x_lo, y_hi, start=False, stop=stop and i == len(parts) - 1)
    return last



def ep_evacuate(nc, g, s, dve, n, np_, nt):
    wait(dve, s.o_out, n * 16)
    wait(dve, s.r_out, n * 16)
    dve.wait_ge(s.hb, n + 1)
    nc.vector.reciprocal(g.rs[0:np_, 0:nt], g.ps[0:np_, 0:nt, D])
    dve.drain()
    nc.vector.tensor_scalar(g.rs[0:np_, 0:nt], g.rs[0:np_, 0:nt], g.isc[0:np_, 5:6], None, ALU.mult)
    dve.drain()
    for t in range(nt):
        nc.vector.scalar_tensor_tensor(out=g.row[0:np_, t, D:2 * D], in0=g.ps[0:np_, t, 0:D],
                                       scalar=g.rs[0:np_, t:t + 1], in1=g.hb[0:np_, t], op0=ALU.mult, op1=ALU.add)
    dve.drain().then_inc(s.o, 1)


def ep_stats(nc, g, s, dve, n, np_, nt):
    stats(nc, dve, g, g.row[:, :, D:2 * D], nt, np_)
    dve.drain().then_inc(s.var2, 1)


def ep_pool_root(nc, g, s, pool, n, np_, nt):
    pool.wait_ge(s.var2, n + 1)
    pool.tensor_tensor(g.rstd[0:np_, 0:nt], g.var[0:np_, 0:nt], g.expo[0:np_, 0:nt], ALU.pow).then_inc(s.rstd2, 1)


def ep_norm(nc, g, s, dve, n, np_, nt):
    dve.wait_ge(s.rstd2, n + 1)
    for t in range(nt):
        nc.vector.tensor_scalar(g.row[0:np_, t, 0:D], g.row[0:np_, t, D:2 * D], g.mv[0:np_, t, 0:1],
                                g.rstd[0:np_, t:t + 1], ALU.subtract, ALU.mult)
    dve.drain().then_inc(s.z, 1)


def ep_turn(nc, g, s, pe, n, c, np_, nt):
    pe.wait_ge(s.z, n + 1)
    if c:
        pe.wait_ge(s.z_t, n * DC + c)
    for t in range(nt):
        last = nc.tensor.transpose(g.ps[:, 7, t * P:t * P + np_], g.row[0:np_, t, c * P:(c + 1) * P],
                                   g.ident[0:np_, 0:np_])
    last.then_inc(s.zT, 1)


def ep_columns(nc, g, s, act, n, c, np_, nt):
    act.wait_ge(s.zT, n * DC + c + 1)
    src = g.ps[:, 7, 0:nt * P] if np_ == P else g.ps[:, 7, 0:np_]
    nc.scalar.activation(g.z_t[:, c, 0:nt * P] if np_ == P else g.z_t[:, c, 0:np_], src, ACT.Copy).then_inc(s.z_t, 1)


def ep_logits(nc, g, s, pe, n, np_, nt):
    pe.wait_ge(s.z_t, n * DC + DC)
    for t in range(nt):
        for c in range(DC):
            last = nc.tensor.matmul(g.ps[0:np_, 7, t * E:(t + 1) * E], g.z_t[:, c, t * P:t * P + np_], g.gate_w[:, c],
                                    start=c == 0, stop=c == DC - 1)
    last.then_inc(s.logits, 1)


def ep_exp(nc, g, s, act, n, np_, nt):
    act.wait_ge(s.l_sub, n + 1)
    nc.scalar.activation(g.r_e[0:np_, 0:nt], g.r_l[0:np_, 0:nt], ACT.Exp).then_inc(s.l_exp, 1)


def ep_route(nc, g, s, dve, n, np_, nt):
    v = nc.vector
    l, e, key, oh = (x[0:np_, 0:nt] for x in (g.r_l, g.r_e, g.r_k, g.r_oh))
    m, d, k = (x[0:np_, 0:nt] for x in (g.r_m, g.r_d, g.r_x))
    wide = lambda x: x.unsqueeze(2).to_broadcast((np_, nt, E))
    dve.wait_ge(s.logits, n + 1)
    v.tensor_tensor(l, g.ps[0:np_, 7, 0:nt * E].rearrange("p (t e) -> p t e", e=E),
                    g.gate_b[0:np_].unsqueeze(1).to_broadcast((np_, nt, E)), ALU.add)
    dve.drain()
    v.reduce_max(m, l, axis=AX.X)
    dve.drain()
    v.tensor_tensor(l, l, wide(m), ALU.subtract)
    dve.drain().then_inc(s.l_sub, 1)
    dve.wait_ge(s.l_exp, n + 1)
    v.reduce_max(m, e, axis=AX.X)
    v.reduce_sum(d, e, axis=AX.X)
    dve.drain()
    v.reciprocal(d, d)
    v.tensor_tensor(key, e, wide(m), ALU.is_equal)
    dve.drain()
    v.tensor_tensor(g.row[0:np_, 0:nt, 2 * D], m, d, ALU.mult)
    v.tensor_tensor(key, key, g.weight[0:np_, 0:nt], ALU.mult)
    dve.drain()
    v.reduce_max(k, key, axis=AX.X)
    dve.drain()
    v.tensor_tensor(oh, key, wide(k), ALU.is_equal)
    dve.drain().then_inc(s.routed, 1)


def ep_prefix(nc, g, s, pe, n, np_, nt):
    pe.wait_ge(s.routed, n + 1)
    for t in range(nt):
        out = g.ps[0:np_, 7, 64 + t * E:64 + (t + 1) * E]
        for u in range(t):
            nc.tensor.matmul(out, g.ones16[0:np_, 0:np_], g.r_oh[0:np_, u], start=u == 0, stop=False)
        nc.tensor.matmul(out, g.upper[0:np_, 0:np_], g.r_oh[0:np_, t], start=t == 0, stop=True)
    for t in range(nt):
        last = nc.tensor.matmul(g.ps[:, 7, 128:128 + E], g.ones16[0:np_, :], g.r_oh[0:np_, t], start=t == 0,
                                stop=t == nt - 1)
    last.then_inc(s.prefix, 1)


def ep_slots(nc, g, s, dve, n, np_, nt):
    v = nc.vector
    c, d = g.r_l[0:np_, 0:nt], g.r_e[0:np_, 0:nt]
    dve.wait_ge(s.prefix, n + 1)
    if isinstance(n, int) and n == 0:
        v.memset(g.idx_f[:], BIG)
        dve.drain()
    else:
        dve.wait_ge(s.tab, s.tab0 + (n - 1) * 16 * SUB + 16)
    v.tensor_tensor(c, g.ps[0:np_, 7, 64:64 + nt * E].rearrange("p (t e) -> p t e", e=E),
                    g.carry[0:np_].unsqueeze(1).to_broadcast((np_, nt, E)), ALU.add)
    dve.drain()
    v.tensor_tensor(g.carry[:], g.ps[:, 7, 128:128 + E], g.carry[:], ALU.add)
    v.tensor_scalar(d, c, float(CAP), BIG, ALU.is_gt, ALU.mult)
    dve.drain()
    v.tensor_tensor(c, c, g.slot0[0:np_, 0:nt], ALU.add)
    dve.drain()
    v.tensor_tensor(c, c, d, ALU.add)
    dve.drain()
    v.tensor_tensor(c, c, g.r_oh[0:np_, 0:nt], ALU.mult)
    dve.drain()
    v.reduce_sum(g.idx_f[0:np_, 0:nt], c, axis=AX.X)
    v.tensor_copy(g.tok_i[:], g.tok_f[:])
    dve.drain()
    v.tensor_copy(g.idx_i[:], g.idx_f[:])
    v.tensor_scalar(g.tok_f[:], g.tok_f[:], float(QB if np_ == P else 1), None, ALU.add)
    dve.drain().then_inc(s.slots, 1)


def ep_pool_table(nc, g, s, pool, n, nt):
    pool.wait_ge(s.slots, n + 1)
    settle(g, pool)
    for t in range(nt):
        pool.indirect_dma_start(out=g.table[:, :], out_offset=bass.IndirectOffsetOnAxis(ap=g.idx_i[:, t:t + 1], axis=0),
                                in_=g.tok_i[:, t:t + 1], in_offset=None, bounds_check=E * STRIDE - 1,
                                oob_is_err=False).then_inc(s.tab, 16)


SEGMENTS = ((0, 1), (1, 3), (3, 5), (5, 7), (7, 9), (9, 10))


def attention(nc, g, a, b, s):
    ps = g.ps

    def keys_loop(engine, body, hooks=None):
        for (lo, hi), hook in zip(SEGMENTS if hooks else ((0, 1), (1, 10)), hooks or (None, None)):
            if hi - lo == 1:
                for k in range(3):
                    body(3 * lo + k, k)
            else:
                with engine.Fori(lo, hi) as r:
                    for k in range(3):
                        body(r * 3 + k, k)
            if hook:
                hook()
        for k in range(3):
            body(30 + k, k)

    def rounds(engine, one):
        one(0, True, False, None)
        one(1, True, True, None)
        with engine.Fori(2, NQB) as j:
            one(j, True, True, j - 1)
        one(NQB, False, True, NQB - 1)
        one(NQB + 1, False, False, NQB)

    with nc.Block() as block:
        @block.sync
        def _(sp):
            def rows(n):
                return bass.ds((n - 1) * QB + 1, QB)

            def load(n):
                sp.wait_ge(s.o, n)
                sp.dma_start(g.hb[:], g.h_res[b, bass.ds((n - 1) * QB, QB), :].rearrange("(t p) d -> p t d", p=P))\
                    .then_inc(s.h_in, 16)

            def store(n):
                sp.wait_ge(s.o, n + 1)
                sp.dma_start(a["out"][b, rows(n), :].rearrange("(t p) d -> p t d", p=P), g.row[:, :, D:2 * D])\
                    .then_inc(s.o_out, 16)
                sp.wait_ge(s.routed, n + 1)
                sp.dma_start(g.rows[bass.ds(b * N + (n - 1) * QB + 1, QB), :].rearrange("(t p) d -> p t d", p=P),
                             g.row[:]).then_inc(s.r_out, 16)

            load(1)
            with sp.Fori(2, NQB + 1) as n:
                load(n)
                store(n - 1)
            store(NQB)
            sp.wait_ge(s.o_out, 16 * (NQB + 1))
            sp.wait_ge(s.r_out, 16 * (NQB + 1))

        @block.gpsimd
        def _(pool):
            def subtract(j, t):
                np_ = 1 if isinstance(t, int) and t == LAST else P
                x = g.panel[0:np_, t]
                pool.tensor_tensor(x, x, g.m[0:np_], ALU.subtract).then_inc(s.sub, 1)

            def one(j, scores, values, n):
                def bias(m):
                    pool.wait_ge(s.h_in, m * 16)
                    for t in range(SUB):
                        pool.tensor_tensor(g.hb[:, t], g.hb[:, t], g.bv[:], ALU.add)
                    pool.drain().then_inc(s.hb, 1)

                if not values:
                    if n is not None:
                        ep_pool_root(nc, g, s, pool, n, P, SUB)
                        ep_pool_table(nc, g, s, pool, n, SUB)
                    return
                pool.wait_ge(s.m, j)
                settle(g, pool)
                body = lambda t, k: subtract(j, t)
                if n is None:
                    bias(1)
                    keys_loop(pool, body)
                else:
                    keys_loop(pool, body, (None, lambda: ep_pool_root(nc, g, s, pool, n, P, SUB), None,
                                           lambda: bias(n + 1), None, None))
                    ep_pool_table(nc, g, s, pool, n, SUB)

            rounds(pool, one)
            pool.wait_ge(s.tab, s.tab0 + 16 * (SUB * NQB + 1))
            settle(g, pool)

        @block.scalar
        def _(act):
            nc.scalar.activation(g.warm[:], g.ones[:, 0:1], ACT.Exp)

            def weights(j, t, k):
                i = (j - 1) * KT + t
                last = isinstance(t, int) and t == LAST
                np_ = 1 if last else P
                act.wait_ge(s.sub, i + 1)
                x = g.panel[0:np_, t]
                nc.scalar.activation(x, x, ACT.Exp, scale=g.score[0:np_])
                act.drain()
                if not (isinstance(i, int) and i <= 2):
                    act.wait_ge(s.pv, i - 2)
                    settle(g, act)
                nc.scalar.activation(g.ph[0:np_, k], x, ACT.Copy, scale=P_SCALE).then_inc(s.p_hi2, 1)

            def keep(j, t, k):
                np_ = 1 if isinstance(t, int) and t == LAST else P
                act.wait_ge(s.qk, j * KT + t + 1)
                if not (isinstance(j, int) and j == 0):
                    act.wait_ge(s.p_lo2, (j - 1) * KT + t + 1)
                settle(g, act)
                nc.scalar.activation(g.panel[0:np_, t], ps[0:np_, 4 + k], ACT.Copy).then_inc(s.kept, 1)

            def one(j, scores, values, n):
                if values:
                    weights(j, 0, 0)

                def body(t, k):
                    if values and not (isinstance(t, int) and t == LAST):
                        weights(j, t + 1, (k + 1) % 3)
                    if scores:
                        keep(j, t, k)

                hooks = None
                if n is not None:
                    hooks = (None, None, lambda: ep_columns(nc, g, s, act, n, 0, P, SUB),
                             lambda: ep_columns(nc, g, s, act, n, 1, P, SUB),
                             lambda: ep_exp(nc, g, s, act, n, P, SUB), None)
                if scores or values:
                    keys_loop(act, body, hooks)
                else:
                    for hook in hooks[2:5]:
                        hook()
                if scores:
                    act.wait_ge(s.m_ps, j + 1)
                    nc.scalar.activation(g.m[:], ps[:, 7], ACT.Copy).then_inc(s.m, 1)

            rounds(act, one)

        @block.vector
        def _(dve):
            def low(j, t, k):
                last = isinstance(t, int) and t == LAST
                np_ = 1 if last else P
                dve.wait_ge(s.p_hi2, (j - 1) * KT + t + 1)
                nc.vector.scalar_tensor_tensor(out=g.pl[0:np_, k], in0=g.panel[0:np_, t], scalar=P_SCALE,
                                               in1=g.ph[0:np_, k], op0=ALU.mult, op1=ALU.subtract).then_inc(s.p_lo2, 1)

            def largest(j, t):
                np_ = 1 if isinstance(t, int) and t == LAST else P
                dve.wait_ge(s.kept, j * KT + t + 1)
                nc.vector.tensor_tensor(g.r[0:np_], g.r[0:np_], g.panel[0:np_, t], ALU.max)
                dve.drain().then_inc(s.maxed, 1)

            def one(j, scores, values, n):
                if n is not None:
                    dve.wait_ge(s.pv, n * KT)
                    ep_evacuate(nc, g, s, dve, n, P, SUB)
                if values:
                    low(j, 0, 0)
                if scores:
                    wait(dve, s.r_t, j)
                    nc.vector.memset(g.r[:], -3.0e38)
                    dve.drain()

                def body(t, k):
                    if values and not (isinstance(t, int) and t == LAST):
                        low(j, t + 1, (k + 1) % 3)
                    if scores:
                        largest(j, t)

                hooks = None
                if n is not None:
                    hooks = (lambda: ep_stats(nc, g, s, dve, n, P, SUB), lambda: ep_norm(nc, g, s, dve, n, P, SUB),
                             None, None, lambda: ep_route(nc, g, s, dve, n, P, SUB), None)
                if scores or values:
                    keys_loop(dve, body, hooks)
                else:
                    for hook in hooks:
                        if hook:
                            hook()
                if n is not None:
                    ep_slots(nc, g, s, dve, n, P, SUB)
                if scores:
                    dve.wait_ge(s.r_t, j + 1)
                    nc.vector.reduce_max(g.mq[:], ps[:, 7].rearrange("p (t q) -> p t q", q=P), axis=AX.X)
                    dve.drain()
                    for t in range(SUB):
                        nc.vector.tensor_scalar(g.diag[:, t * P:(t + 1) * P], g.ident[:], g.mq[:, t:t + 1], None,
                                                ALU.mult)
                    dve.drain().then_inc(s.diag, 1)

            rounds(dve, one)

        @block.tensor
        def _(pe):
            def score(j, t, k):
                i = j * KT + t
                last = isinstance(t, int) and t == LAST
                queries = bass.ds(j * QB, QB)
                keys = slice(NP, N) if last else bass.ds(t * P, P)
                wait(pe, s.kept, i - 2)
                if last:
                    settle(g, pe)
                out = ps[0:1, 4 + k] if last else ps[:, 4 + k]
                products(nc, out, [(g.k_hi[:, c, keys], g.k_lo[:, c, keys], g.q_hi[:, c, queries],
                                    g.q_lo[:, c, queries]) for c in range(DC)]).then_inc(s.qk, 1)

            def value(j, t, k):
                i = (j - 1) * KT + t
                first, last = isinstance(t, int) and t == 0, isinstance(t, int) and t == LAST
                np_ = 1 if last else P
                pe.wait_ge(s.p_lo2, i + 1)
                if first:
                    pe.wait_ge(s.o, j)
                v, vl = g.v_hi[0:np_, t], g.v_lo[0:np_, t]
                for u in range(SUB):
                    q = slice(u * P, (u + 1) * P)
                    nc.tensor.matmul(ps[:, u, 0:VW], g.ph[0:np_, k, q], v, start=first, stop=False)
                    nc.tensor.matmul(ps[:, u, 0:D], g.ph[0:np_, k, q], vl, start=False, stop=False)
                    mm = nc.tensor.matmul(ps[:, u, 0:VW], g.pl[0:np_, k, q], v, start=False, stop=last)
                mm.then_inc(s.pv, 1)

            def one(j, scores, values, n):
                def body(t, k):
                    if scores:
                        score(j, t, k)
                    if values:
                        value(j, t, k)

                hooks = None
                if n is not None:
                    hooks = (None, None, lambda: ep_turn(nc, g, s, pe, n, 0, P, SUB),
                             lambda: ep_turn(nc, g, s, pe, n, 1, P, SUB),
                             lambda: ep_logits(nc, g, s, pe, n, P, SUB),
                             lambda: ep_prefix(nc, g, s, pe, n, P, SUB))
                if scores or values:
                    keys_loop(pe, body, hooks)
                else:
                    for hook in hooks[2:]:
                        hook()
                if scores:
                    pe.wait_ge(s.maxed, (j + 1) * KT)
                    if n is not None:
                        pe.wait_ge(s.slots, n + 1)
                    for t in range(SUB):
                        mm = nc.tensor.transpose(ps[:, 7, t * P:(t + 1) * P], g.r[:, t * P:(t + 1) * P], g.ident[:])
                    mm.then_inc(s.r_t, 1)
                    pe.wait_ge(s.diag, j + 1)
                    nc.tensor.matmul(ps[:, 7], g.ones[:], g.diag[:], start=True, stop=True).then_inc(s.m_ps, 1)

            rounds(pe, one)


GROUPS = tuple((at, min(QB, CAP - at)) for at in range(0, CAP, QB))
NG = len(GROUPS)
PAIR = 2


def expert_loads(nc, g, a, sp, e, half, sem):
    sp.dma_start(g.w1_raw[:], a["L0_ffn_w1"][e].rearrange("(c p) f -> p c f", p=P)).then_inc(sem, 16)
    sp.dma_start(g.w2_raw[:], a["L0_ffn_w2"][e].rearrange("(c p) d -> p c d", p=P)).then_inc(sem, 16)
    with nc.allow_non_contiguous_dma(reason="a bias onto the partitions"):
        sp.dma_start(g.b1[:, half], a["L0_ffn_b1"][e].rearrange("(c p) -> p c", p=P)).then_inc(sem, 16)
    sp.dma_start(g.b2[:, half], a["L0_ffn_b2"][e].rearrange("(a n) -> a n", a=1).to_broadcast((P, D)))\
        .then_inc(sem, 16)


def expert_largest(nc, g, dve, half, which):
    if which == 0:
        nc.vector.tensor_reduce(g.f_mx[:, half, 0:1], g.w1_raw[:], axis=AX.XY, op=ALU.max, apply_absolute_value=True)
    else:
        nc.vector.tensor_reduce(g.f_mx[:, half, 1:2], g.w2_raw[:], axis=AX.XY, op=ALU.max, apply_absolute_value=True)
        nc.vector.tensor_reduce(g.f_mx[:, half, 2:3], g.b1[:, half], axis=AX.X, op=ALU.max, apply_absolute_value=True)


def expert_scales(nc, g, dve, half):
    v, m = nc.vector, g.f_mx[:, half]
    sc, isc = g.f_sc[:, half], g.f_isc[:, half]
    v.scalar_tensor_tensor(out=m[:, 2:3], in0=m[:, 0:1], scalar=float(D), in1=m[:, 2:3], op0=ALU.mult, op1=ALU.add)
    dve.drain()
    scale_of(nc, dve, sc, isc, m)
    v.tensor_tensor(g.f_in[:, half], sc[:, 2:3], isc[:, 0:1], ALU.mult)
    v.tensor_tensor(g.f_out[:, half], isc[:, 2:3], isc[:, 1:2], ALU.mult)
    v.tensor_scalar(g.b1[:, half], g.b1[:, half], sc[:, 2:3], None, ALU.mult)
    dve.drain()
    v.tensor_scalar(g.f_in[:, half], g.f_in[:, half], 1.0 / A_SCALE, None, ALU.mult)


def expert_high(nc, g, half, which):
    raw, hi = ((g.w1_raw, g.w1_hi), (g.w2_raw, g.w2_hi))[which]
    return nc.scalar.activation(hi[:, half], raw[:], ACT.Copy, scale=g.f_sc[:, half, which:which + 1])


def expert_low(nc, g, half, which):
    raw, hi, lo = ((g.w1_raw, g.w1_hi, g.w1_lo), (g.w2_raw, g.w2_hi, g.w2_lo))[which]
    return nc.vector.scalar_tensor_tensor(out=lo[:, half], in0=raw[:], scalar=g.f_sc[:, half, which:which + 1],
                                          in1=hi[:, half], op0=ALU.mult, op1=ALU.subtract)


def first_expert(nc, g, a):
    s = Names()
    (s.f0_in, s.f0_max, s.f0_red, s.f0_sc, s.f0_hi) = s.handles = semaphores(nc, "f0_in f0_max f0_red f0_sc f0_hi")
    with nc.Block() as block:
        @block.sync
        def _(sp):
            expert_loads(nc, g, a, sp, 0, 0, s.f0_in)

        @block.vector
        def _(dve):
            nc.vector.memset(g.y[:], 0.0)
            nc.vector.memset(g.huge[:, 0:1], 10000.0)
            nc.vector.memset(g.huge[:, 1:2], -10000.0)
            dve.wait_ge(s.f0_in, 64)
            expert_largest(nc, g, dve, 0, 0)
            expert_largest(nc, g, dve, 0, 1)
            dve.drain().then_inc(s.f0_max, 1)
            dve.wait_ge(s.f0_red, 1)
            expert_scales(nc, g, dve, 0)
            dve.drain().then_inc(s.f0_sc, 1)
            dve.wait_ge(s.f0_hi, 1)
            expert_low(nc, g, 0, 0)
            expert_low(nc, g, 0, 1)

        @block.gpsimd
        def _(pool):
            pool.wait_ge(s.f0_max, 1)
            pool.partition_all_reduce(g.f_mx[:, 0], g.f_mx[:, 0], P, bass.bass_isa.ReduceOp.max).then_inc(s.f0_red, 1)

        @block.scalar
        def _(act):
            act.wait_ge(s.f0_sc, 1)
            expert_high(nc, g, 0, 0)
            expert_high(nc, g, 0, 1)
            act.drain().then_inc(s.f0_hi, 1)


def experts(nc, g, a, ep, s):
    ps = g.ps
    every = [(half, k) for half in range(PAIR) for k in range(NG)]
    tiles = [-(-GROUPS[k][1] // P) for _, k in every]
    total = len(every)
    out = a["out"].rearrange("b n d -> (b n) d")

    def got(i):
        return ep * (16 * sum(tiles[i % 2::2])) + 16 * sum(tiles[i % 2:i + 1:2])

    def put(i):
        return ep * (16 * sum(tiles)) + 16 * sum(tiles[:i])

    def rows_of(i, t):
        return min(P, GROUPS[every[i][1]][1] - t * P)

    with nc.Block() as block:
        @block.sync
        def _(sp):
            with nc.allow_non_contiguous_dma(reason="token numbers onto the partitions"):
                for i, (half, k) in enumerate(every):
                    at = ep * (PAIR * STRIDE) + (half * STRIDE + GROUPS[k][0])
                    sp.dma_start(g.ids[:, i, 0:tiles[i]], g.table[bass.ds(at, tiles[i] * P), 0]
                                 .rearrange("(t p) -> p t", p=P)).then_inc(s.ids[i], 16)
            expert_loads(nc, g, a, sp, ep * 2 + 1, 1, s.f_w)
            sp.wait_ge(s.w_low, 2)
            sp.wait_ge(s.y_made, NG)
            expert_loads(nc, g, a, sp, (ep * 2 + 2) % E, 0, s.f_w)

        @block.gpsimd
        def _(pool):
            def gather(i):
                pool.wait_ge(s.ids[i], 16)
                for t in range(tiles[i]):
                    pool.indirect_dma_start(out=g.tok[:, i % 2, t], out_offset=None, in_=g.rows[:, :],
                                            in_offset=bass.IndirectOffsetOnAxis(ap=g.ids[:, i, t:t + 1], axis=0))\
                        .then_inc(s.got[i % 2], 16)

            def scatter(i):
                pool.wait_ge(s.y_done, i + 1)
                for t in range(tiles[i]):
                    pool.indirect_dma_start(out=out, out_offset=bass.IndirectOffsetOnAxis(ap=g.ids[:, i, t:t + 1],
                                                                                          axis=0),
                                            in_=g.y[:, t], in_offset=None, bounds_check=T - 1, oob_is_err=False)\
                        .then_inc(s.put, 16)

            gather(0)
            gather(1)
            for i, (half, k) in enumerate(every):
                if k == 1:
                    pool.wait_ge(s.w_max, half + 1)
                    pool.partition_all_reduce(g.f_mx[:, 1 - half], g.f_mx[:, 1 - half], P,
                                              bass.bass_isa.ReduceOp.max).then_inc(s.w_red, 1)
                scatter(i)
                if i + 2 < total:
                    gather(i + 2)
            pool.wait_ge(s.put, put(total))
            settle(g, pool)

        @block.scalar
        def _(act):
            nc.scalar.activation(g.warm[:], g.ones[:, 0:1], ACT.Exp)

            def high(i):
                act.wait_ge(s.turned, i + 1)
                w = tiles[i] * P
                nc.scalar.activation(g.x_hi[:, i % 2, :, 0:w], ps[:, 6:8, 0:w], ACT.Copy, scale=A_SCALE)\
                    .then_inc(s.x_high, 1)

            high(0)
            for i, (half, k) in enumerate(every):
                w = GROUPS[k][1]
                for f in range(FC):
                    n = i * FC + f
                    if f == 5 and i + 1 < total:
                        high(i + 1)
                    act.wait_ge(s.l1, n + 1)
                    wait(act, s.h_low, n - 1)
                    nc.scalar.activation(g.hf[:, n % 2, 0:w], ps[:, 4 + n % 2, 0:w], ACT.Relu,
                                         scale=g.f_in[:, half], bias=g.b1[:, half, f:f + 1])
                    act.drain().then_inc(s.relu, 1)
                    wait(act, s.l2, n - 1)
                    nc.scalar.activation(g.hh[:, n % 2, 0:w], g.hf[:, n % 2, 0:w], ACT.Copy).then_inc(s.h_high, 1)
                    if (k, f) in ((1, 7), (2, 0)):
                        act.wait_ge(s.w_sc, half + 1)
                        expert_high(nc, g, 1 - half, 0 if k == 1 else 1)
                        act.drain().then_inc(s.w_high, 1)

        @block.vector
        def _(dve):
            def low(i):
                dve.wait_ge(s.x_high, i + 1)
                w = tiles[i] * P
                nc.vector.scalar_tensor_tensor(out=g.x_lo[:, i % 2, :, 0:w], in0=ps[:, 6:8, 0:w], scalar=A_SCALE,
                                               in1=g.x_hi[:, i % 2, :, 0:w], op0=ALU.mult, op1=ALU.subtract)\
                    .then_inc(s.x_low, 1)

            def collect(i):
                half = every[i][0]
                dve.wait_ge(s.l2, (i + 1) * FC)
                if i:
                    dve.wait_ge(s.put, put(i))
                for t in range(tiles[i]):
                    m = rows_of(i, t)
                    nc.vector.scalar_tensor_tensor(out=g.y[0:m, t], in0=ps[0:m, t, 0:D], scalar=g.f_out[0:m, half],
                                                   in1=g.b2[0:m, half], op0=ALU.mult, op1=ALU.add)
                dve.drain().then_inc(s.y_made, 1)
                dve.wait_ge(s.got[i % 2], got(i))
                for t in range(tiles[i]):
                    nc.vector.tensor_scalar(g.y[:, t], g.y[:, t], g.tok[:, i % 2, t, 2 * D:ROW], None, ALU.mult)
                dve.drain()

            def guard(i):
                v, w = nc.vector, tiles[i]
                y, ok, bad = g.y[:, 0:w], g.guarded[:, 0:w], g.mask[:, 0:w]
                v.memset(ok, 0.0)
                v.tensor_tensor(bad, y, y, ALU.is_equal)
                dve.drain()
                v.copy_predicated(ok, bad, y)
                dve.drain()
                for n, inf in enumerate((float("inf"), float("-inf"))):
                    v.tensor_scalar(bad, y, inf, None, ALU.is_equal)
                    dve.drain()
                    v.copy_predicated(ok, bad, g.huge[:, n:n + 1].unsqueeze(2).to_broadcast((P, w, D)))
                    dve.drain()
                v.tensor_tensor(y, ok, g.tok[:, i % 2, 0:w, D:2 * D], ALU.add)
                dve.drain().then_inc(s.y_done, 1)

            low(0)
            for i, (half, k) in enumerate(every):
                w = GROUPS[k][1]
                for f in range(FC):
                    n = i * FC + f
                    if f == 5 and i + 1 < total:
                        low(i + 1)
                    dve.wait_ge(s.h_high, n + 1)
                    nc.vector.tensor_tensor(g.hl[:, n % 2, 0:w], g.hf[:, n % 2, 0:w], g.hh[:, n % 2, 0:w],
                                            ALU.subtract).then_inc(s.h_low, 1)
                    if i and f == 0:
                        collect(i - 1)
                    if i and f == 1:
                        guard(i - 1)
                    if (k, f) in ((1, 2), (1, 4)):
                        dve.wait_ge(s.f_w, 64 * (half + 1))
                        expert_largest(nc, g, dve, 1 - half, 0 if f == 2 else 1)
                        if f == 4:
                            dve.drain().then_inc(s.w_max, 1)
                    if (k, f) == (1, 6):
                        dve.wait_ge(s.w_red, half + 1)
                        expert_scales(nc, g, dve, 1 - half)
                        dve.drain().then_inc(s.w_sc, 1)
                    if (k, f) in ((2, 1), (2, 3)):
                        which = 0 if f == 1 else 1
                        dve.wait_ge(s.w_high, half * 2 + which + 1)
                        expert_low(nc, g, 1 - half, which)
                        dve.drain().then_inc(s.w_low, 1)
            collect(total - 1)
            guard(total - 1)

        @block.tensor
        def _(pe):
            def turn(i):
                pe.wait_ge(s.got[i % 2], got(i))
                wait(pe, s.x_low, i)
                for c in range(DC):
                    for t in range(tiles[i]):
                        last = nc.tensor.transpose(ps[:, 6 + c, t * P:(t + 1) * P],
                                                   g.tok[:, i % 2, t, c * P:(c + 1) * P], g.ident[:])
                last.then_inc(s.turned, 1)

            def hidden(n):
                i, f = n // FC, n % FC
                half, k = every[i]
                w = GROUPS[k][1]
                if f == 0:
                    pe.wait_ge(s.x_low, i + 1)
                if (k, f) == (0, 0) and half:
                    pe.wait_ge(s.w_low, 2)
                wait(pe, s.relu, n - 1)
                cols = slice(f * P, (f + 1) * P)
                products(nc, ps[:, 4 + n % 2, 0:w], [(g.w1_hi[:, half, c, cols], g.w1_lo[:, half, c, cols],
                                                      g.x_hi[:, i % 2, c, 0:w], g.x_lo[:, i % 2, c, 0:w])
                                                     for c in range(DC)]).then_inc(s.l1, 1)

            def output(n):
                i, f = n // FC, n % FC
                half = every[i][0]
                pe.wait_ge(s.h_low, n + 1)
                if f == 0:
                    wait(pe, s.y_made, i)
                for t in range(tiles[i]):
                    m = rows_of(i, t)
                    at = slice(t * P, t * P + m)
                    last = products(nc, ps[0:m, t, 0:D], [(g.hh[:, n % 2, at], g.hl[:, n % 2, at],
                                                           g.w2_hi[:, half, f], g.w2_lo[:, half, f])],
                                    start=f == 0, stop=f == FC - 1)
                last.then_inc(s.l2, 1)

            turn(0)
            hidden(0)
            for n in range(total * FC):
                if n % FC == 4 and n // FC + 1 < total:
                    turn(n // FC + 1)
                if n + 1 < total * FC:
                    hidden(n + 1)
                output(n)


class Arena:

    def __init__(self, words, at):
        self.words, self.at = words, at

    def take(self, shape, dt):
        n = 1
        for x in shape[1:]:
            n *= x
        n = n if dt != F16 else n // 2
        view = self.words[:, self.at:self.at + n]
        self.at += n
        if dt != F32:
            view = view.bitcast(dt)
        if len(shape) == 3:
            view = view.rearrange("p (a b) -> p a b", b=shape[2])
        if len(shape) == 4:
            view = view.rearrange("p (a b c) -> p a b c", b=shape[2], c=shape[3])
        return view


def tower(nc, a):
    g = Names()
    g.w_hi = nc.alloc_sbuf_tensor("w_hi", [P, 3, DC, D], F16)
    g.w_lo = nc.alloc_sbuf_tensor("w_lo", [P, 3, DC, D], F16)
    g.lin_t = nc.alloc_sbuf_tensor("lin_t", [P, DC, D], F32)
    g.gate_w = nc.alloc_sbuf_tensor("gate_w", [P, DC, E], F32)
    g.taps = nc.alloc_sbuf_tensor("taps", [P, DC, 9], F32)
    g.vecs = nc.alloc_sbuf_tensor("vecs", [P, 8, DC], F32)
    g.lin_b = nc.alloc_sbuf_tensor("lin_b", [P, D], F32)
    g.bv = nc.alloc_sbuf_tensor("bv", [P, D], F32)
    g.gate_b = nc.alloc_sbuf_tensor("gate_b", [P, E], F32)
    g.mx = nc.alloc_sbuf_tensor("mx", [P, 6], F32)
    g.sc = nc.alloc_sbuf_tensor("sc", [P, 6], F32)
    g.isc = nc.alloc_sbuf_tensor("isc", [P, 6], F32)
    g.ratio = nc.alloc_sbuf_tensor("ratio", [P, 3], F32)
    g.score = nc.alloc_sbuf_tensor("score", [P, 1], F32)
    g.bqk = nc.alloc_sbuf_tensor("bqk", [P, 2, DC], F32)
    g.bn_v = nc.alloc_sbuf_tensor("bn_v", [P, DC], F32)
    g.bn_r = nc.alloc_sbuf_tensor("bn_r", [P, DC], F32)
    g.bn_s = nc.alloc_sbuf_tensor("bn_s", [P, DC], F32)
    g.bn_h = nc.alloc_sbuf_tensor("bn_h", [P, DC], F32)
    g.ones = nc.alloc_sbuf_tensor("ones", [P, P], F32)
    g.ones16 = nc.alloc_sbuf_tensor("ones16", [P, P], F16)
    g.upper = nc.alloc_sbuf_tensor("upper", [P, P], F16)
    g.ident = nc.alloc_sbuf_tensor("ident", [P, P], F32)
    g.expo = nc.alloc_sbuf_tensor("expo", [P, SUB], F32)
    g.carry = nc.alloc_sbuf_tensor("carry", [P, E], F32)
    g.warm = nc.alloc_sbuf_tensor("warm", [P, 1], F32)
    g.tok_f = nc.alloc_sbuf_tensor("tok_f", [P, SUB], F32)
    g.tok_i = nc.alloc_sbuf_tensor("tok_i", [P, SUB], I32)
    g.weight = nc.alloc_sbuf_tensor("weight", [P, SUB, E], F32)
    g.slot0 = nc.alloc_sbuf_tensor("slot0", [P, SUB, E], F32)
    g.st = nc.alloc_sbuf_tensor("st", [P, SUB, 6], F32)
    g.mv = nc.alloc_sbuf_tensor("mv", [P, SUB, 2], F32)
    g.var = nc.alloc_sbuf_tensor("var", [P, SUB], F32)
    g.rstd = nc.alloc_sbuf_tensor("rstd", [P, SUB], F32)
    g.rs = nc.alloc_sbuf_tensor("rs", [P, SUB], F32)
    g.r_l = nc.alloc_sbuf_tensor("r_l", [P, SUB, E], F32)
    g.r_e = nc.alloc_sbuf_tensor("r_e", [P, SUB, E], F32)
    g.r_k = nc.alloc_sbuf_tensor("r_k", [P, SUB, E], F32)
    g.r_oh = nc.alloc_sbuf_tensor("r_oh", [P, SUB, E], F16)
    g.r_m = nc.alloc_sbuf_tensor("r_m", [P, SUB], F32)
    g.r_d = nc.alloc_sbuf_tensor("r_d", [P, SUB], F32)
    g.r_x = nc.alloc_sbuf_tensor("r_x", [P, SUB], F32)
    g.idx_f = nc.alloc_sbuf_tensor("idx_f", [P, SUB], F32)
    g.idx_i = nc.alloc_sbuf_tensor("idx_i", [P, SUB], I32)
    g.c_m = nc.alloc_sbuf_tensor("c_m", [P, 1], F32)
    g.c_m1 = nc.alloc_sbuf_tensor("c_m1", [P, 1], F32)
    g.mq = nc.alloc_sbuf_tensor("mq", [P, SUB], F32)
    words = 49000
    g.arena = nc.alloc_sbuf_tensor("arena", [P, words], F32)
    g.ps = nc.alloc_psum_tensor("ps", [P, 8, 512], F32)

    kept = Arena(g.arena, 0)
    g.q_hi = kept.take([P, DC, N + 7], F16)
    g.q_lo = kept.take([P, DC, N + 7], F16)
    g.k_hi = kept.take([P, DC, N + 7], F16)
    g.k_lo = kept.take([P, DC, N + 7], F16)
    g.v_hi = kept.take([P, KT, VW + 3], F16)
    g.v_lo = kept.take([P, KT, D], F16)
    g.v_hi = g.v_hi[:, :, 0:VW]
    g.row = kept.take([P, SUB, ROW], F32)
    g.hb = kept.take([P, SUB, D], F32)
    strips = Arena(g.arena, kept.at)
    g.xp = strips.take([P, DC, PW, PW], F32)
    g.x_in = strips.take([P, DC, QB], F32)
    g.y_t = strips.take([P, DC, QB], F32)
    g.h = strips.take([P, SUB, D], F32)
    g.a = strips.take([P, SUB, D], F32)
    g.a_hi = strips.take([P, DC, QB], F16)
    g.a_lo = strips.take([P, DC, QB], F16)
    g.p_f = strips.take([P, 2, QB], F32)
    g.c_s = strips.take([P, KT], F32)
    g.c_hi = strips.take([P, KT + 1], F16)
    g.c_lo = strips.take([P, KT + 1], F16)
    blocks = Arena(g.arena, kept.at)
    g.panel = blocks.take([P, KT, QB], F32)
    g.ph = blocks.take([P, 3, QB], F16)
    g.pl = blocks.take([P, 3, QB], F16)
    g.r = blocks.take([P, QB], F32)
    g.m = blocks.take([P, QB], F32)
    g.z_t = blocks.take([P, DC, QB], F32)
    g.diag = g.z_t[:, 0]
    mixture = Arena(g.arena, 0)
    g.w1_raw = mixture.take([P, DC, F], F32)
    g.w2_raw = mixture.take([P, FC, D], F32)
    g.w1_hi = mixture.take([P, PAIR, DC, F], F16)
    g.w1_lo = mixture.take([P, PAIR, DC, F], F16)
    g.w2_hi = mixture.take([P, PAIR, FC, D], F16)
    g.w2_lo = mixture.take([P, PAIR, FC, D], F16)
    g.b1 = mixture.take([P, PAIR, FC], F32)
    g.b2 = mixture.take([P, PAIR, D], F32)
    g.tok = mixture.take([P, 2, SUB, ROW], F32)
    g.x_hi = mixture.take([P, 2, DC, QB], F16)
    g.x_lo = mixture.take([P, 2, DC, QB], F16)
    g.hf = mixture.take([P, 2, QB], F32)
    g.hh = mixture.take([P, 2, QB], F16)
    g.hl = mixture.take([P, 2, QB], F16)
    g.y = mixture.take([P, SUB, D], F32)
    g.guarded = mixture.take([P, SUB, D], F32)
    g.mask = mixture.take([P, SUB, D], I32)
    g.ids = mixture.take([P, PAIR * NG, SUB], I32)
    g.huge = mixture.take([P, 2], F32)
    g.f_mx = mixture.take([P, PAIR, 3], F32)
    g.f_sc = mixture.take([P, PAIR, 3], F32)
    g.f_isc = mixture.take([P, PAIR, 3], F32)
    g.f_in = mixture.take([P, PAIR, 1], F32)
    g.f_out = mixture.take([P, PAIR, 1], F32)
    first = Arena(g.arena, 0)
    g.w_raw = first.take([P, 3, DC, D], F32)
    g.zrow = first.take([P, ROW], F32)
    g.iota_i = first.take([P, SUB], I32)
    g.weight_i = first.take([P, SUB, E], I32)
    g.base_i = first.take([P, SUB, E], I32)
    g.none_f = first.take([P, E * STRIDE // P], F32)
    g.none_i = first.take([P, E * STRIDE // P], I32)
    assert max(strips.at, blocks.at, mixture.at) <= words
    assert strips.at <= kept.at + KT * QB

    g.table = nc.dram_tensor("slot_tokens", [E * STRIDE, 1], I32, kind="Internal").ap()
    g.rows = nc.dram_tensor("token_rows", [T + 1, ROW], F32, kind="Internal").ap()
    g.h_res = nc.dram_tensor("residual_rows", [B, NP, D], F32, kind="Internal").ap()

    setup(nc, g, a)
    s = Names()
    (s.cleared, s.x_in, s.xn, s.y_t, s.lin, s.h_made, s.h_out, s.var, s.rstd, s.a, s.aT, s.a_hi, s.a_lo,
     s.proj, s.p_f, s.p_hi, s.p_lo, s.hb, s.o, s.var2, s.rstd2, s.z, s.zT, s.z_t, s.logits, s.l_sub, s.l_exp,
     s.routed, s.prefix, s.slots, s.o_out, s.r_out, s.h_in, s.sub, s.m, s.m_ps, s.p_hi2, s.p_lo2, s.pv, s.qk,
     s.kept, s.maxed, s.r_t, s.diag, s.step, s.settled) = \
        s.handles = semaphores(nc, "cleared x_in xn y_t lin h_made h_out var rstd a aT a_hi a_lo proj p_f p_hi p_lo hb o var2 rstd2 z "
                 "zT z_t logits l_sub l_exp routed prefix slots o_out r_out h_in sub m m_ps p_hi2 p_lo2 pv qk "
                 "kept maxed r_t diag step settled")
    g.settled = s.settled
    once = Names()
    (once.tab, once.got0, once.got1, once.put) = once.handles = semaphores(nc, "tab got0 got1 put")
    with nc.Fori(0, B) as b:
        clear(nc, s)
        s.tab, s.tab0 = once.tab, b * (16 * (SUB * NQB + 1))
        tokenizer(nc, g, a, b, s)
        class_token(nc, g, a, b, s)
        attention(nc, g, a, b, s)
    first_expert(nc, g, a)
    f = Names()
    (f.f_w, f.w_max, f.w_red, f.w_sc, f.w_high, f.w_low, f.turned, f.x_high, f.x_low, f.l1, f.relu, f.h_high,
     f.h_low, f.l2, f.y_made, f.y_done) = \
        f.handles = semaphores(nc, "f_w w_max w_red w_sc w_high w_low turned x_high x_low l1 relu h_high h_low l2 y_made y_done")
    f.ids = [nc.alloc_semaphore(f"ids{i}") for i in range(PAIR * NG)]
    f.handles += f.ids
    with nc.Fori(0, E // PAIR) as ep:
        clear(nc, f)
        f.got, f.put = [once.got0, once.got1], once.put
        experts(nc, g, a, ep, f)


_INS = ["xT", "cls_tok", "L0_tok_bn_gamma", "L0_tok_bn_beta", "L0_tok_bn_mean", "L0_tok_bn_var", "conv_taps",
        "L0_tok_conv_b", "lin_wT", "L0_tok_lin_b", "L0_attn_Wq", "L0_attn_bq", "L0_attn_Wk", "L0_attn_bk",
        "L0_attn_Wv", "L0_attn_bv", "L0_ffn_gate_w", "L0_ffn_gate_b", "L0_ffn_w1", "L0_ffn_b1", "L0_ffn_w2",
        "L0_ffn_b2"]


def kernel(**inputs):
    import numpy as _np
    import concourse.bacc as _bacc
    from concourse.bass_utils import run_bass_kernel_spmd as _run

    laid = {k: _np.asarray(v) for k, v in inputs.items()}
    laid["xT"] = laid["x"].reshape(B, NP, D).transpose(0, 2, 1)
    laid["conv_taps"] = laid["L0_tok_conv_w"].reshape(D, 9)
    laid["lin_wT"] = laid["L0_tok_lin_w"].T
    nc = _bacc.Bacc("TRN2", target_bir_lowering=False, num_devices=1)
    arrays, a = {}, {}
    for name in _INS:
        arrays[f"in_{name}"] = _np.ascontiguousarray(laid[name])
        a[name] = nc.dram_tensor(f"in_{name}", arrays[f"in_{name}"].shape, F32, kind="ExternalInput").ap()
    a["out"] = nc.dram_tensor("out_tokens", (B, N, D), F32, kind="ExternalOutput").ap()
    tower(nc, a)
    r = _run(nc, [arrays], core_ids=[0])
    return r.results[0]["out_tokens"]
```

```python
import concourse.bass as bass
from concourse import mybir

F32, F16, I32 = mybir.dt.float32, mybir.dt.float16, mybir.dt.int32
ALU, ACT, AX = mybir.AluOpType, mybir.ActivationFunctionType, mybir.AxisListType

B, IMG, D, E, F = 2, 64, 256, 8, 1024
P = 128
NP = IMG * IMG
N = NP + 1
T = B * N
DC, FC = D // P, F // P
CAP = -(-5 * T // (4 * E))
GT = -(-CAP // P)
STRIDE = GT * P
QB = 512
NQB = NP // QB
SUB = QB // P
KT = NP // P + 1
LAST = KT - 1
ROWS8 = QB // IMG
PW = IMG + 2
VW = D + 1
ROW = 2 * D + 1
A_SCALE, P_SCALE, TOP = 2.0 ** 10, 2.0 ** 14, 2.0 ** 13
NONE = T
BIG = float(2 ** 20)
EPS = 1e-5


class Names:
    pass


def semaphores(nc, names):
    return [nc.alloc_semaphore(n) for n in names.split()]


def clear(nc, s):
    with nc.Block() as block:
        @block.gpsimd
        def _(pool):
            for handle in s.handles:
                pool.sem_clear(handle)


def setup(nc, g, a):
    s = Names()
    (s.w_in, s.c_made, s.w0_max, s.w0_red, s.sc_made, s.w0_hi) = \
        s.handles = semaphores(nc, "w_in c_made w0_max w0_red sc_made w0_hi")
    W = (a["L0_attn_Wq"], a["L0_attn_Wk"], a["L0_attn_Wv"])
    with nc.Block() as block:
        @block.sync
        def _(sp):
            for i in range(3):
                sp.dma_start(g.w_raw[:, i], W[i].rearrange("(c p) e -> p c e", p=P)).then_inc(s.w_in, 16)
            sp.dma_start(g.lin_t[:], a["lin_wT"].rearrange("(c p) d -> p c d", p=P)).then_inc(s.w_in, 16)
            sp.dma_start(g.gate_w[:], a["L0_ffn_gate_w"].rearrange("(c p) e -> p c e", p=P)).then_inc(s.w_in, 16)
            sp.dma_start(g.taps[:], a["conv_taps"].rearrange("(c p) k -> p c k", p=P)).then_inc(s.w_in, 16)
            with nc.allow_non_contiguous_dma(reason="vectors of 256 onto the partitions"):
                for i, n in enumerate(("L0_tok_bn_gamma", "L0_tok_bn_beta", "L0_tok_bn_mean", "L0_tok_bn_var",
                                       "L0_tok_conv_b", "L0_attn_bq", "L0_attn_bk", "L0_attn_bv")):
                    sp.dma_start(g.vecs[:, i], a[n].rearrange("(c p) -> p c", p=P)).then_inc(s.w_in, 16)
            for dst, n in ((g.lin_b, "L0_tok_lin_b"), (g.bv, "L0_attn_bv"), (g.gate_b, "L0_ffn_gate_b")):
                sp.dma_start(dst[:], a[n].rearrange("(a n) -> a n", a=1).to_broadcast((P, a[n].shape[0])))\
                    .then_inc(s.w_in, 16)
            sp.wait_ge(s.c_made, 1)
            sp.dma_start(g.table.rearrange("(p n) a -> p (n a)", p=P), g.none_i[:]).then_inc(s.w_in, 16)
            sp.dma_start(g.rows[T:T + 1, :], g.zrow[0:1, :]).then_inc(s.w_in, 16)
            sp.wait_ge(s.w_in, 16 * 19)

        @block.gpsimd
        def _(pool):
            pool.memset(g.ones[:], 1.0)
            pool.memset(g.none_f[:], float(NONE))
            pool.memset(g.zrow[:], 0.0)
            pool.memset(g.ident[:], 0.0)
            pool.memset(g.expo[:], -0.5)
            pool.memset(g.carry[:], 0.0)
            pool.memset(g.ones16[:], 1.0)
            pool.iota(g.iota_i[:], [[P, SUB]], base=0, channel_multiplier=1)
            pool.iota(g.weight_i[:], [[0, SUB], [-1, E]], base=E, channel_multiplier=0)
            pool.iota(g.base_i[:], [[0, SUB], [STRIDE, E]], base=-1, channel_multiplier=0)
            pool.drain()
            pool.affine_select(out=g.ident[:], in_=g.ident[:], compare_op=ALU.not_equal, fill=1.0, base=0,
                               pattern=[[-1, P]], channel_multiplier=1)
            pool.affine_select(out=g.upper[:], in_=g.ones16[:], compare_op=ALU.is_ge, fill=0.0, base=0,
                               pattern=[[1, P]], channel_multiplier=-1)
            pool.tensor_copy(g.none_i[:], g.none_f[:])
            pool.tensor_copy(g.tok_f[:], g.iota_i[:])
            pool.tensor_copy(g.weight[:], g.weight_i[:])
            pool.tensor_copy(g.slot0[:], g.base_i[:])
            pool.drain().then_inc(s.c_made, 1)
            pool.wait_ge(s.w0_max, 1)
            pool.partition_all_reduce(g.mx[:, 0:6], g.mx[:, 0:6], P, bass.bass_isa.ReduceOp.max).then_inc(s.w0_red, 1)
            pool.wait_ge(s.sc_made, 1)
            pool.tensor_tensor(g.bn_r[:], g.bn_v[:], g.expo[:, 0:DC], ALU.pow)
            pool.drain().then_inc(s.w0_red, 1)

        @block.vector
        def _(dve):
            dve.wait_ge(s.w_in, 16 * 19)
            for i in range(3):
                nc.vector.tensor_reduce(g.mx[:, i:i + 1], g.w_raw[:, i], axis=AX.XY, op=ALU.max,
                                        apply_absolute_value=True)
                nc.vector.tensor_reduce(g.mx[:, 3 + i:4 + i], g.vecs[:, 5 + i], axis=AX.X, op=ALU.max,
                                        apply_absolute_value=True)
            nc.vector.tensor_scalar(g.bn_v[:], g.vecs[:, 3], EPS, None, ALU.add)
            dve.drain().then_inc(s.w0_max, 1)
            dve.wait_ge(s.w0_red, 1)
            nc.vector.scalar_tensor_tensor(out=g.mx[:, 3:6], in0=g.mx[:, 0:3], scalar=float(D), in1=g.mx[:, 3:6],
                                           op0=ALU.mult, op1=ALU.add)
            dve.drain()
            scale_of(nc, dve, g.sc[:, 0:6], g.isc[:, 0:6], g.mx[:, 0:6])
            nc.vector.tensor_tensor(g.ratio[:], g.sc[:, 3:6], g.isc[:, 0:3], ALU.mult)
            nc.vector.tensor_tensor(g.score[:], g.isc[:, 3:4], g.isc[:, 4:5], ALU.mult)
            dve.drain()
            nc.vector.tensor_scalar(g.ratio[:], g.ratio[:], 1.0 / A_SCALE, None, ALU.mult)
            nc.vector.tensor_scalar(g.score[:], g.score[:], float(D) ** -0.5, None, ALU.mult)
            for i in range(2):
                nc.vector.tensor_scalar(g.bqk[:, i], g.vecs[:, 5 + i], g.sc[:, 3 + i:4 + i], None, ALU.mult)
            dve.drain().then_inc(s.sc_made, 1)
            dve.wait_ge(s.w0_red, 2)
            nc.vector.tensor_tensor(g.bn_s[:], g.vecs[:, 0], g.bn_r[:], ALU.mult)
            dve.drain()
            nc.vector.tensor_tensor(g.bn_h[:], g.vecs[:, 2], g.bn_s[:], ALU.mult)
            dve.drain()
            nc.vector.tensor_tensor(g.bn_h[:], g.vecs[:, 1], g.bn_h[:], ALU.subtract)
            dve.wait_ge(s.w0_hi, 1)
            for i in range(3):
                nc.vector.scalar_tensor_tensor(out=g.w_lo[:, i], in0=g.w_raw[:, i], scalar=g.sc[:, i:i + 1],
                                               in1=g.w_hi[:, i], op0=ALU.mult, op1=ALU.subtract)

        @block.scalar
        def _(act):
            act.wait_ge(s.sc_made, 1)
            for i in range(3):
                last = nc.scalar.activation(g.w_hi[:, i], g.w_raw[:, i], ACT.Copy, scale=g.sc[:, i:i + 1])
            last.then_inc(s.w0_hi, 1)


def scale_of(nc, dve, scale, inverse, bound):
    nc.vector.tensor_scalar(inverse, bound, 2.0 ** -30, 2.0 ** 60, ALU.max, ALU.min)
    dve.drain()
    nc.vector.tensor_scalar(inverse.bitcast(I32), inverse.bitcast(I32), 0x7F800000, None, ALU.bitwise_and)
    dve.drain()
    nc.vector.reciprocal(scale, inverse)
    dve.drain()
    nc.vector.tensor_scalar(scale, scale, TOP, None, ALU.mult)
    nc.vector.tensor_scalar(inverse, inverse, 1.0 / TOP, None, ALU.mult)
    dve.drain()


def wait(engine, semaphore, value):
    if not isinstance(value, int) or value > 0:
        engine.wait_ge(semaphore, value)


def settle(g, engine):
    engine.sem_inc(g.settled, 1)


def tokenizer(nc, g, a, b, s):
    ps, xp = g.ps, g.xp

    def projected(m, i, parts):
        w, c = m // 2, m % 2
        if w < 2:
            return parts[w][:, c, bass.ds(i * QB, QB)], g.p_f[:, m % 2]
        return parts[2][:, bass.ds(i * SUB + 2 * c, 2), 0:D], g.p_f[:, m % 2].rearrange("p (t d) -> p t d", d=D)

    def rounds(engine, one):
        one(0, 0, True, False, False)
        one(1, 1, True, True, False)
        one(2, 0, True, True, True)
        one(3, 1, True, True, True)
        with engine.Fori(2, NQB // 2) as r:
            one(r * 2, 0, True, True, True)
            one(r * 2 + 1, 1, True, True, True)
        one(NQB, 0, False, True, True)
        one(NQB + 1, 1, False, False, True)

    with nc.Block() as block:
        @block.sync
        def _(sp):
            def load(i, k):
                wait(sp, s.xn, i - 1)
                sp.dma_start(g.x_in[:, k], a["xT"][b, :, bass.ds(i * QB, QB)].rearrange("(c p) n -> p c n", p=P))\
                    .then_inc(s.x_in[k], 16)

            def store(i):
                wait(sp, s.h_made, i + 1)
                sp.dma_start(g.h_res[b, bass.ds(i * QB, QB), :].rearrange("(t p) d -> p t d", p=P), g.h[:])\
                    .then_inc(s.h_out, 16)

            load(0, 0)
            load(1, 1)
            with sp.Fori(1, NQB // 2) as r:
                load(r * 2, 0)
                load(r * 2 + 1, 1)
            with sp.Fori(0, NQB) as i:
                store(i)
            sp.wait_ge(s.h_out, 16 * NQB)

        @block.scalar
        def _(act):
            nc.scalar.activation(g.warm[:], g.ones[:, 0:1], ACT.Exp)
            act.wait_ge(s.cleared, 1)
            with act.Fori(0, NQB // 2) as r:
                for k in range(2):
                    act.wait_ge(s.x_in[k], r * 16 + 16)
                    for c in range(DC):
                        nc.scalar.activation(xp[:, c, bass.ds(r * (2 * ROWS8) + (k * ROWS8 + 1), ROWS8), 1:1 + IMG],
                                             g.x_in[:, k, c].rearrange("p (r w) -> p r w", w=IMG), ACT.Identity,
                                             scale=g.bn_s[:, c:c + 1], bias=g.bn_h[:, c:c + 1])
                    act.drain().then_inc(s.xn, 1)
            act.sem_inc(s.xn, 1)

            def high(i, k):
                act.wait_ge(s.aT, i + 1)
                wait(act, s.proj, i * 6 - 6)
                nc.scalar.activation(g.a_hi[:, k], ps[:, 2:4], ACT.Copy, scale=A_SCALE).then_inc(s.a_hi, 1)

            def project(i, k):
                for m in range(6):
                    act.wait_ge(s.proj, i * 6 + m + 1)
                    wait(act, s.p_lo, i * 6 + m - 1)
                    bias = g.bqk[:, m // 2, m % 2:m % 2 + 1] if m < 4 else 0.0
                    nc.scalar.activation(g.p_f[:, m % 2], ps[:, 4 + (2 * k + m) % 4], ACT.Identity,
                                         scale=g.ratio[:, m // 2:m // 2 + 1], bias=bias)
                    act.drain().then_inc(s.p_f, 1)
                    out, src = projected(m, i, (g.q_hi, g.k_hi, g.v_hi))
                    nc.scalar.activation(out, src, ACT.Copy).then_inc(s.p_hi, 1)

            def one(i, k, taps, norm, last):
                if norm:
                    high(i - 1, 1 - k)
                if last:
                    project(i - 2, k)

            rounds(act, one)

        @block.gpsimd
        def _(pool):
            def root(i):
                pool.wait_ge(s.var, i + 1)
                pool.tensor_tensor(g.rstd[:], g.var[:], g.expo[:, 0:SUB], ALU.pow).then_inc(s.rstd, 1)

            def low(i):
                for m in range(6):
                    pool.wait_ge(s.p_hi, i * 6 + m + 1)
                    out, src = projected(m, i, (g.q_lo, g.k_lo, g.v_lo))
                    hi, _ = projected(m, i, (g.q_hi, g.k_hi, g.v_hi))
                    pool.tensor_tensor(out, src, hi, ALU.subtract).then_inc(s.p_lo, 1)

            def one(i, k, taps, norm, last):
                if norm:
                    root(i - 1)
                if last:
                    low(i - 2)

            rounds(pool, one)

        @block.tensor
        def _(pe):
            def linear(i, k):
                pe.wait_ge(s.y_t, i + 1)
                wait(pe, s.h_made, i)
                for t in range(SUB):
                    for c in range(DC):
                        last = nc.tensor.matmul(ps[:, t // 2, (t % 2) * D:(t % 2 + 1) * D],
                                                g.y_t[:, k, c, t * P:(t + 1) * P], g.lin_t[:, c],
                                                start=c == 0, stop=c == DC - 1)
                last.then_inc(s.lin, 1)

            def turn(i):
                pe.wait_ge(s.a, i + 1)
                wait(pe, s.a_lo, i)
                for c in range(DC):
                    for t in range(SUB):
                        last = nc.tensor.transpose(ps[:, 2 + c, t * P:(t + 1) * P], g.a[:, t, c * P:(c + 1) * P],
                                                   g.ident[:])
                last.then_inc(s.aT, 1)

            def project(i, k):
                pe.wait_ge(s.a_lo, i + 1)
                for m in range(6):
                    wait(pe, s.p_f, i * 6 + m - 3)
                    w, c, out = m // 2, m % 2, ps[:, 4 + (2 * k + m) % 4]
                    for t in range(1 if w < 2 else 2):
                        n = 0
                        for q in range(DC):
                            for x, y in ((g.w_hi, g.a_hi), (g.w_hi, g.a_lo), (g.w_lo, g.a_hi)):
                                if w < 2:
                                    last = nc.tensor.matmul(out, x[:, w, q, c * P:(c + 1) * P], y[:, k, q],
                                                            start=n == 0, stop=n == 5)
                                else:
                                    last = nc.tensor.matmul(out[:, t * D:(t + 1) * D],
                                                            y[:, k, q, (2 * c + t) * P:(2 * c + t + 1) * P], x[:, w, q],
                                                            start=n == 0, stop=n == 5)
                                n += 1
                    last.then_inc(s.proj, 1)

            def one(i, k, taps, norm, last):
                if taps:
                    linear(i, k)
                if norm:
                    turn(i - 1)
                if last:
                    project(i - 2, k)

            rounds(pe, one)

        @block.vector
        def _(dve):
            for edge in (0, PW - 1):
                nc.vector.memset(xp[:, :, edge, :], 0.0)
                nc.vector.memset(xp[:, :, 1:1 + IMG, edge], 0.0)
            dve.drain().then_inc(s.cleared, 1)
            nc.vector.memset(g.v_hi[:, :, D:VW], 1.0)

            def conv(i, k):
                dve.wait_ge(s.xn, i + 2)
                wait(dve, s.lin, i - 1)
                for tap in range(9):
                    for c in range(DC):
                        view = xp[:, c, bass.ds(i * ROWS8 + tap // 3, ROWS8), tap % 3:tap % 3 + IMG]
                        out = g.y_t[:, k, c].rearrange("p (r w) -> p r w", w=IMG)
                        if tap == 0:
                            nc.vector.tensor_scalar(out, view, g.taps[:, c, 0:1], g.vecs[:, 4, c:c + 1],
                                                    ALU.mult, ALU.add)
                        else:
                            nc.vector.scalar_tensor_tensor(out=out, in0=view, scalar=g.taps[:, c, tap:tap + 1],
                                                           in1=out, op0=ALU.mult, op1=ALU.add)
                    if tap < 8:
                        dve.drain()
                dve.drain().then_inc(s.y_t, 1)

            def rows(i):
                dve.wait_ge(s.lin, i + 1)
                wait(dve, s.h_out, i * 16)
                for t in range(SUB):
                    nc.vector.tensor_tensor(g.h[:, t], ps[:, t // 2, (t % 2) * D:(t % 2 + 1) * D], g.lin_b[:], ALU.add)
                dve.drain().then_inc(s.h_made, 1)
                stats(nc, dve, g, g.h, SUB)
                dve.drain().then_inc(s.var, 1)

            def norm(i):
                dve.wait_ge(s.rstd, i + 1)
                wait(dve, s.aT, i)
                for t in range(SUB):
                    nc.vector.tensor_scalar(g.a[:, t], g.h[:, t], g.mv[:, t, 0:1], g.rstd[:, t:t + 1],
                                            ALU.subtract, ALU.mult)
                dve.drain().then_inc(s.a, 1)

            def low(i, k):
                dve.wait_ge(s.a_hi, i + 1)
                nc.vector.scalar_tensor_tensor(out=g.a_lo[:, k], in0=ps[:, 2:4], scalar=A_SCALE, in1=g.a_hi[:, k],
                                               op0=ALU.mult, op1=ALU.subtract)
                dve.drain().then_inc(s.a_lo, 1)

            def one(i, k, taps, norm_, last):
                if taps:
                    conv(i, k)
                if norm_:
                    rows(i - 1)
                if last:
                    low(i - 2, k)
                if norm_:
                    norm(i - 1)

            rounds(dve, one)


def stats(nc, dve, g, x, nt, np_=P):
    for t in range(nt):
        nc.vector.bn_stats(g.st[0:np_, t], x[0:np_, t])
    dve.drain()
    for t in range(nt):
        nc.vector.bn_aggr(g.mv[0:np_, t], g.st[0:np_, t])
    dve.drain()
    nc.vector.tensor_scalar(g.var[0:np_, 0:nt], g.mv[0:np_, 0:nt, 1], EPS, None, ALU.add)


def class_row(nc, g, a):
    ps = g.ps
    s = Names()
    s.c_in, s.c_step = semaphores(nc, "c_in c_step")
    with nc.Block() as block:
        @block.sync
        def _(sp):
            sp.dma_start(g.h[0:1, 0], a["cls_tok"][0]).then_inc(s.c_in, 16)

        @block.gpsimd
        def _(pool):
            pool.wait_ge(s.c_step, 1)
            pool.tensor_tensor(g.rstd[0:1, 0:1], g.var[0:1, 0:1], g.expo[0:1, 0:1], ALU.pow)
            pool.tensor_tensor(g.c_hb[0:1, 0], g.h[0:1, 0], g.bv[0:1], ALU.add)
            pool.drain().then_inc(s.c_step, 1)

        @block.vector
        def _(dve):
            dve.wait_ge(s.c_in, 16)
            stats(nc, dve, g, g.h, 1, 1)
            dve.drain().then_inc(s.c_step, 1)
            dve.wait_ge(s.c_step, 2)
            nc.vector.tensor_scalar(g.a[0:1, 0], g.h[0:1, 0], g.mv[0:1, 0, 0:1], g.rstd[0:1, 0:1],
                                    ALU.subtract, ALU.mult)
            dve.drain().then_inc(s.c_step, 1)
            dve.wait_ge(s.c_step, 5)
            nc.vector.scalar_tensor_tensor(out=g.a_lo[:, 0, :, 0:1], in0=ps[:, 2:4, 0:1], scalar=A_SCALE,
                                           in1=g.a_hi[:, 0, :, 0:1], op0=ALU.mult, op1=ALU.subtract)
            dve.drain().then_inc(s.c_step, 1)
            dve.wait_ge(s.c_step, 8)
            nc.vector.tensor_tensor(g.c_q[:, :, 1], g.p_f[:, 0, 0:2], g.c_q[:, :, 0], ALU.subtract)
            nc.vector.tensor_tensor(g.k_lo[:, :, NP], g.p_f[:, 0, 2:4], g.k_hi[:, :, NP], ALU.subtract)
            nc.vector.tensor_tensor(g.v_lo[0:1, LAST], g.p_f[0:1, 1, 0:D], g.v_hi[0:1, LAST, 0:D], ALU.subtract)

        @block.scalar
        def _(act):
            act.wait_ge(s.c_step, 4)
            nc.scalar.activation(g.a_hi[:, 0, :, 0:1], ps[:, 2:4, 0:1], ACT.Copy, scale=A_SCALE)
            act.drain().then_inc(s.c_step, 1)
            act.wait_ge(s.c_step, 7)
            for m in range(4):
                nc.scalar.activation(g.p_f[:, 0, m:m + 1], ps[:, 4, m:m + 1], ACT.Identity,
                                     scale=g.ratio[:, m // 2:m // 2 + 1], bias=g.bqk[:, m // 2, m % 2:m % 2 + 1])
            nc.scalar.activation(g.p_f[0:1, 1, 0:D], ps[0:1, 5, 0:D], ACT.Copy, scale=g.ratio[0:1, 2:3])
            act.drain()
            nc.scalar.activation(g.c_q[:, :, 0], g.p_f[:, 0, 0:2], ACT.Copy)
            nc.scalar.activation(g.k_hi[:, :, NP], g.p_f[:, 0, 2:4], ACT.Copy)
            nc.scalar.activation(g.v_hi[0:1, LAST, 0:D], g.p_f[0:1, 1, 0:D], ACT.Copy)
            act.drain().then_inc(s.c_step, 1)

        @block.tensor
        def _(pe):
            pe.wait_ge(s.c_step, 3)
            for c in range(DC):
                nc.tensor.transpose(ps[:, 2 + c, 0:1], g.a[0:1, 0, c * P:(c + 1) * P], g.ident[0:1, 0:1])
            pe.drain().then_inc(s.c_step, 1)
            pe.wait_ge(s.c_step, 6)
            for m in range(4):
                products(nc, ps[:, 4, m:m + 1], [(g.w_hi[:, m // 2, k, m % 2 * P:(m % 2 + 1) * P],
                                                  g.w_lo[:, m // 2, k, m % 2 * P:(m % 2 + 1) * P],
                                                  g.a_hi[:, 0, k, 0:1], g.a_lo[:, 0, k, 0:1]) for k in range(DC)])
            products(nc, ps[0:1, 5, 0:D], [(g.a_hi[:, 0, k, 0:1], g.a_lo[:, 0, k, 0:1],
                                            g.w_hi[:, 2, k], g.w_lo[:, 2, k]) for k in range(DC)])
            pe.drain().then_inc(s.c_step, 1)



def cls_scores(nc, g, s, pe):
    def score(t, np_, keys):
        out, n = g.ps[0:np_, 7, t * 2:t * 2 + 2], 0
        for c in range(DC):
            for part in (g.k_hi, g.k_lo):
                last = nc.tensor.matmul(out, part[:, c, keys], g.c_q[:, c], start=n == 0, stop=n == 2 * DC - 1)
                n += 1
        return last

    for t in range(LAST):
        score(t, P, slice(t * P, (t + 1) * P))
    score(LAST, 1, slice(NP, N)).then_inc(s.c_qk, 1)


def cls_largest(nc, g, s, dve):
    pair = g.ps[:, 7, 0:2 * KT].rearrange("p (t h) -> p t h", h=2)
    dve.wait_ge(s.c_qk, 1)
    nc.vector.reduce_sum(g.c_s[:, 0:LAST], pair[:, 0:LAST], axis=AX.X)
    nc.vector.reduce_sum(g.c_s[0:1, LAST:KT], pair[0:1, LAST:KT], axis=AX.X)
    dve.drain()
    nc.vector.reduce_max(g.c_m[:], g.c_s[:, 0:LAST], axis=AX.X)
    dve.drain()
    nc.vector.tensor_tensor(g.c_m[0:1], g.c_m[0:1], g.c_s[0:1, LAST:KT], ALU.max)
    dve.drain().then_inc(s.c_maxed, 1)


def cls_turn(nc, g, s, pe):
    pe.wait_ge(s.c_maxed, 1)
    nc.tensor.transpose(g.ps[0:1, 7, P:2 * P], g.c_m[:], g.ident[:]).then_inc(s.c_turned, 1)


def cls_top(nc, g, s, dve):
    dve.wait_ge(s.c_turned, 1)
    nc.vector.reduce_max(g.c_m1[0:1], g.ps[0:1, 7, P:2 * P], axis=AX.X).then_inc(s.c_top, 1)


def cls_spread(nc, g, s, pe):
    pe.wait_ge(s.c_top, 1)
    nc.tensor.matmul(g.ps[:, 7, 2 * P:2 * P + 1], g.ones[0:1, :], g.c_m1[0:1], start=True, stop=True)\
        .then_inc(s.c_spread, 1)


def cls_subtract(nc, g, s, dve):
    dve.wait_ge(s.c_spread, 1)
    nc.vector.tensor_copy(g.c_m[:], g.ps[:, 7, 2 * P:2 * P + 1])
    dve.drain()
    nc.vector.tensor_scalar(g.c_s[:, 0:LAST], g.c_s[:, 0:LAST], g.c_m[:], None, ALU.subtract)
    nc.vector.tensor_scalar(g.c_s[0:1, LAST:KT], g.c_s[0:1, LAST:KT], g.c_m[0:1], None, ALU.subtract)
    dve.drain().then_inc(s.c_sub, 1)


def cls_weights(nc, g, s, act):
    act.wait_ge(s.c_sub, 1)
    nc.scalar.activation(g.c_s[:, 0:LAST], g.c_s[:, 0:LAST], ACT.Exp, scale=g.score[:])
    nc.scalar.activation(g.c_s[0:1, LAST:KT], g.c_s[0:1, LAST:KT], ACT.Exp, scale=g.score[0:1])
    act.drain()
    nc.scalar.activation(g.c_hi[:, 0:LAST], g.c_s[:, 0:LAST], ACT.Copy, scale=P_SCALE)
    nc.scalar.activation(g.c_hi[0:1, LAST:KT], g.c_s[0:1, LAST:KT], ACT.Copy, scale=P_SCALE)
    act.drain().then_inc(s.c_high, 1)


def cls_low(nc, g, s, dve):
    dve.wait_ge(s.c_high, 1)
    nc.vector.scalar_tensor_tensor(out=g.c_lo[:, 0:LAST], in0=g.c_s[:, 0:LAST], scalar=P_SCALE,
                                   in1=g.c_hi[:, 0:LAST], op0=ALU.mult, op1=ALU.subtract)
    nc.vector.scalar_tensor_tensor(out=g.c_lo[0:1, LAST:KT], in0=g.c_s[0:1, LAST:KT], scalar=P_SCALE,
                                   in1=g.c_hi[0:1, LAST:KT], op0=ALU.mult, op1=ALU.subtract)
    dve.drain().then_inc(s.c_low, 1)


def cls_values(nc, g, s, pe):
    def value(t, np_, first, last):
        at = slice(t, t + 1)
        v, vl = g.v_hi[0:np_, t, :], g.v_lo[0:np_, t, :]
        nc.tensor.matmul(g.ps[0:1, 0, 0:VW], g.c_hi[0:np_, at], v, start=first, stop=False)
        nc.tensor.matmul(g.ps[0:1, 0, 0:D], g.c_hi[0:np_, at], vl, start=False, stop=False)
        return nc.tensor.matmul(g.ps[0:1, 0, 0:VW], g.c_lo[0:np_, at], v, start=False, stop=last)

    pe.wait_ge(s.c_low, 1)
    value(0, P, True, False)
    for t in range(1, LAST):
        value(t, P, False, False)
    value(LAST, 1, False, True).then_inc(s.c_pv, 1)


def products(nc, out, parts, start=True, stop=True):
    for i, (x_hi, x_lo, y_hi, y_lo) in enumerate(parts):
        nc.tensor.matmul(out, x_hi, y_hi, start=start and i == 0, stop=False)
        nc.tensor.matmul(out, x_hi, y_lo, start=False, stop=False)
        last = nc.tensor.matmul(out, x_lo, y_hi, start=False, stop=stop and i == len(parts) - 1)
    return last



def ep_evacuate(nc, g, s, dve, n, np_, nt):
    wait(dve, s.o_out, n * 16)
    wait(dve, s.r_out, n * 16)
    wait(dve, s.hb, n)
    hb = g.hb if np_ == P else g.c_hb
    nc.vector.reciprocal(g.rs[0:np_, 0:nt], g.ps[0:np_, 0:nt, D])
    dve.drain()
    nc.vector.tensor_scalar(g.rs[0:np_, 0:nt], g.rs[0:np_, 0:nt], g.isc[0:np_, 5:6], None, ALU.mult)
    dve.drain()
    for t in range(nt):
        nc.vector.scalar_tensor_tensor(out=g.row[0:np_, t, D:2 * D], in0=g.ps[0:np_, t, 0:D],
                                       scalar=g.rs[0:np_, t:t + 1], in1=hb[0:np_, t], op0=ALU.mult, op1=ALU.add)
    dve.drain().then_inc(s.o, 1)


def ep_stats(nc, g, s, dve, n, np_, nt):
    stats(nc, dve, g, g.row[:, :, D:2 * D], nt, np_)
    dve.drain().then_inc(s.var2, 1)


def ep_pool_root(nc, g, s, pool, n, np_, nt):
    pool.wait_ge(s.var2, n + 1)
    pool.tensor_tensor(g.rstd[0:np_, 0:nt], g.var[0:np_, 0:nt], g.expo[0:np_, 0:nt], ALU.pow).then_inc(s.rstd2, 1)


def ep_norm(nc, g, s, dve, n, np_, nt):
    dve.wait_ge(s.rstd2, n + 1)
    for t in range(nt):
        nc.vector.tensor_scalar(g.row[0:np_, t, 0:D], g.row[0:np_, t, D:2 * D], g.mv[0:np_, t, 0:1],
                                g.rstd[0:np_, t:t + 1], ALU.subtract, ALU.mult)
    dve.drain().then_inc(s.z, 1)


def ep_turn(nc, g, s, pe, n, c, np_, nt):
    pe.wait_ge(s.z, n + 1)
    if c:
        pe.wait_ge(s.z_t, n * DC + c)
    for t in range(nt):
        last = nc.tensor.transpose(g.ps[:, 7, t * P:t * P + np_], g.row[0:np_, t, c * P:(c + 1) * P],
                                   g.ident[0:np_, 0:np_])
    last.then_inc(s.zT, 1)


def ep_columns(nc, g, s, act, n, c, np_, nt):
    act.wait_ge(s.zT, n * DC + c + 1)
    src = g.ps[:, 7, 0:nt * P] if np_ == P else g.ps[:, 7, 0:np_]
    nc.scalar.activation(g.z_t[:, c, 0:nt * P] if np_ == P else g.z_t[:, c, 0:np_], src, ACT.Copy).then_inc(s.z_t, 1)


def ep_logits(nc, g, s, pe, n, np_, nt):
    pe.wait_ge(s.z_t, n * DC + DC)
    for t in range(nt):
        for c in range(DC):
            last = nc.tensor.matmul(g.ps[0:np_, 7, t * E:(t + 1) * E], g.z_t[:, c, t * P:t * P + np_], g.gate_w[:, c],
                                    start=c == 0, stop=c == DC - 1)
    last.then_inc(s.logits, 1)


def ep_exp(nc, g, s, act, n, np_, nt):
    act.wait_ge(s.l_sub, n + 1)
    nc.scalar.activation(g.r_e[0:np_, 0:nt], g.r_l[0:np_, 0:nt], ACT.Exp).then_inc(s.l_exp, 1)


def ep_route(nc, g, s, dve, n, np_, nt):
    v = nc.vector
    l, e, key, oh = (x[0:np_, 0:nt] for x in (g.r_l, g.r_e, g.r_k, g.r_oh))
    m, d, k = (x[0:np_, 0:nt] for x in (g.r_m, g.r_d, g.r_x))
    wide = lambda x: x.unsqueeze(2).to_broadcast((np_, nt, E))
    dve.wait_ge(s.logits, n + 1)
    v.tensor_tensor(l, g.ps[0:np_, 7, 0:nt * E].rearrange("p (t e) -> p t e", e=E),
                    g.gate_b[0:np_].unsqueeze(1).to_broadcast((np_, nt, E)), ALU.add)
    dve.drain()
    v.reduce_max(m, l, axis=AX.X)
    dve.drain()
    v.tensor_tensor(l, l, wide(m), ALU.subtract)
    dve.drain().then_inc(s.l_sub, 1)
    dve.wait_ge(s.l_exp, n + 1)
    v.reduce_max(m, e, axis=AX.X)
    v.reduce_sum(d, e, axis=AX.X)
    dve.drain()
    v.reciprocal(d, d)
    v.tensor_tensor(key, e, wide(m), ALU.is_equal)
    dve.drain()
    v.tensor_tensor(g.row[0:np_, 0:nt, 2 * D], m, d, ALU.mult)
    v.tensor_tensor(key, key, g.weight[0:np_, 0:nt], ALU.mult)
    dve.drain()
    v.reduce_max(k, key, axis=AX.X)
    dve.drain()
    v.tensor_tensor(oh, key, wide(k), ALU.is_equal)
    dve.drain().then_inc(s.routed, 1)


def ep_prefix(nc, g, s, pe, n, np_, nt):
    pe.wait_ge(s.routed, n + 1)
    for t in range(nt):
        out = g.ps[0:np_, 7, 64 + t * E:64 + (t + 1) * E]
        for u in range(t):
            nc.tensor.matmul(out, g.ones16[0:np_, 0:np_], g.r_oh[0:np_, u], start=u == 0, stop=False)
        nc.tensor.matmul(out, g.upper[0:np_, 0:np_], g.r_oh[0:np_, t], start=t == 0, stop=True)
    for t in range(nt):
        last = nc.tensor.matmul(g.ps[:, 7, 128:128 + E], g.ones16[0:np_, :], g.r_oh[0:np_, t], start=t == 0,
                                stop=t == nt - 1)
    last.then_inc(s.prefix, 1)


def ep_slots(nc, g, s, dve, n, np_, nt):
    v = nc.vector
    c, d = g.r_l[0:np_, 0:nt], g.r_e[0:np_, 0:nt]
    dve.wait_ge(s.prefix, n + 1)
    if isinstance(n, int) and n == 0:
        v.memset(g.idx_f[:], BIG)
        dve.drain()
    else:
        dve.wait_ge(s.tab, s.tab0 + (n - 1) * 16 * SUB + 16)
    v.tensor_tensor(c, g.ps[0:np_, 7, 64:64 + nt * E].rearrange("p (t e) -> p t e", e=E),
                    g.carry[0:np_].unsqueeze(1).to_broadcast((np_, nt, E)), ALU.add)
    dve.drain()
    v.tensor_tensor(g.carry[:], g.ps[:, 7, 128:128 + E], g.carry[:], ALU.add)
    v.tensor_scalar(d, c, float(CAP), BIG, ALU.is_gt, ALU.mult)
    dve.drain()
    v.tensor_tensor(c, c, g.slot0[0:np_, 0:nt], ALU.add)
    dve.drain()
    v.tensor_tensor(c, c, d, ALU.add)
    dve.drain()
    v.tensor_tensor(c, c, g.r_oh[0:np_, 0:nt], ALU.mult)
    dve.drain()
    v.reduce_sum(g.idx_f[0:np_, 0:nt], c, axis=AX.X)
    v.tensor_copy(g.tok_i[:], g.tok_f[:])
    dve.drain()
    v.tensor_copy(g.idx_i[:], g.idx_f[:])
    v.tensor_scalar(g.tok_f[:], g.tok_f[:], float(QB if np_ == P else 1), None, ALU.add)
    dve.drain().then_inc(s.slots, 1)


def ep_pool_table(nc, g, s, pool, n, nt):
    pool.wait_ge(s.slots, n + 1)
    settle(g, pool)
    for t in range(nt):
        pool.indirect_dma_start(out=g.table[:, :], out_offset=bass.IndirectOffsetOnAxis(ap=g.idx_i[:, t:t + 1], axis=0),
                                in_=g.tok_i[:, t:t + 1], in_offset=None, bounds_check=E * STRIDE - 1,
                                oob_is_err=False).then_inc(s.tab, 16)


def attention(nc, g, a, b, s):
    ps = g.ps

    def keys_loop(engine, body, steps):
        cuts = sorted({0, 1, 10} | set(steps))
        for lo, hi in zip(cuts, cuts[1:] + [11]):
            if lo in steps:
                steps[lo]()
            if hi - lo == 1:
                for k in range(3):
                    body(3 * lo + k, k)
            else:
                with engine.Fori(lo, hi) as r:
                    for k in range(3):
                        body(r * 3 + k, k)

    def rounds(engine, one):
        one(0, True, False, None)
        one(1, True, True, 0)
        with engine.Fori(2, NQB) as j:
            one(j, True, True, j - 1)
        one(NQB, False, True, NQB - 1)
        one(NQB + 1, False, False, NQB)

    def size(n):
        return (1, 1) if isinstance(n, int) and n == 0 else (P, SUB)

    with nc.Block() as block:
        @block.sync
        def _(sp):
            def rows(n):
                return bass.ds((n - 1) * QB + 1, QB)

            def load(n):
                sp.wait_ge(s.o, n)
                sp.dma_start(g.hb[:], g.h_res[b, bass.ds((n - 1) * QB, QB), :].rearrange("(t p) d -> p t d", p=P))\
                    .then_inc(s.h_in, 16)

            def store(n):
                sp.wait_ge(s.o, n + 1)
                sp.dma_start(a["out"][b, rows(n), :].rearrange("(t p) d -> p t d", p=P), g.row[:, :, D:2 * D])\
                    .then_inc(s.o_out, 16)
                sp.wait_ge(s.routed, n + 1)
                sp.dma_start(g.rows[bass.ds(b * N + (n - 1) * QB + 1, QB), :].rearrange("(t p) d -> p t d", p=P),
                             g.row[:]).then_inc(s.r_out, 16)

            load(1)
            sp.dma_start(a["out"][b, 0:1, :], g.row[0:1, 0, D:2 * D]).then_inc(s.o_out, 16)
            sp.wait_ge(s.routed, 1)
            sp.dma_start(g.rows[bass.ds(b * N, 1), :], g.row[0:1, 0]).then_inc(s.r_out, 16)
            with sp.Fori(2, NQB + 1) as n:
                load(n)
                store(n - 1)
            store(NQB)
            sp.wait_ge(s.o_out, 16 * (NQB + 1))
            sp.wait_ge(s.r_out, 16 * (NQB + 1))

        @block.gpsimd
        def _(pool):
            def subtract(j, t):
                np_ = 1 if isinstance(t, int) and t == LAST else P
                x = g.panel[0:np_, t]
                pool.tensor_tensor(x, x, g.m[0:np_], ALU.subtract).then_inc(s.sub, 1)

            def one(j, scores, values, n):
                def bias(m):
                    pool.wait_ge(s.h_in, m * 16)
                    for t in range(SUB):
                        pool.tensor_tensor(g.hb[:, t], g.hb[:, t], g.bv[:], ALU.add)
                    pool.drain().then_inc(s.hb, 1)

                if not values:
                    if n is not None:
                        ep_pool_root(nc, g, s, pool, n, *size(n))
                        ep_pool_table(nc, g, s, pool, n, size(n)[1])
                    return
                pool.wait_ge(s.m, j)
                settle(g, pool)
                body = lambda t, k: subtract(j, t)
                keys_loop(pool, body, {2: lambda: ep_pool_root(nc, g, s, pool, n, *size(n)), 7: lambda: bias(n + 1)})
                ep_pool_table(nc, g, s, pool, n, size(n)[1])

            rounds(pool, one)
            pool.wait_ge(s.tab, s.tab0 + 16 * (SUB * NQB + 1))
            settle(g, pool)

        @block.scalar
        def _(act):
            nc.scalar.activation(g.warm[:], g.ones[:, 0:1], ACT.Exp)

            def weights(j, t, k):
                i = (j - 1) * KT + t
                last = isinstance(t, int) and t == LAST
                np_ = 1 if last else P
                act.wait_ge(s.sub, i + 1)
                x = g.panel[0:np_, t]
                nc.scalar.activation(x, x, ACT.Exp, scale=g.score[0:np_])
                act.drain()
                if not (isinstance(i, int) and i <= 2):
                    act.wait_ge(s.pv, i - 2)
                    settle(g, act)
                nc.scalar.activation(g.ph[0:np_, k], x, ACT.Copy, scale=P_SCALE).then_inc(s.p_hi2, 1)

            def keep(j, t, k):
                np_ = 1 if isinstance(t, int) and t == LAST else P
                act.wait_ge(s.qk, j * KT + t + 1)
                if not (isinstance(j, int) and j == 0):
                    act.wait_ge(s.p_lo2, (j - 1) * KT + t + 1)
                settle(g, act)
                nc.scalar.activation(g.panel[0:np_, t], ps[0:np_, 4 + k], ACT.Copy).then_inc(s.kept, 1)

            def one(j, scores, values, n):
                if values:
                    weights(j, 0, 0)

                def body(t, k):
                    if values and not (isinstance(t, int) and t == LAST):
                        weights(j, t + 1, (k + 1) % 3)
                    if scores:
                        keep(j, t, k)

                if n is None:
                    steps = {5: lambda: cls_weights(nc, g, s, act)}
                else:
                    steps = {4: lambda: ep_columns(nc, g, s, act, n, 0, *size(n)),
                             6: lambda: ep_columns(nc, g, s, act, n, 1, *size(n)),
                             8: lambda: ep_exp(nc, g, s, act, n, *size(n))}
                if scores or values:
                    keys_loop(act, body, steps)
                else:
                    for step in steps.values():
                        step()
                if scores:
                    act.wait_ge(s.m_ps, j + 1)
                    nc.scalar.activation(g.m[:], ps[:, 7], ACT.Copy).then_inc(s.m, 1)

            rounds(act, one)

        @block.vector
        def _(dve):
            def low(j, t, k):
                last = isinstance(t, int) and t == LAST
                np_ = 1 if last else P
                dve.wait_ge(s.p_hi2, (j - 1) * KT + t + 1)
                nc.vector.scalar_tensor_tensor(out=g.pl[0:np_, k], in0=g.panel[0:np_, t], scalar=P_SCALE,
                                               in1=g.ph[0:np_, k], op0=ALU.mult, op1=ALU.subtract).then_inc(s.p_lo2, 1)

            def largest(j, t):
                np_ = 1 if isinstance(t, int) and t == LAST else P
                dve.wait_ge(s.kept, j * KT + t + 1)
                nc.vector.tensor_tensor(g.r[0:np_], g.r[0:np_], g.panel[0:np_, t], ALU.max)
                dve.drain().then_inc(s.maxed, 1)

            def one(j, scores, values, n):
                if n is None:
                    cls_largest(nc, g, s, dve)
                elif isinstance(n, int) and n == 0:
                    dve.wait_ge(s.c_pv, 1)
                else:
                    dve.wait_ge(s.pv, n * KT)
                if n is not None:
                    ep_evacuate(nc, g, s, dve, n, *size(n))
                if values:
                    low(j, 0, 0)
                if scores:
                    wait(dve, s.r_t, j)
                    nc.vector.memset(g.r[:], -3.0e38)
                    dve.drain()

                def body(t, k):
                    if values and not (isinstance(t, int) and t == LAST):
                        low(j, t + 1, (k + 1) % 3)
                    if scores:
                        largest(j, t)

                if n is None:
                    steps = {1: lambda: cls_top(nc, g, s, dve), 4: lambda: cls_subtract(nc, g, s, dve),
                             6: lambda: cls_low(nc, g, s, dve)}
                else:
                    steps = {1: lambda: ep_stats(nc, g, s, dve, n, *size(n)),
                             2: lambda: ep_norm(nc, g, s, dve, n, *size(n)),
                             8: lambda: ep_route(nc, g, s, dve, n, *size(n)),
                             10: lambda: ep_slots(nc, g, s, dve, n, *size(n))}
                if scores or values:
                    keys_loop(dve, body, steps)
                else:
                    for step in steps.values():
                        step()
                if scores:
                    dve.wait_ge(s.r_t, j + 1)
                    nc.vector.reduce_max(g.mq[:], ps[:, 7].rearrange("p (t q) -> p t q", q=P), axis=AX.X)
                    dve.drain()
                    for t in range(SUB):
                        nc.vector.tensor_scalar(g.diag[:, t * P:(t + 1) * P], g.ident[:], g.mq[:, t:t + 1], None,
                                                ALU.mult)
                    dve.drain().then_inc(s.diag, 1)

            rounds(dve, one)

        @block.tensor
        def _(pe):
            def score(j, t, k):
                i = j * KT + t
                last = isinstance(t, int) and t == LAST
                queries = bass.ds(j * QB, QB)
                keys = slice(NP, N) if last else bass.ds(t * P, P)
                wait(pe, s.kept, i - 2)
                if last:
                    settle(g, pe)
                out = ps[0:1, 4 + k] if last else ps[:, 4 + k]
                products(nc, out, [(g.k_hi[:, c, keys], g.k_lo[:, c, keys], g.q_hi[:, c, queries],
                                    g.q_lo[:, c, queries]) for c in range(DC)]).then_inc(s.qk, 1)

            def value(j, t, k):
                i = (j - 1) * KT + t
                first, last = isinstance(t, int) and t == 0, isinstance(t, int) and t == LAST
                np_ = 1 if last else P
                pe.wait_ge(s.p_lo2, i + 1)
                if first:
                    pe.wait_ge(s.o, j)
                v, vl = g.v_hi[0:np_, t], g.v_lo[0:np_, t]
                for u in range(SUB):
                    q = slice(u * P, (u + 1) * P)
                    nc.tensor.matmul(ps[:, u, 0:VW], g.ph[0:np_, k, q], v, start=first, stop=False)
                    nc.tensor.matmul(ps[:, u, 0:D], g.ph[0:np_, k, q], vl, start=False, stop=False)
                    mm = nc.tensor.matmul(ps[:, u, 0:VW], g.pl[0:np_, k, q], v, start=False, stop=last)
                mm.then_inc(s.pv, 1)

            def one(j, scores, values, n, next_scores):
                def body(t, k):
                    if values:
                        value(j, t, k)
                    if scores and not (isinstance(t, int) and t + 3 > LAST):
                        score(j, t + 3, k)
                    if scores and isinstance(t, int) and t == LAST - 2:
                        pe.wait_ge(s.maxed, (j + 1) * KT)
                        if n is not None:
                            pe.wait_ge(s.slots, n + 1)
                        for u in range(SUB):
                            mm = nc.tensor.transpose(ps[:, 7, u * P:(u + 1) * P], g.r[:, u * P:(u + 1) * P],
                                                     g.ident[:])
                        mm.then_inc(s.r_t, 1)

                if n is None:
                    cls_scores(nc, g, s, pe)
                    for k in range(3):
                        score(j, k, k)
                    steps = {1: lambda: cls_turn(nc, g, s, pe), 3: lambda: cls_spread(nc, g, s, pe),
                             7: lambda: cls_values(nc, g, s, pe), 9: lambda: None}
                else:
                    steps = {3: lambda: ep_turn(nc, g, s, pe, n, 0, *size(n)),
                             5: lambda: ep_turn(nc, g, s, pe, n, 1, *size(n)),
                             7: lambda: ep_logits(nc, g, s, pe, n, *size(n)),
                             9: lambda: ep_prefix(nc, g, s, pe, n, *size(n))}
                if scores or values:
                    keys_loop(pe, body, steps)
                else:
                    for step in steps.values():
                        step()
                if next_scores:
                    score(j + 1, 0, 0)
                if scores:
                    pe.wait_ge(s.diag, j + 1)
                    nc.tensor.matmul(ps[:, 7], g.ones[:], g.diag[:], start=True, stop=True).then_inc(s.m_ps, 1)
                if next_scores:
                    score(j + 1, 1, 1)
                    score(j + 1, 2, 2)

            one(0, True, False, None, True)
            one(1, True, True, 0, True)
            with pe.Fori(2, NQB - 1) as j:
                one(j, True, True, j - 1, True)
            one(NQB - 1, True, True, NQB - 2, False)
            one(NQB, False, True, NQB - 1, False)
            one(NQB + 1, False, False, NQB, False)


GROUPS = tuple((at, min(QB, CAP - at)) for at in range(0, CAP, QB))
NG = len(GROUPS)
PAIR = 2
TILES = tuple(-(-w // P) for _, w in GROUPS)
PG = PAIR * NG
ROUNDS = E // PAIR


def expert_weights(nc, g, a, sp, e, sem):
    sp.dma_start(g.w1_raw[:], a["L0_ffn_w1"][e].rearrange("(c p) f -> p c f", p=P)).then_inc(sem, 16)
    sp.dma_start(g.w2_raw[:], a["L0_ffn_w2"][e].rearrange("(c p) d -> p c d", p=P)).then_inc(sem, 16)


def expert_biases(nc, g, a, sp, e, half, sem):
    with nc.allow_non_contiguous_dma(reason="a bias onto the partitions"):
        sp.dma_start(g.b1[:, half], a["L0_ffn_b1"][e].rearrange("(c p) -> p c", p=P)).then_inc(sem, 16)
    sp.dma_start(g.b2[:, half], a["L0_ffn_b2"][e].rearrange("(a n) -> a n", a=1).to_broadcast((P, D)))\
        .then_inc(sem, 16)


def expert_largest(nc, g, dve, half, which):
    if which == 0:
        nc.vector.tensor_reduce(g.f_mx[:, half, 0:1], g.w1_raw[:], axis=AX.XY, op=ALU.max, apply_absolute_value=True)
    else:
        nc.vector.tensor_reduce(g.f_mx[:, half, 1:2], g.w2_raw[:], axis=AX.XY, op=ALU.max, apply_absolute_value=True)
        nc.vector.tensor_reduce(g.f_mx[:, half, 2:3], g.b1[:, half], axis=AX.X, op=ALU.max, apply_absolute_value=True)


def expert_scales(nc, g, dve, half):
    v, m = nc.vector, g.f_mx[:, half]
    sc, isc = g.f_sc[:, half], g.f_isc[:, half]
    v.scalar_tensor_tensor(out=m[:, 2:3], in0=m[:, 0:1], scalar=float(D), in1=m[:, 2:3], op0=ALU.mult, op1=ALU.add)
    dve.drain()
    scale_of(nc, dve, sc, isc, m)
    v.tensor_tensor(g.f_in[:, half], sc[:, 2:3], isc[:, 0:1], ALU.mult)
    v.tensor_tensor(g.f_out[:, half], isc[:, 2:3], isc[:, 1:2], ALU.mult)
    v.tensor_scalar(g.b1[:, half], g.b1[:, half], sc[:, 2:3], None, ALU.mult)
    dve.drain()
    v.tensor_scalar(g.f_in[:, half], g.f_in[:, half], 1.0 / A_SCALE, None, ALU.mult)


def expert_high(nc, g, half, which):
    raw, hi = ((g.w1_raw, g.w1_hi), (g.w2_raw, g.w2_hi))[which]
    return nc.scalar.activation(hi[:, half], raw[:], ACT.Copy, scale=g.f_sc[:, half, which:which + 1])


def expert_scaled(nc, g, half, which):
    raw = (g.w1_raw, g.w2_raw)[which]
    return nc.scalar.activation(raw[:], raw[:], ACT.Copy, scale=g.f_sc[:, half, which:which + 1])


def expert_low(nc, g, half, which):
    raw, hi, lo = ((g.w1_raw, g.w1_hi, g.w1_lo), (g.w2_raw, g.w2_hi, g.w2_lo))[which]
    return nc.vector.scalar_tensor_tensor(out=lo[:, half], in0=raw[:], scalar=g.f_sc[:, half, which:which + 1],
                                          in1=hi[:, half], op0=ALU.mult, op1=ALU.subtract)


def first_expert(nc, g, a):
    s = Names()
    s.f0_in, s.f0_max, s.f0_red, s.f0_sc, s.f0_hi = semaphores(nc, "f0_in f0_max f0_red f0_sc f0_hi")
    with nc.Block() as block:
        @block.sync
        def _(sp):
            expert_weights(nc, g, a, sp, 0, s.f0_in)
            expert_biases(nc, g, a, sp, 0, 0, s.f0_in)

        @block.vector
        def _(dve):
            nc.vector.memset(g.y[:], 0.0)
            dve.wait_ge(s.f0_in, 64)
            expert_largest(nc, g, dve, 0, 0)
            expert_largest(nc, g, dve, 0, 1)
            dve.drain().then_inc(s.f0_max, 1)
            dve.wait_ge(s.f0_red, 1)
            expert_scales(nc, g, dve, 0)
            dve.drain().then_inc(s.f0_sc, 1)
            dve.wait_ge(s.f0_hi, 1)
            expert_low(nc, g, 0, 0)
            expert_low(nc, g, 0, 1)

        @block.gpsimd
        def _(pool):
            pool.wait_ge(s.f0_max, 1)
            pool.partition_all_reduce(g.f_mx[:, 0], g.f_mx[:, 0], P, bass.bass_isa.ReduceOp.max).then_inc(s.f0_red, 1)

        @block.scalar
        def _(act):
            act.wait_ge(s.f0_sc, 1)
            expert_high(nc, g, 0, 0)
            expert_high(nc, g, 0, 1)
            act.drain().then_inc(s.f0_hi, 1)


def experts(nc, g, a, s):
    ps = g.ps
    out = a["out"].rearrange("b n d -> (b n) d")

    def width(i):
        return GROUPS[i % NG][1]

    def tiles(i):
        return TILES[i % NG]

    def rows_of(i, t):
        return min(P, width(i) - t * P)

    def later(ep, i, by):
        i += by
        if i >= PG:
            ep, i = ep + i // PG, i % PG
        return None if isinstance(ep, int) and ep >= ROUNDS else (ep, i)

    def count(ep, i):
        return ep * PG + i

    def got(ep, i):
        return (ep * PAIR + (i // NG + 1)) * (16 * tiles(i))

    def put(ep, i):
        whole, part = (sum(tiles(n) for n in range(i % 2, end, 2)) for end in (PG, i + 1))
        return ep * (16 * whole) + 16 * part

    def prepared(ep, i):
        q = ep * PAIR + i // NG
        return None if isinstance(q, int) and q == E - 1 else q

    def rounds(engine, group):
        group(0, 0)
        with engine.Fori(0, ROUNDS - 1) as ep:
            for i in range(1, PG):
                group(ep, i)
            group(ep + 1, 0)
        for i in range(1, PG):
            group(ROUNDS - 1, i)

    with nc.Block() as block:
        @block.sync
        def _(sp):
            def numbers(ep, i):
                at = ep * (PAIR * STRIDE) + (i // NG * STRIDE + GROUPS[i % NG][0])
                with nc.allow_non_contiguous_dma(reason="token numbers onto the partitions"):
                    sp.dma_start(g.ids[:, i, 0:tiles(i)], g.table[bass.ds(at, tiles(i) * P), 0]
                                 .rearrange("(t p) -> p t", p=P)).then_inc(s.ids[i], 16)

            for i in range(PG):
                numbers(0, i)
            expert_weights(nc, g, a, sp, 1, s.f_w)
            expert_biases(nc, g, a, sp, 1, 1, s.f_w)
            with sp.Fori(0, ROUNDS - 1) as ep:
                for i in range(PG):
                    if i % NG == NG - 1:
                        sp.wait_ge(s.w_low, (ep * PAIR + (i // NG + 1)) * 2)
                        settle(g, sp)
                        expert_weights(nc, g, a, sp, ep * PAIR + (i // NG + 2), s.f_w)
                        sp.wait_ge(s.y_made, count(ep, i) + 1)
                        settle(g, sp)
                        expert_biases(nc, g, a, sp, ep * PAIR + (i // NG + 2), i // NG, s.f_w)
                    sp.wait_ge(s.put[i % 2], put(ep, i))
                    settle(g, sp)
                    numbers(ep + 1, i)

        @block.gpsimd
        def _(pool):
            def gather(ep, i):
                pool.wait_ge(s.ids[i], ep * 16 + 16)
                settle(g, pool)
                for t in range(tiles(i)):
                    pool.indirect_dma_start(out=g.tok[:, i % 3, t], out_offset=None, in_=g.rows[:, :],
                                            in_offset=bass.IndirectOffsetOnAxis(ap=g.ids[:, i, t:t + 1], axis=0))\
                        .then_inc(s.got[i % 3], 16)

            def scatter(ep, i):
                for t in range(tiles(i)):
                    pool.indirect_dma_start(out=out, out_offset=bass.IndirectOffsetOnAxis(ap=g.ids[:, i, t:t + 1],
                                                                                          axis=0),
                                            in_=g.res[:, i % 2, t], in_offset=None, bounds_check=T - 1,
                                            oob_is_err=False).then_inc(s.put[i % 2], 16)

            def low(q, half, which):
                pool.wait_ge(s.w_high, q * 2 + which + 1)
                settle(g, pool)
                raw, hi, lo = ((g.w1_raw, g.w1_hi, g.w1_lo), (g.w2_raw, g.w2_hi, g.w2_lo))[which]
                pool.tensor_tensor(lo[:, half], raw[:], hi[:, half], ALU.subtract).then_inc(s.w_low, 1)

            def group(ep, i):
                q = prepared(ep, i)
                half = i // NG
                prepare = i % NG == 1 and q is not None
                if prepare:
                    pool.wait_ge(s.w_max, q + 1)
                    settle(g, pool)
                    pool.partition_all_reduce(g.f_mx[:, 1 - half], g.f_mx[:, 1 - half], P,
                                              bass.bass_isa.ReduceOp.max).then_inc(s.w_red, 1)
                    low(q, 1 - half, 0)
                if not (isinstance(ep, int) and ep == 0 and i == 0):
                    before = (ep, i - 1) if i else (ep - 1, PG - 1)
                    pool.wait_ge(s.y_done, count(*before) + 1)
                    settle(g, pool)
                    if later(ep, i, 2):
                        gather(*later(ep, i, 2))
                    if prepare:
                        low(q, 1 - half, 1)
                    scatter(*before)

            for i in range(3):
                gather(0, i)
            rounds(pool, group)
            pool.wait_ge(s.y_done, ROUNDS * PG)
            scatter(ROUNDS - 1, PG - 1)
            for i in (PG - 2, PG - 1):
                pool.wait_ge(s.put[i % 2], put(ROUNDS - 1, i))

        @block.scalar
        def _(act):
            nc.scalar.activation(g.warm[:], g.ones[:, 0:1], ACT.Exp)

            def high(ep, i, c):
                act.wait_ge(s.turned, count(ep, i) * DC + (c + 1))
                w = tiles(i) * P
                nc.scalar.activation(g.x_hi[:, i % 2, c, 0:w], ps[:, 7, 0:w], ACT.Copy, scale=A_SCALE)\
                    .then_inc(s.x_high, 1)

            def group(ep, i):
                w, half = width(i), i // NG
                for f in range(FC):
                    n = count(ep, i) * FC + f
                    bank, k = (i * FC + f) % 3, (i * FC + f) % 3
                    if f in (4, 6) and later(ep, i, 1):
                        high(*later(ep, i, 1), f // 2 - 2)
                    act.wait_ge(s.l1, n + 1)
                    wait(act, s.h_low, n - 2)
                    nc.scalar.activation(g.hf[:, k, 0:w], ps[:, 4 + bank, 0:w], ACT.Relu,
                                         scale=g.f_in[:, half], bias=g.b1[:, half, f:f + 1])
                    act.drain().then_inc(s.relu, 1)
                    wait(act, s.l2, n - 2)
                    nc.scalar.activation(g.hh[:, k, 0:w], g.hf[:, k, 0:w], ACT.Copy).then_inc(s.h_high, 1)
                    q = prepared(ep, i)
                    if i % NG == 1 and f in (4, 6) and q is not None:
                        act.wait_ge(s.w_sc, q + 1)
                        expert_scaled(nc, g, 1 - half, f // 2 - 2)
                    if i % NG == 1 and f in (5, 7) and q is not None:
                        raw, hi = ((g.w1_raw, g.w1_hi), (g.w2_raw, g.w2_hi))[f // 2 - 2]
                        nc.scalar.activation(hi[:, 1 - half], raw[:], ACT.Copy)
                        act.drain().then_inc(s.w_high, 1)

            for c in range(DC):
                high(0, 0, c)
            rounds(act, group)

        @block.vector
        def _(dve):
            v = nc.vector

            def low(ep, i, c):
                dve.wait_ge(s.x_high, count(ep, i) * DC + (c + 1))
                w = tiles(i) * P
                v.scalar_tensor_tensor(out=g.x_lo[:, i % 2, c, 0:w], in0=ps[:, 7, 0:w], scalar=A_SCALE,
                                       in1=g.x_hi[:, i % 2, c, 0:w], op0=ALU.mult, op1=ALU.subtract)\
                    .then_inc(s.x_low, 1)

            def collect(ep, i):
                half = i // NG
                dve.wait_ge(s.l2, (count(ep, i) + 1) * FC)
                for t in range(tiles(i)):
                    m = rows_of(i, t)
                    v.scalar_tensor_tensor(out=g.y[0:m, t], in0=ps[0:m, i % 2 * 2 + t // 2, t % 2 * D:(t % 2 + 1) * D],
                                           scalar=g.f_out[0:m, half], in1=g.b2[0:m, half],
                                           op0=ALU.mult, op1=ALU.add)
                dve.drain().then_inc(s.y_made, 1)

            def finish(ep, i, stage):
                w = tiles(i)
                y, sign, finite, res = g.y[:, 0:w], g.sign[:, 0:w], g.finite[:, 0:w], g.res[:, i % 2, 0:w]
                z = g.tok[:, i % 3, 0:w, D:2 * D]
                if stage == 0:
                    dve.wait_ge(s.got[i % 3], got(ep, i))
                    for t in range(w):
                        v.tensor_scalar(g.y[:, t], g.y[:, t], g.tok[:, i % 3, t, 2 * D:ROW], None, ALU.mult)
                    dve.drain()
                    v.tensor_scalar(sign, y, float("inf"), None, ALU.is_equal)
                    v.tensor_scalar(finite, y, 0.0, 0.0, ALU.mult, ALU.is_equal)
                if stage == 1:
                    v.scalar_tensor_tensor(out=sign, in0=y, scalar=float("-inf"), in1=sign,
                                           op0=ALU.is_equal, op1=ALU.subtract)
                if stage == 2:
                    before = (ep, i - 2) if i >= 2 else (ep - 1, i + PG - 2)
                    if not (isinstance(before[0], int) and before[0] < 0):
                        dve.wait_ge(s.put[i % 2], put(*before))
                        settle(g, dve)
                    v.scalar_tensor_tensor(out=res, in0=sign, scalar=-10000.0, in1=z, op0=ALU.mult, op1=ALU.add)
                if stage == 3:
                    v.tensor_tensor(y, y, z, ALU.add)
                if stage == 4:
                    v.copy_predicated(res, finite, y)
                dve.drain()
                if stage == 4:
                    dve.sem_inc(s.y_done, 1)

            def group(ep, i):
                w, half = width(i), i // NG
                started = not (isinstance(ep, int) and ep == 0 and i == 0)
                before = (ep, i - 1) if i else (ep - 1, PG - 1)
                q = prepared(ep, i)
                for f in range(FC):
                    n, k = count(ep, i) * FC + f, (i * FC + f) % 3
                    if f in (4, 6) and later(ep, i, 1):
                        low(*later(ep, i, 1), f // 2 - 2)
                    dve.wait_ge(s.h_high, n + 1)
                    v.tensor_tensor(g.hl[:, k, 0:w], g.hf[:, k, 0:w], g.hh[:, k, 0:w], ALU.subtract)\
                        .then_inc(s.h_low, 1)
                    if f == 1 and started:
                        collect(*before)
                    if f >= 2 and f - 2 < 5 and started:
                        finish(*before, f - 2)
                    if q is not None and (i % NG, f) == (0, FC - 1):
                        dve.wait_ge(s.f_w, q * 64 + 64)
                        expert_largest(nc, g, dve, 1 - half, 0)
                    if q is not None and (i % NG, f) == (1, 0):
                        expert_largest(nc, g, dve, 1 - half, 1)
                        dve.drain().then_inc(s.w_max, 1)
                    if q is not None and (i % NG, f) == (1, 3):
                        dve.wait_ge(s.w_red, q + 1)
                        expert_scales(nc, g, dve, 1 - half)
                        dve.drain().then_inc(s.w_sc, 1)

            for c in range(DC):
                low(0, 0, c)
            rounds(dve, group)
            collect(ROUNDS - 1, PG - 1)
            for stage in range(5):
                finish(ROUNDS - 1, PG - 1, stage)

        @block.tensor
        def _(pe):
            def turn(ep, i, c):
                if c == 0:
                    pe.wait_ge(s.got[i % 3], got(ep, i))
                wait(pe, s.x_low, count(ep, i) * DC + c)
                for t in range(tiles(i)):
                    last = nc.tensor.transpose(ps[:, 7, t * P:(t + 1) * P],
                                               g.tok[:, i % 3, t, c * P:(c + 1) * P], g.ident[:])
                last.then_inc(s.turned, 1)

            def hidden(ep, i, f):
                half, w, n = i // NG, width(i), count(ep, i) * FC + f
                if f == 0:
                    pe.wait_ge(s.x_low, (count(ep, i) + 1) * DC)
                    if i % NG == 0:
                        wait(pe, s.w_low, (ep * PAIR + half) * 2)
                wait(pe, s.relu, n - 2)
                k, cols = (i * FC + f) % 3, slice(f * P, (f + 1) * P)
                products(nc, ps[:, 4 + k, 0:w], [(g.w1_hi[:, half, c, cols], g.w1_lo[:, half, c, cols],
                                                  g.x_hi[:, i % 2, c, 0:w], g.x_lo[:, i % 2, c, 0:w])
                                                 for c in range(DC)]).then_inc(s.l1, 1)

            def output(ep, i, f):
                half, n, k = i // NG, count(ep, i) * FC + f, (i * FC + f) % 3
                pe.wait_ge(s.h_low, n + 1)
                if f == 0:
                    wait(pe, s.y_made, count(ep, i) - 1)
                for t in range(tiles(i)):
                    m = rows_of(i, t)
                    at = slice(t * P, t * P + m)
                    last = products(nc, ps[0:m, i % 2 * 2 + t // 2, t % 2 * D:(t % 2 + 1) * D],
                                    [(g.hh[:, k, at], g.hl[:, k, at], g.w2_hi[:, half, f], g.w2_lo[:, half, f])],
                                    start=f == 0 and t % 2 == 0,
                                    stop=f == FC - 1 and (t % 2 == 1 or t == tiles(i) - 1))
                last.then_inc(s.l2, 1)

            def group(ep, i):
                for f in range(FC):
                    if f in (3, 5) and later(ep, i, 1):
                        turn(*later(ep, i, 1), f // 2 - 1)
                    ahead = (ep, i) if f < FC - 2 else later(ep, i, 1)
                    if ahead:
                        hidden(*ahead, (f + 2) % FC)
                    output(ep, i, f)

            turn(0, 0, 0)
            turn(0, 0, 1)
            hidden(0, 0, 0)
            hidden(0, 0, 1)
            rounds(pe, group)


class Arena:

    def __init__(self, words, at):
        self.words, self.at = words, at

    def take(self, shape, dt):
        n = 1
        for x in shape[1:]:
            n *= x
        n = n if dt != F16 else n // 2
        view = self.words[:, self.at:self.at + n]
        self.at += n
        if dt != F32:
            view = view.bitcast(dt)
        if len(shape) == 3:
            view = view.rearrange("p (a b) -> p a b", b=shape[2])
        if len(shape) == 4:
            view = view.rearrange("p (a b c) -> p a b c", b=shape[2], c=shape[3])
        return view


def tower(nc, a):
    g = Names()
    g.w_hi = nc.alloc_sbuf_tensor("w_hi", [P, 3, DC, D], F16)
    g.w_lo = nc.alloc_sbuf_tensor("w_lo", [P, 3, DC, D], F16)
    g.lin_t = nc.alloc_sbuf_tensor("lin_t", [P, DC, D], F32)
    g.gate_w = nc.alloc_sbuf_tensor("gate_w", [P, DC, E], F32)
    g.taps = nc.alloc_sbuf_tensor("taps", [P, DC, 9], F32)
    g.vecs = nc.alloc_sbuf_tensor("vecs", [P, 8, DC], F32)
    g.lin_b = nc.alloc_sbuf_tensor("lin_b", [P, D], F32)
    g.bv = nc.alloc_sbuf_tensor("bv", [P, D], F32)
    g.gate_b = nc.alloc_sbuf_tensor("gate_b", [P, E], F32)
    g.mx = nc.alloc_sbuf_tensor("mx", [P, 6], F32)
    g.sc = nc.alloc_sbuf_tensor("sc", [P, 6], F32)
    g.isc = nc.alloc_sbuf_tensor("isc", [P, 6], F32)
    g.ratio = nc.alloc_sbuf_tensor("ratio", [P, 3], F32)
    g.score = nc.alloc_sbuf_tensor("score", [P, 1], F32)
    g.bqk = nc.alloc_sbuf_tensor("bqk", [P, 2, DC], F32)
    g.bn_v = nc.alloc_sbuf_tensor("bn_v", [P, DC], F32)
    g.bn_r = nc.alloc_sbuf_tensor("bn_r", [P, DC], F32)
    g.bn_s = nc.alloc_sbuf_tensor("bn_s", [P, DC], F32)
    g.bn_h = nc.alloc_sbuf_tensor("bn_h", [P, DC], F32)
    g.ones = nc.alloc_sbuf_tensor("ones", [P, P], F32)
    g.ones16 = nc.alloc_sbuf_tensor("ones16", [P, P], F16)
    g.upper = nc.alloc_sbuf_tensor("upper", [P, P], F16)
    g.ident = nc.alloc_sbuf_tensor("ident", [P, P], F32)
    g.expo = nc.alloc_sbuf_tensor("expo", [P, SUB], F32)
    g.carry = nc.alloc_sbuf_tensor("carry", [P, E], F32)
    g.warm = nc.alloc_sbuf_tensor("warm", [P, 1], F32)
    g.tok_f = nc.alloc_sbuf_tensor("tok_f", [P, SUB], F32)
    g.tok_i = nc.alloc_sbuf_tensor("tok_i", [P, SUB], I32)
    g.weight = nc.alloc_sbuf_tensor("weight", [P, SUB, E], F32)
    g.slot0 = nc.alloc_sbuf_tensor("slot0", [P, SUB, E], F32)
    g.st = nc.alloc_sbuf_tensor("st", [P, SUB, 6], F32)
    g.mv = nc.alloc_sbuf_tensor("mv", [P, SUB, 2], F32)
    g.var = nc.alloc_sbuf_tensor("var", [P, SUB], F32)
    g.rstd = nc.alloc_sbuf_tensor("rstd", [P, SUB], F32)
    g.rs = nc.alloc_sbuf_tensor("rs", [P, SUB], F32)
    g.r_l = nc.alloc_sbuf_tensor("r_l", [P, SUB, E], F32)
    g.r_e = nc.alloc_sbuf_tensor("r_e", [P, SUB, E], F32)
    g.r_k = nc.alloc_sbuf_tensor("r_k", [P, SUB, E], F32)
    g.r_oh = nc.alloc_sbuf_tensor("r_oh", [P, SUB, E], F16)
    g.r_m = nc.alloc_sbuf_tensor("r_m", [P, SUB], F32)
    g.r_d = nc.alloc_sbuf_tensor("r_d", [P, SUB], F32)
    g.r_x = nc.alloc_sbuf_tensor("r_x", [P, SUB], F32)
    g.idx_f = nc.alloc_sbuf_tensor("idx_f", [P, SUB], F32)
    g.idx_i = nc.alloc_sbuf_tensor("idx_i", [P, SUB], I32)
    g.c_m = nc.alloc_sbuf_tensor("c_m", [P, 1], F32)
    g.c_m1 = nc.alloc_sbuf_tensor("c_m1", [P, 1], F32)
    g.c_hb = nc.alloc_sbuf_tensor("c_hb", [P, 1, D], F32)
    g.c_q = nc.alloc_sbuf_tensor("c_q", [P, DC, 2], F16)
    g.c_s = nc.alloc_sbuf_tensor("c_s", [P, KT], F32)
    g.c_hi = nc.alloc_sbuf_tensor("c_hi", [P, KT + 1], F16)
    g.c_lo = nc.alloc_sbuf_tensor("c_lo", [P, KT + 1], F16)
    g.mq = nc.alloc_sbuf_tensor("mq", [P, SUB], F32)
    words = 49000
    g.arena = nc.alloc_sbuf_tensor("arena", [P, words], F32)
    g.ps = nc.alloc_psum_tensor("ps", [P, 8, 512], F32)

    kept = Arena(g.arena, 0)
    g.q_hi = kept.take([P, DC, N + 7], F16)
    g.q_lo = kept.take([P, DC, N + 7], F16)
    g.k_hi = kept.take([P, DC, N + 7], F16)
    g.k_lo = kept.take([P, DC, N + 7], F16)
    g.v_hi = kept.take([P, KT, VW + 3], F16)
    g.v_lo = kept.take([P, KT, D], F16)
    g.v_hi = g.v_hi[:, :, 0:VW]
    g.row = kept.take([P, SUB, ROW], F32)
    g.hb = kept.take([P, SUB, D], F32)
    strips = Arena(g.arena, kept.at)
    g.xp = strips.take([P, DC, PW, PW], F32)
    g.x_in = strips.take([P, 2, DC, QB], F32)
    g.y_t = strips.take([P, 2, DC, QB], F32)
    g.h = strips.take([P, SUB, D], F32)
    g.a = strips.take([P, SUB, D], F32)
    g.a_hi = strips.take([P, 2, DC, QB], F16)
    g.a_lo = strips.take([P, 2, DC, QB], F16)
    g.p_f = strips.take([P, 2, QB], F32)
    blocks = Arena(g.arena, kept.at)
    g.panel = blocks.take([P, KT, QB], F32)
    g.ph = blocks.take([P, 3, QB], F16)
    g.pl = blocks.take([P, 3, QB], F16)
    g.r = blocks.take([P, QB], F32)
    g.m = blocks.take([P, QB], F32)
    g.z_t = blocks.take([P, DC, QB], F32)
    g.diag = g.z_t[:, 0]
    mixture = Arena(g.arena, 0)
    g.w1_raw = mixture.take([P, DC, F], F32)
    g.w2_raw = mixture.take([P, FC, D], F32)
    g.w1_hi = mixture.take([P, PAIR, DC, F], F16)
    g.w1_lo = mixture.take([P, PAIR, DC, F], F16)
    g.w2_hi = mixture.take([P, PAIR, FC, D], F16)
    g.w2_lo = mixture.take([P, PAIR, FC, D], F16)
    g.b1 = mixture.take([P, PAIR, FC], F32)
    g.b2 = mixture.take([P, PAIR, D], F32)
    g.tok = mixture.take([P, 3, SUB, ROW], F32)
    g.x_hi = mixture.take([P, 2, DC, QB], F16)
    g.x_lo = mixture.take([P, 2, DC, QB], F16)
    g.hf = mixture.take([P, 3, QB], F32)
    g.hh = mixture.take([P, 3, QB], F16)
    g.hl = mixture.take([P, 3, QB], F16)
    g.y = mixture.take([P, SUB, D], F32)
    g.sign = mixture.take([P, SUB, D], F32)
    g.finite = mixture.take([P, SUB, D], I32)
    g.res = mixture.take([P, 2, SUB, D], F32)
    g.ids = mixture.take([P, PAIR * NG, SUB], I32)
    g.f_mx = mixture.take([P, PAIR, 3], F32)
    g.f_sc = mixture.take([P, PAIR, 3], F32)
    g.f_isc = mixture.take([P, PAIR, 3], F32)
    g.f_in = mixture.take([P, PAIR, 1], F32)
    g.f_out = mixture.take([P, PAIR, 1], F32)
    first = Arena(g.arena, strips.at)
    g.w_raw = first.take([P, 3, DC, D], F32)
    g.zrow = first.take([P, ROW], F32)
    g.iota_i = first.take([P, SUB], I32)
    g.weight_i = first.take([P, SUB, E], I32)
    g.base_i = first.take([P, SUB, E], I32)
    g.none_f = first.take([P, E * STRIDE // P], F32)
    g.none_i = first.take([P, E * STRIDE // P], I32)
    assert max(first.at, blocks.at, mixture.at) <= words, (kept.at, strips.at, first.at, blocks.at, mixture.at)

    g.table = nc.dram_tensor("slot_tokens", [E * STRIDE, 1], I32, kind="Internal").ap()
    g.rows = nc.dram_tensor("token_rows", [T + 1, ROW], F32, kind="Internal").ap()
    g.h_res = nc.dram_tensor("residual_rows", [B, NP, D], F32, kind="Internal").ap()

    setup(nc, g, a)
    class_row(nc, g, a)
    s = Names()
    (s.cleared, s.x_in0, s.x_in1, s.xn, s.y_t, s.lin, s.h_made, s.h_out, s.var, s.rstd, s.a, s.aT, s.a_hi, s.a_lo,
     s.proj, s.p_f, s.p_hi, s.p_lo, s.hb, s.o, s.var2, s.rstd2, s.z, s.zT, s.z_t, s.logits, s.l_sub, s.l_exp,
     s.routed, s.prefix, s.slots, s.o_out, s.r_out, s.h_in, s.sub, s.m, s.m_ps, s.p_hi2, s.p_lo2, s.pv, s.qk,
     s.kept, s.maxed, s.r_t, s.diag, s.settled, s.c_qk, s.c_maxed, s.c_turned, s.c_top, s.c_spread, s.c_sub,
     s.c_high, s.c_low, s.c_pv) = \
        s.handles = semaphores(
            nc, "cleared x_in0 x_in1 xn y_t lin h_made h_out var rstd a aT a_hi a_lo proj p_f p_hi p_lo hb o var2 rstd2 "
                "z zT z_t logits l_sub l_exp routed prefix slots o_out r_out h_in sub m m_ps p_hi2 p_lo2 pv qk "
                 "kept maxed r_t diag settled c_qk c_maxed c_turned c_top c_spread c_sub c_high c_low c_pv")
    s.x_in, g.settled = (s.x_in0, s.x_in1), s.settled
    s.tab, = semaphores(nc, "tab")
    with nc.Fori(0, B) as b:
        clear(nc, s)
        s.tab0 = b * (16 * (SUB * NQB + 1))
        tokenizer(nc, g, a, b, s)
        attention(nc, g, a, b, s)
    first_expert(nc, g, a)
    f = Names()
    (f.f_w, f.w_max, f.w_red, f.w_sc, f.w_high, f.w_low, f.turned, f.x_high, f.x_low, f.l1, f.relu, f.h_high,
     f.h_low, f.l2, f.y_made, f.y_done) = semaphores(
        nc, "f_w w_max w_red w_sc w_high w_low turned x_high x_low l1 relu h_high h_low l2 y_made y_done")
    f.ids = semaphores(nc, "ids0 ids1 ids2 ids3 ids4 ids5")
    f.got, f.put = semaphores(nc, "got0 got1 got2"), semaphores(nc, "put0 put1")
    experts(nc, g, a, f)


_INS = ["xT", "cls_tok", "L0_tok_bn_gamma", "L0_tok_bn_beta", "L0_tok_bn_mean", "L0_tok_bn_var", "conv_taps",
        "L0_tok_conv_b", "lin_wT", "L0_tok_lin_b", "L0_attn_Wq", "L0_attn_bq", "L0_attn_Wk", "L0_attn_bk",
        "L0_attn_Wv", "L0_attn_bv", "L0_ffn_gate_w", "L0_ffn_gate_b", "L0_ffn_w1", "L0_ffn_b1", "L0_ffn_w2",
        "L0_ffn_b2"]


def kernel(**inputs):
    import numpy as _np
    import concourse.bacc as _bacc
    from concourse.bass_utils import run_bass_kernel_spmd as _run

    laid = {k: _np.asarray(v) for k, v in inputs.items()}
    laid["xT"] = laid["x"].reshape(B, NP, D).transpose(0, 2, 1)
    laid["conv_taps"] = laid["L0_tok_conv_w"].reshape(D, 9)
    laid["lin_wT"] = laid["L0_tok_lin_w"].T
    nc = _bacc.Bacc("TRN2", target_bir_lowering=False, num_devices=1)
    arrays, a = {}, {}
    for name in _INS:
        arrays[f"in_{name}"] = _np.ascontiguousarray(laid[name])
        a[name] = nc.dram_tensor(f"in_{name}", arrays[f"in_{name}"].shape, F32, kind="ExternalInput").ap()
    a["out"] = nc.dram_tensor("out_tokens", (B, N, D), F32, kind="ExternalOutput").ap()
    tower(nc, a)
    r = _run(nc, [arrays], core_ids=[0])
    return r.results[0]["out_tokens"]
```

```python
import concourse.bass as bass
from concourse import mybir

F32, F16, I32 = mybir.dt.float32, mybir.dt.float16, mybir.dt.int32
ALU, ACT, AX = mybir.AluOpType, mybir.ActivationFunctionType, mybir.AxisListType

B, IMG, D, E, F = 2, 64, 256, 8, 1024
P = 128
NP = IMG * IMG
N = NP + 1
T = B * N
DC, FC = D // P, F // P
CAP = -(-5 * T // (4 * E))
GT = -(-CAP // P)
STRIDE = GT * P
QB = 512
NQB = NP // QB
SUB = QB // P
KT = NP // P + 1
LAST = KT - 1
NT = LAST
KEYED = 256
ROWS8 = QB // IMG
UPPER = 3
PW = IMG + 2
VW = D + 1
ROW = 2 * D + 1
A_SCALE, P_SCALE, TOP = 2.0 ** 10, 2.0 ** 14, 2.0 ** 13
NONE = T
BIG = float(2 ** 20)
EPS = 1e-5


class Names:
    pass


def semaphores(nc, names):
    return [nc.alloc_semaphore(n) for n in names.split()]


def clear(nc, s):
    with nc.Block() as block:
        @block.gpsimd
        def _(pool):
            for handle in s.handles[0::4]:
                pool.sem_clear(handle)

        @block.vector
        def _(dve):
            for handle in s.handles[1::4]:
                dve.sem_clear(handle)

        @block.scalar
        def _(act):
            for handle in s.handles[2::4]:
                act.sem_clear(handle)

        @block.tensor
        def _(pe):
            for handle in s.handles[3::4]:
                pe.sem_clear(handle)


def setup(nc, g, a):
    s = Names()
    s.w_in, s.qkv_in, s.vec_in, s.c_made, s.w0_max, s.w0_red, s.sc_made, s.w0_hi = semaphores(
        nc, "w_in qkv_in vec_in c_made w0_max w0_red sc_made w0_hi")
    W = (a["L0_attn_Wq"], a["L0_attn_Wk"], a["L0_attn_Wv"])
    with nc.Block() as block:
        @block.sync
        def _(sp):
            for i in range(3):
                sp.dma_start(g.w_raw[:, i], W[i].rearrange("(c p) e -> p c e", p=P)).then_inc(s.qkv_in, 16)
            sp.dma_start(g.lin_t[:], a["lin_wT"].rearrange("(c p) d -> p c d", p=P)).then_inc(s.w_in, 16)
            sp.dma_start(g.gate_w[:], a["L0_ffn_gate_w"].rearrange("(c p) e -> p c e", p=P)).then_inc(s.w_in, 16)
            sp.dma_start(g.taps[:], a["conv_taps"].rearrange("(c p) k -> p c k", p=P)).then_inc(s.w_in, 16)
            for dst, n in ((g.lin_b, "L0_tok_lin_b"), (g.bv, "L0_attn_bv"), (g.gate_b, "L0_ffn_gate_b")):
                sp.dma_start(dst[:], a[n].rearrange("(a n) -> a n", a=1).to_broadcast((P, a[n].shape[0])))\
                    .then_inc(s.w_in, 16)
            sp.wait_ge(s.c_made, 1)
            sp.dma_start(g.table.rearrange("(p n) a -> p (n a)", p=P), g.none_i[:]).then_inc(s.w_in, 16)
            sp.dma_start(g.rows[T:T + 1, :], g.zrow[0:1, :]).then_inc(s.w_in, 16)
            sp.wait_ge(s.w_in, 16 * 8)

        @block.gpsimd
        def _(pool):
            pool.memset(g.ones[:], 1.0)
            pool.memset(g.none_f[:], float(NONE))
            pool.memset(g.zrow[:], 0.0)
            pool.memset(g.ident[:], 0.0)
            pool.memset(g.expo[:], -0.5)
            pool.memset(g.carry[:], 0.0)
            pool.memset(g.ones16[:], 1.0)
            pool.iota(g.iota_i[:], [[P, SUB]], base=0, channel_multiplier=1)
            pool.iota(g.weight_i[:], [[0, SUB], [-1, E]], base=E, channel_multiplier=0)
            pool.iota(g.base_i[:], [[0, SUB], [STRIDE, E]], base=-1, channel_multiplier=0)
            pool.drain()
            pool.affine_select(out=g.ident[:], in_=g.ident[:], compare_op=ALU.not_equal, fill=1.0, base=0,
                               pattern=[[-1, P]], channel_multiplier=1)
            pool.affine_select(out=g.upper[:], in_=g.ones16[:], compare_op=ALU.is_ge, fill=0.0, base=0,
                               pattern=[[1, P]], channel_multiplier=-1)
            pool.tensor_copy(g.none_i[:], g.none_f[:])
            pool.tensor_copy(g.tok_f[:], g.iota_i[:])
            pool.tensor_copy(g.weight[:], g.weight_i[:])
            pool.tensor_copy(g.slot0[:], g.base_i[:])
            pool.drain().then_inc(s.c_made, 1)
            pool.wait_ge(s.w0_max, 1)
            pool.partition_all_reduce(g.mx[:, 0:6], g.mx[:, 0:6], P, bass.bass_isa.ReduceOp.max).then_inc(s.w0_red, 1)
            pool.wait_ge(s.sc_made, 1)
            pool.tensor_tensor(g.bn_r[:], g.bn_v[:], g.expo[:, 0:DC], ALU.pow)
            pool.drain().then_inc(s.w0_red, 1)

        @block.vector
        def _(dve):
            dve.wait_ge(s.qkv_in, 16 * 3)
            dve.wait_ge(s.vec_in, 16 * 8)
            for i in range(3):
                nc.vector.tensor_reduce(g.mx[:, i:i + 1], g.w_raw[:, i], axis=AX.XY, op=ALU.max,
                                        apply_absolute_value=True)
                nc.vector.tensor_reduce(g.mx[:, 3 + i:4 + i], g.vecs[:, 5 + i], axis=AX.X, op=ALU.max,
                                        apply_absolute_value=True)
            nc.vector.tensor_scalar(g.bn_v[:], g.vecs[:, 3], EPS, None, ALU.add)
            dve.drain().then_inc(s.w0_max, 1)
            dve.wait_ge(s.w0_red, 1)
            nc.vector.scalar_tensor_tensor(out=g.mx[:, 3:6], in0=g.mx[:, 0:3], scalar=float(D), in1=g.mx[:, 3:6],
                                           op0=ALU.mult, op1=ALU.add)
            dve.drain()
            scale_of(nc, dve, g.sc[:, 0:6], g.isc[:, 0:6], g.mx[:, 0:6])
            nc.vector.tensor_tensor(g.ratio[:], g.sc[:, 3:6], g.isc[:, 0:3], ALU.mult)
            nc.vector.tensor_tensor(g.score[:], g.isc[:, 3:4], g.isc[:, 4:5], ALU.mult)
            dve.drain()
            nc.vector.tensor_scalar(g.ratio[:], g.ratio[:], 1.0 / A_SCALE, None, ALU.mult)
            nc.vector.tensor_scalar(g.score[:], g.score[:], float(D) ** -0.5, None, ALU.mult)
            for i in range(2):
                nc.vector.tensor_scalar(g.bqk[:, i], g.vecs[:, 5 + i], g.sc[:, 3 + i:4 + i], None, ALU.mult)
            dve.drain().then_inc(s.sc_made, 1)
            dve.wait_ge(s.w0_red, 2)
            nc.vector.tensor_tensor(g.bn_s[:], g.vecs[:, 0], g.bn_r[:], ALU.mult)
            dve.drain()
            nc.vector.tensor_tensor(g.bn_h[:], g.vecs[:, 2], g.bn_s[:], ALU.mult)
            dve.drain()
            nc.vector.tensor_tensor(g.bn_h[:], g.vecs[:, 1], g.bn_h[:], ALU.subtract)
            dve.wait_ge(s.w_in, 16 * 8)
            for c in range(DC):
                for tap in range(UPPER):
                    nc.vector.tensor_scalar(g.t_diag[:, c, tap], g.ident[:], g.taps[:, c, tap:tap + 1], None, ALU.mult)
            dve.wait_ge(s.w0_hi, 1)
            for i in range(3):
                nc.vector.scalar_tensor_tensor(out=g.w_lo[:, i], in0=g.w_raw[:, i], scalar=g.sc[:, i:i + 1],
                                               in1=g.w_hi[:, i], op0=ALU.mult, op1=ALU.subtract)

        @block.scalar
        def _(act):
            with nc.allow_non_contiguous_dma(reason="vectors of 256 onto the partitions"):
                for i, n in enumerate(("L0_tok_bn_gamma", "L0_tok_bn_beta", "L0_tok_bn_mean", "L0_tok_bn_var",
                                       "L0_tok_conv_b", "L0_attn_bq", "L0_attn_bk", "L0_attn_bv")):
                    act.dma_start(g.vecs[:, i], a[n].rearrange("(c p) -> p c", p=P)).then_inc(s.vec_in, 16)
            act.wait_ge(s.sc_made, 1)
            for i in range(3):
                last = nc.scalar.activation(g.w_hi[:, i], g.w_raw[:, i], ACT.Copy, scale=g.sc[:, i:i + 1])
            last.then_inc(s.w0_hi, 1)


def scale_of(nc, dve, scale, inverse, bound):
    nc.vector.tensor_scalar(inverse, bound, 2.0 ** -30, 2.0 ** 60, ALU.max, ALU.min)
    dve.drain()
    nc.vector.tensor_scalar(inverse.bitcast(I32), inverse.bitcast(I32), 0x7F800000, None, ALU.bitwise_and)
    dve.drain()
    nc.vector.reciprocal(scale, inverse)
    dve.drain()
    nc.vector.tensor_scalar(scale, scale, TOP, None, ALU.mult)
    nc.vector.tensor_scalar(inverse, inverse, 1.0 / TOP, None, ALU.mult)
    dve.drain()


def wait(engine, semaphore, value):
    if not isinstance(value, int) or value > 0:
        engine.wait_ge(semaphore, value)


def settle(g, engine):
    engine.sem_inc(g.settled, 1)


def tokenizer(nc, g, a, b, s):
    ps, xp = g.ps, g.xp

    def projected(m, i, parts):
        w, c = m // 2, m % 2
        if w < 2:
            return parts[w][:, c, bass.ds(i * QB, QB)], g.p_f[:, m % 2]
        return parts[2][:, bass.ds(i * SUB + 2 * c, 2), 0:D], g.p_f[:, m % 2].rearrange("p (t d) -> p t d", d=D)

    def rounds(engine, one):
        one(0, 0, "ab")
        one(1, 1, "abc")
        with engine.Fori(1, NQB // 2 - 1) as r:
            one(r * 2, 0, "abcd")
            one(r * 2 + 1, 1, "abcd")
        one(NQB - 2, 0, "abcd")
        one(NQB - 1, 1, "bcd")
        one(NQB, 0, "cd")
        one(NQB + 1, 1, "d")

    def under(c, i, tap):
        return xp[:, c, bass.ds(i * ROWS8 + tap // 3, ROWS8), tap % 3:tap % 3 + IMG]

    with nc.Block() as block:
        @block.sync
        def _(sp):
            def load(i, k):
                wait(sp, s.xn, i - 1)
                load_strip(g, a, sp, b, i, k, s.x_in[k])

            def store(i):
                wait(sp, s.h_made, i + 1)
                sp.dma_start(g.h_res[b, bass.ds(i * QB, QB), :].rearrange("(t p) d -> p t d", p=P), g.h[:])\
                    .then_inc(s.h_out, 16)

            with sp.Fori(1, NQB // 2) as r:
                load(r * 2, 0)
                load(r * 2 + 1, 1)
            with sp.Fori(0, NQB) as i:
                store(i)
            sp.wait_ge(s.h_out, 16 * NQB)

        @block.scalar
        def _(act):
            nc.scalar.activation(g.warm[:], g.ones[:, 0:1], ACT.Exp)
            act.wait_ge(s.cleared, 1)

            def padded(r, k):
                wait(act, s.x_in[k], r * 16)
                for c in range(DC):
                    nc.scalar.activation(xp[:, c, bass.ds(r * (2 * ROWS8) + (k * ROWS8 + 1), ROWS8), 1:1 + IMG],
                                         g.x_in[:, k, c].rearrange("p (r w) -> p r w", w=IMG), ACT.Identity,
                                         scale=g.bn_s[:, c:c + 1], bias=g.bn_h[:, c:c + 1])
                act.drain().then_inc(s.xn, 1)

            def start(i, k):
                act.wait_ge(s.upper, i + 1)
                wait(act, s.lin, i - 1)
                for c in range(DC):
                    mm = nc.scalar.activation(g.y_t[:, k, c], ps[:, 6 + c], ACT.Identity, bias=g.vecs[:, 4, c:c + 1])
                mm.then_inc(s.started, 1)

            act.sem_inc(s.p_f, 2)
            for k in range(2):
                padded(0, k)
            start(0, 0)
            for k in range(2):
                padded(1, k)
            start(1, 1)
            with act.Fori(2, NQB // 2) as r:
                for k in range(2):
                    padded(r, k)
            act.sem_inc(s.xn, 1)

            def high(i, k):
                act.wait_ge(s.aT, i + 1)
                wait(act, s.proj, i * 6 - 5)
                nc.scalar.activation(g.a_hi[:, k], ps[:, 2:4], ACT.Copy, scale=A_SCALE).then_inc(s.a_hi, 1)

            def project(i):
                for m in range(6):
                    act.wait_ge(s.proj, i * 6 + m + 2)
                    act.wait_ge(s.p_lo, i * 6 + m + 1)
                    bias = g.bqk[:, m // 2, m % 2:m % 2 + 1] if m < 4 else 0.0
                    nc.scalar.activation(g.p_f[:, m % 2], ps[:, 4 + m % 2], ACT.Identity,
                                         scale=g.ratio[:, m // 2:m // 2 + 1], bias=bias)
                    act.drain().then_inc(s.p_f, 1)
                    out, src = projected(m, i, (g.q_hi, g.k_hi, g.v_hi))
                    nc.scalar.activation(out, src, ACT.Copy).then_inc(s.p_hi, 1)

            def one(i, k, stages):
                if "a" in stages and not (isinstance(i, int) and i == 0):
                    start(i + 1, 1 - k)
                if "c" in stages:
                    high(i - 1, 1 - k)
                if "d" in stages:
                    project(i - 2)

            rounds(act, one)

        @block.gpsimd
        def _(pool):
            def root(i):
                pool.wait_ge(s.var, i + 1)
                pool.tensor_tensor(g.rstd[:], g.var[:], g.expo[:, 0:SUB], ALU.pow).then_inc(s.rstd, 1)

            def low(i):
                for m in range(6):
                    pool.wait_ge(s.p_hi, i * 6 + m + 1)
                    out, src = projected(m, i, (g.q_lo, g.k_lo, g.v_lo))
                    hi, _ = projected(m, i, (g.q_hi, g.k_hi, g.v_hi))
                    pool.tensor_tensor(out, src, hi, ALU.subtract).then_inc(s.p_lo, 1)

            def one(i, k, stages):
                last = isinstance(i, int) and i == NQB
                if "c" in stages and not last:
                    root(i - 1)
                if "a" not in stages and "b" in stages:
                    root(i)
                if "d" in stages:
                    low(i - 2)

            pool.sem_inc(s.p_lo, 2)
            rounds(pool, one)

        @block.tensor
        def _(pe):
            def upper(i):
                pe.wait_ge(s.xn, i + 1)
                wait(pe, s.started, i)
                for c in range(DC):
                    for tap in range(UPPER):
                        last = nc.tensor.matmul(ps[:, 6 + c], g.t_diag[:, c, tap], under(c, i, tap),
                                                start=tap == 0, stop=tap == UPPER - 1)
                last.then_inc(s.upper, 1)

            def linear(i, k):
                pe.wait_ge(s.y_t, i + 1)
                wait(pe, s.h_made, i)
                for t in range(SUB):
                    for c in range(DC):
                        last = nc.tensor.matmul(ps[:, t // 2, (t % 2) * D:(t % 2 + 1) * D],
                                                g.y_t[:, k, c, t * P:(t + 1) * P], g.lin_t[:, c],
                                                start=c == 0, stop=c == DC - 1)
                last.then_inc(s.lin, 1)

            def turn(i):
                pe.wait_ge(s.a, i + 1)
                wait(pe, s.a_lo, i)
                for c in range(DC):
                    for t in range(SUB):
                        last = nc.tensor.transpose(ps[:, 2 + c, t * P:(t + 1) * P], g.a[:, t, c * P:(c + 1) * P],
                                                   g.ident[:])
                last.then_inc(s.aT, 1)

            def project(i, k):
                pe.wait_ge(s.a_lo, i + 1)
                for m in range(6):
                    pe.wait_ge(s.p_f, i * 6 + m + 1)
                    w, c, out = m // 2, m % 2, ps[:, 4 + m % 2]
                    for t in range(1 if w < 2 else 2):
                        n = 0
                        for q in range(DC):
                            for x, y in ((g.w_hi, g.a_hi), (g.w_hi, g.a_lo), (g.w_lo, g.a_hi)):
                                if w < 2:
                                    last = nc.tensor.matmul(out, x[:, w, q, c * P:(c + 1) * P], y[:, k, q],
                                                            start=n == 0, stop=n == 5)
                                else:
                                    last = nc.tensor.matmul(out[:, t * D:(t + 1) * D],
                                                            y[:, k, q, (2 * c + t) * P:(2 * c + t + 1) * P], x[:, w, q],
                                                            start=n == 0, stop=n == 5)
                                n += 1
                    last.then_inc(s.proj, 1)

            def one(i, k, stages):
                if "a" in stages:
                    upper(i + 1)
                if "b" in stages:
                    linear(i, k)
                if "c" in stages:
                    turn(i - 1)
                if "d" in stages:
                    project(i - 2, k)

            pe.sem_inc(s.proj, 1)
            upper(0)
            rounds(pe, one)

        @block.vector
        def _(dve):
            for edge in (0, PW - 1):
                nc.vector.memset(xp[:, :, edge, :], 0.0)
                nc.vector.memset(xp[:, :, 1:1 + IMG, edge], 0.0)
            dve.drain().then_inc(s.cleared, 1)
            nc.vector.memset(g.v_hi[:, :, D:VW], 1.0)

            def conv(i, k):
                dve.wait_ge(s.started, i + 1)
                dve.wait_ge(s.xn, i + 2)
                for tap in range(UPPER, 9):
                    for c in range(DC):
                        out = g.y_t[:, k, c].rearrange("p (r w) -> p r w", w=IMG)
                        nc.vector.scalar_tensor_tensor(out=out, in0=under(c, i, tap), scalar=g.taps[:, c, tap:tap + 1],
                                                       in1=out, op0=ALU.mult, op1=ALU.add)
                    if tap < 8:
                        dve.drain()
                dve.drain().then_inc(s.y_t, 1)

            def rows(i):
                dve.wait_ge(s.lin, i + 1)
                wait(dve, s.h_out, i * 16)
                for t in range(SUB):
                    nc.vector.tensor_tensor(g.h[:, t], ps[:, t // 2, (t % 2) * D:(t % 2 + 1) * D], g.lin_b[:], ALU.add)
                dve.drain().then_inc(s.h_made, 1)
                stats(nc, dve, g, g.h, SUB)
                dve.drain().then_inc(s.var, 1)

            def norm(i):
                dve.wait_ge(s.rstd, i + 1)
                wait(dve, s.aT, i)
                for t in range(SUB):
                    nc.vector.tensor_scalar(g.a[:, t], g.h[:, t], g.mv[:, t, 0:1], g.rstd[:, t:t + 1],
                                            ALU.subtract, ALU.mult)
                dve.drain().then_inc(s.a, 1)

            def low(i, k):
                dve.wait_ge(s.a_hi, i + 1)
                nc.vector.scalar_tensor_tensor(out=g.a_lo[:, k], in0=ps[:, 2:4], scalar=A_SCALE, in1=g.a_hi[:, k],
                                               op0=ALU.mult, op1=ALU.subtract)
                dve.drain().then_inc(s.a_lo, 1)

            def one(i, k, stages):
                if "b" in stages:
                    conv(i, k)
                if "c" in stages:
                    rows(i - 1)
                if "d" in stages:
                    low(i - 2, k)
                if "c" in stages:
                    norm(i - 1)

            rounds(dve, one)


def stats(nc, dve, g, x, nt, np_=P):
    for t in range(nt):
        nc.vector.bn_stats(g.st[0:np_, t], x[0:np_, t])
    dve.drain()
    for t in range(nt):
        nc.vector.bn_aggr(g.mv[0:np_, t], g.st[0:np_, t])
    dve.drain()
    nc.vector.tensor_scalar(g.var[0:np_, 0:nt], g.mv[0:np_, 0:nt, 1], EPS, None, ALU.add)


def load_strip(g, a, sp, b, i, k, sem):
    sp.dma_start(g.x_in[:, k], a["xT"][b, :, bass.ds(i * QB, QB)].rearrange("(c p) n -> p c n", p=P)).then_inc(sem, 16)


def class_row(nc, g, a):
    ps = g.ps
    s = Names()
    s.c_in, s.c_x, s.c_step = semaphores(nc, "c_in c_x c_step")
    with nc.Block() as block:
        @block.sync
        def _(sp):
            sp.dma_start(g.h[0:1, 0], a["cls_tok"][0]).then_inc(s.c_in, 16)
            for k in range(2):
                load_strip(g, a, sp, 0, k, k, s.c_x)
            sp.wait_ge(s.c_x, 32)

        @block.gpsimd
        def _(pool):
            pool.wait_ge(s.c_step, 1)
            pool.tensor_tensor(g.rstd[0:1, 0:1], g.var[0:1, 0:1], g.expo[0:1, 0:1], ALU.pow)
            pool.tensor_tensor(g.c_hb[0:1, 0], g.h[0:1, 0], g.bv[0:1], ALU.add)
            pool.drain().then_inc(s.c_step, 1)

        @block.vector
        def _(dve):
            dve.wait_ge(s.c_in, 16)
            stats(nc, dve, g, g.h, 1, 1)
            dve.drain().then_inc(s.c_step, 1)
            dve.wait_ge(s.c_step, 2)
            nc.vector.tensor_scalar(g.a[0:1, 0], g.h[0:1, 0], g.mv[0:1, 0, 0:1], g.rstd[0:1, 0:1],
                                    ALU.subtract, ALU.mult)
            dve.drain().then_inc(s.c_step, 1)
            dve.wait_ge(s.c_step, 5)
            nc.vector.scalar_tensor_tensor(out=g.a_lo[:, 0, :, 0:1], in0=ps[:, 2:4, 0:1], scalar=A_SCALE,
                                           in1=g.a_hi[:, 0, :, 0:1], op0=ALU.mult, op1=ALU.subtract)
            dve.drain().then_inc(s.c_step, 1)
            dve.wait_ge(s.c_step, 8)
            nc.vector.tensor_tensor(g.c_q[:, :, 1], g.p_f[:, 0, 0:2], g.c_q[:, :, 0], ALU.subtract)
            nc.vector.tensor_tensor(g.k_lo[:, :, NP], g.p_f[:, 0, 2:4], g.k_hi[:, :, NP], ALU.subtract)
            nc.vector.tensor_tensor(g.v_lo[0:1, LAST], g.p_f[0:1, 1, 0:D], g.v_hi[0:1, LAST, 0:D], ALU.subtract)
            nc.vector.tensor_tensor(g.c_k[:, :, 1], g.p_f[:, 0, 2:4], g.k_hi[:, :, NP], ALU.subtract)
            nc.vector.tensor_copy(g.c_k[:, :, 0], g.k_hi[:, :, NP])
            dve.wait_ge(s.c_step, 9)
            nc.vector.tensor_scalar(g.c_v[:], ps[:, 6, 0:D], g.isc[:, 5:6], None, ALU.mult)

        @block.scalar
        def _(act):
            act.wait_ge(s.c_step, 4)
            nc.scalar.activation(g.a_hi[:, 0, :, 0:1], ps[:, 2:4, 0:1], ACT.Copy, scale=A_SCALE)
            act.drain().then_inc(s.c_step, 1)
            act.wait_ge(s.c_step, 7)
            for m in range(4):
                nc.scalar.activation(g.p_f[:, 0, m:m + 1], ps[:, 4, m:m + 1], ACT.Identity,
                                     scale=g.ratio[:, m // 2:m // 2 + 1], bias=g.bqk[:, m // 2, m % 2:m % 2 + 1])
            nc.scalar.activation(g.p_f[0:1, 1, 0:D], ps[0:1, 5, 0:D], ACT.Copy, scale=g.ratio[0:1, 2:3])
            act.drain()
            nc.scalar.activation(g.c_q[:, :, 0], g.p_f[:, 0, 0:2], ACT.Copy)
            nc.scalar.activation(g.k_hi[:, :, NP], g.p_f[:, 0, 2:4], ACT.Copy)
            nc.scalar.activation(g.v_hi[0:1, LAST, 0:D], g.p_f[0:1, 1, 0:D], ACT.Copy)
            act.drain().then_inc(s.c_step, 1)

        @block.tensor
        def _(pe):
            pe.wait_ge(s.c_step, 3)
            for c in range(DC):
                nc.tensor.transpose(ps[:, 2 + c, 0:1], g.a[0:1, 0, c * P:(c + 1) * P], g.ident[0:1, 0:1])
            pe.drain().then_inc(s.c_step, 1)
            pe.wait_ge(s.c_step, 6)
            for m in range(4):
                products(nc, ps[:, 4, m:m + 1], [(g.w_hi[:, m // 2, k, m % 2 * P:(m % 2 + 1) * P],
                                                  g.w_lo[:, m // 2, k, m % 2 * P:(m % 2 + 1) * P],
                                                  g.a_hi[:, 0, k, 0:1], g.a_lo[:, 0, k, 0:1]) for k in range(DC)])
            products(nc, ps[0:1, 5, 0:D], [(g.a_hi[:, 0, k, 0:1], g.a_lo[:, 0, k, 0:1],
                                            g.w_hi[:, 2, k], g.w_lo[:, 2, k]) for k in range(DC)])
            pe.drain().then_inc(s.c_step, 1)
            pe.wait_ge(s.c_step, 8)
            nc.tensor.matmul(ps[:, 6, 0:D], g.ones[0:1, :], g.p_f[0:1, 1, 0:D], start=True, stop=True)
            pe.drain().then_inc(s.c_step, 1)



def cls_scores(nc, g, s, pe):
    def score(t, np_, keys):
        out, n = g.ps[0:np_, 7, t * 2:t * 2 + 2], 0
        for c in range(DC):
            for part in (g.k_hi, g.k_lo):
                last = nc.tensor.matmul(out, part[:, c, keys], g.c_q[:, c], start=n == 0, stop=n == 2 * DC - 1)
                n += 1
        return last

    for t in range(LAST):
        score(t, P, slice(t * P, (t + 1) * P))
    score(LAST, 1, slice(NP, N)).then_inc(s.c_qk, 1)


def cls_largest(nc, g, s, dve):
    pair = g.ps[:, 7, 0:2 * KT].rearrange("p (t h) -> p t h", h=2)
    dve.wait_ge(s.c_qk, 1)
    nc.vector.reduce_sum(g.c_s[:, 0:LAST], pair[:, 0:LAST], axis=AX.X)
    nc.vector.reduce_sum(g.c_s[0:1, LAST:KT], pair[0:1, LAST:KT], axis=AX.X)
    dve.drain()
    nc.vector.reduce_max(g.c_m[:], g.c_s[:, 0:LAST], axis=AX.X)
    dve.drain()
    nc.vector.tensor_tensor(g.c_m[0:1], g.c_m[0:1], g.c_s[0:1, LAST:KT], ALU.max)
    dve.drain().then_inc(s.c_maxed, 1)


def cls_turn(nc, g, s, pe):
    pe.wait_ge(s.c_maxed, 1)
    nc.tensor.transpose(g.ps[0:1, 7, P:2 * P], g.c_m[:], g.ident[:]).then_inc(s.c_turned, 1)


def cls_top(nc, g, s, dve):
    dve.wait_ge(s.c_turned, 1)
    nc.vector.reduce_max(g.c_m1[0:1], g.ps[0:1, 7, P:2 * P], axis=AX.X).then_inc(s.c_top, 1)


def cls_spread(nc, g, s, pe):
    pe.wait_ge(s.c_top, 1)
    nc.tensor.matmul(g.ps[:, 7, 2 * P:2 * P + 1], g.ones[0:1, :], g.c_m1[0:1], start=True, stop=True)\
        .then_inc(s.c_spread, 1)


def cls_subtract(nc, g, s, dve):
    dve.wait_ge(s.c_spread, 1)
    nc.vector.tensor_copy(g.c_m[:], g.ps[:, 7, 2 * P:2 * P + 1])
    dve.drain()
    nc.vector.tensor_scalar(g.c_s[:, 0:LAST], g.c_s[:, 0:LAST], g.c_m[:], None, ALU.subtract)
    nc.vector.tensor_scalar(g.c_s[0:1, LAST:KT], g.c_s[0:1, LAST:KT], g.c_m[0:1], None, ALU.subtract)
    dve.drain().then_inc(s.c_sub, 1)


def cls_weights(nc, g, s, act):
    act.wait_ge(s.c_sub, 1)
    nc.scalar.activation(g.c_s[:, 0:LAST], g.c_s[:, 0:LAST], ACT.Exp, scale=g.score[:])
    nc.scalar.activation(g.c_s[0:1, LAST:KT], g.c_s[0:1, LAST:KT], ACT.Exp, scale=g.score[0:1])
    act.drain()
    nc.scalar.activation(g.c_hi[:, 0:LAST], g.c_s[:, 0:LAST], ACT.Copy, scale=P_SCALE)
    nc.scalar.activation(g.c_hi[0:1, LAST:KT], g.c_s[0:1, LAST:KT], ACT.Copy, scale=P_SCALE)
    act.drain().then_inc(s.c_high, 1)


def cls_low(nc, g, s, dve):
    dve.wait_ge(s.c_high, 1)
    nc.vector.scalar_tensor_tensor(out=g.c_lo[:, 0:LAST], in0=g.c_s[:, 0:LAST], scalar=P_SCALE,
                                   in1=g.c_hi[:, 0:LAST], op0=ALU.mult, op1=ALU.subtract)
    nc.vector.scalar_tensor_tensor(out=g.c_lo[0:1, LAST:KT], in0=g.c_s[0:1, LAST:KT], scalar=P_SCALE,
                                   in1=g.c_hi[0:1, LAST:KT], op0=ALU.mult, op1=ALU.subtract)
    dve.drain().then_inc(s.c_low, 1)


def cls_values(nc, g, s, pe):
    def value(t, np_, first, last):
        at = slice(t, t + 1)
        v, vl = g.v_hi[0:np_, t, :], g.v_lo[0:np_, t, :]
        nc.tensor.matmul(g.ps[0:1, 0, 0:VW], g.c_hi[0:np_, at], v, start=first, stop=False)
        nc.tensor.matmul(g.ps[0:1, 0, 0:D], g.c_hi[0:np_, at], vl, start=False, stop=False)
        return nc.tensor.matmul(g.ps[0:1, 0, 0:VW], g.c_lo[0:np_, at], v, start=False, stop=last)

    pe.wait_ge(s.c_low, 1)
    value(0, P, True, False)
    for t in range(1, LAST):
        value(t, P, False, False)
    value(LAST, 1, False, True).then_inc(s.c_pv, 1)


def products(nc, out, parts, start=True, stop=True):
    for i, (x_hi, x_lo, y_hi, y_lo) in enumerate(parts):
        nc.tensor.matmul(out, x_hi, y_hi, start=start and i == 0, stop=False)
        nc.tensor.matmul(out, x_hi, y_lo, start=False, stop=False)
        last = nc.tensor.matmul(out, x_lo, y_hi, start=False, stop=stop and i == len(parts) - 1)
    return last



def ep_evacuate(nc, g, s, dve, n, np_, nt):
    wait(dve, s.o_out, n * 16)
    wait(dve, s.r_out, n * 16)
    wait(dve, s.hb, n)
    hb = g.hb if np_ == P else g.c_hb
    if np_ == P:
        nc.vector.scalar_tensor_tensor(out=g.rs[:], in0=g.ck_w[:], scalar=P_SCALE, in1=g.ps[:, 0:nt, D],
                                       op0=ALU.mult, op1=ALU.add)
        dve.drain()
        nc.vector.reciprocal(g.rs[:], g.rs[:])
        dve.drain()
        nc.vector.scalar_tensor_tensor(out=g.ck_c[:], in0=g.rs[:], scalar=P_SCALE, in1=g.ck_w[:],
                                       op0=ALU.mult, op1=ALU.mult)
    else:
        nc.vector.reciprocal(g.rs[0:np_, 0:nt], g.ps[0:np_, 0:nt, D])
    dve.drain()
    nc.vector.tensor_scalar(g.rs[0:np_, 0:nt], g.rs[0:np_, 0:nt], g.isc[0:np_, 5:6], None, ALU.mult)
    dve.drain()
    for t in range(nt):
        nc.vector.scalar_tensor_tensor(out=g.row[0:np_, t, D:2 * D], in0=g.ps[0:np_, t, 0:D],
                                       scalar=g.rs[0:np_, t:t + 1], in1=hb[0:np_, t], op0=ALU.mult, op1=ALU.add)
    dve.drain().then_inc(s.freed, 1)


def ep_class_value(nc, g, s, dve, n, np_, nt):
    if np_ == P:
        for t in range(nt):
            nc.vector.scalar_tensor_tensor(out=g.row[:, t, D:2 * D], in0=g.c_v[:], scalar=g.ck_c[:, t:t + 1],
                                           in1=g.row[:, t, D:2 * D], op0=ALU.mult, op1=ALU.add)
    dve.drain().then_inc(s.o, 1)


def ep_stats(nc, g, s, dve, n, np_, nt):
    stats(nc, dve, g, g.row[:, :, D:2 * D], nt, np_)
    dve.drain().then_inc(s.var2, 1)


def ep_pool_root(nc, g, s, pool, n, np_, nt):
    pool.wait_ge(s.var2, n + 1)
    pool.tensor_tensor(g.rstd[0:np_, 0:nt], g.var[0:np_, 0:nt], g.expo[0:np_, 0:nt], ALU.pow).then_inc(s.rstd2, 1)


def ep_norm(nc, g, s, dve, n, np_, nt):
    dve.wait_ge(s.rstd2, n + 1)
    for t in range(nt):
        nc.vector.tensor_scalar(g.row[0:np_, t, 0:D], g.row[0:np_, t, D:2 * D], g.mv[0:np_, t, 0:1],
                                g.rstd[0:np_, t:t + 1], ALU.subtract, ALU.mult)
    dve.drain().then_inc(s.z, 1)


def ep_turn(nc, g, s, pe, n, c, np_, nt):
    pe.wait_ge(s.z, n + 1)
    if c:
        pe.wait_ge(s.z_t, n * DC + c)
    for t in range(nt):
        last = nc.tensor.transpose(g.ps[:, 7, t * P:t * P + np_], g.row[0:np_, t, c * P:(c + 1) * P],
                                   g.ident[0:np_, 0:np_])
    last.then_inc(s.zT, 1)


def ep_columns(nc, g, s, act, n, c, np_, nt):
    act.wait_ge(s.zT, n * DC + c + 1)
    src = g.ps[:, 7, 0:nt * P] if np_ == P else g.ps[:, 7, 0:np_]
    nc.scalar.activation(g.z_t[:, c, 0:nt * P] if np_ == P else g.z_t[:, c, 0:np_], src, ACT.Copy).then_inc(s.z_t, 1)


def ep_logits(nc, g, s, pe, n, np_, nt):
    pe.wait_ge(s.z_t, n * DC + DC)
    for t in range(nt):
        for c in range(DC):
            last = nc.tensor.matmul(g.ps[0:np_, 7, t * E:(t + 1) * E], g.z_t[:, c, t * P:t * P + np_], g.gate_w[:, c],
                                    start=c == 0, stop=c == DC - 1)
    last.then_inc(s.logits, 1)


def ep_exp(nc, g, s, act, n, np_, nt):
    act.wait_ge(s.l_sub, n + 1)
    nc.scalar.activation(g.r_e[0:np_, 0:nt], g.r_l[0:np_, 0:nt], ACT.Exp).then_inc(s.l_exp, 1)


def ep_route(nc, g, s, dve, n, np_, nt):
    v = nc.vector
    l, e, key, oh = (x[0:np_, 0:nt] for x in (g.r_l, g.r_e, g.r_k, g.r_oh))
    m, d, k = (x[0:np_, 0:nt] for x in (g.r_m, g.r_d, g.r_x))
    wide = lambda x: x.unsqueeze(2).to_broadcast((np_, nt, E))
    dve.wait_ge(s.logits, n + 1)
    v.tensor_tensor(l, g.ps[0:np_, 7, 0:nt * E].rearrange("p (t e) -> p t e", e=E),
                    g.gate_b[0:np_].unsqueeze(1).to_broadcast((np_, nt, E)), ALU.add)
    dve.drain()
    v.reduce_max(m, l, axis=AX.X)
    dve.drain()
    v.tensor_tensor(l, l, wide(m), ALU.subtract)
    dve.drain().then_inc(s.l_sub, 1)
    dve.wait_ge(s.l_exp, n + 1)
    v.reduce_max(m, e, axis=AX.X)
    v.reduce_sum(d, e, axis=AX.X)
    dve.drain()
    v.reciprocal(d, d)
    v.tensor_tensor(key, e, wide(m), ALU.is_equal)
    dve.drain()
    v.tensor_tensor(g.row[0:np_, 0:nt, 2 * D], m, d, ALU.mult)
    v.tensor_tensor(key, key, g.weight[0:np_, 0:nt], ALU.mult)
    dve.drain()
    v.reduce_max(k, key, axis=AX.X)
    dve.drain()
    v.tensor_tensor(oh, key, wide(k), ALU.is_equal)
    dve.drain().then_inc(s.routed, 1)


def ep_prefix(nc, g, s, pe, n, np_, nt):
    pe.wait_ge(s.routed, n + 1)
    for t in range(nt):
        out = g.ps[0:np_, 7, 64 + t * E:64 + (t + 1) * E]
        for u in range(t):
            nc.tensor.matmul(out, g.ones16[0:np_, 0:np_], g.r_oh[0:np_, u], start=u == 0, stop=False)
        nc.tensor.matmul(out, g.upper[0:np_, 0:np_], g.r_oh[0:np_, t], start=t == 0, stop=True)
    for t in range(nt):
        last = nc.tensor.matmul(g.ps[:, 7, 128:128 + E], g.ones16[0:np_, :], g.r_oh[0:np_, t], start=t == 0,
                                stop=t == nt - 1)
    last.then_inc(s.prefix, 1)


def ep_slots(nc, g, s, dve, n, np_, nt):
    v = nc.vector
    c, d = g.r_l[0:np_, 0:nt], g.r_e[0:np_, 0:nt]
    dve.wait_ge(s.prefix, n + 1)
    if isinstance(n, int) and n == 0:
        v.memset(g.idx_f[:], BIG)
        dve.drain()
    else:
        dve.wait_ge(s.tab, s.tab0 + (n - 1) * 16 * SUB + 16)
    v.tensor_tensor(c, g.ps[0:np_, 7, 64:64 + nt * E].rearrange("p (t e) -> p t e", e=E),
                    g.carry[0:np_].unsqueeze(1).to_broadcast((np_, nt, E)), ALU.add)
    dve.drain()
    v.tensor_tensor(g.carry[:], g.ps[:, 7, 128:128 + E], g.carry[:], ALU.add)
    v.tensor_scalar(d, c, float(CAP), BIG, ALU.is_gt, ALU.mult)
    dve.drain()
    v.tensor_tensor(c, c, g.slot0[0:np_, 0:nt], ALU.add)
    dve.drain()
    v.tensor_tensor(c, c, d, ALU.add)
    dve.drain()
    v.tensor_tensor(c, c, g.r_oh[0:np_, 0:nt], ALU.mult)
    dve.drain()
    v.reduce_sum(g.idx_f[0:np_, 0:nt], c, axis=AX.X)
    v.tensor_copy(g.tok_i[:], g.tok_f[:])
    dve.drain()
    v.tensor_copy(g.idx_i[:], g.idx_f[:])
    v.tensor_scalar(g.tok_f[:], g.tok_f[:], float(QB if np_ == P else 1), None, ALU.add)
    dve.drain().then_inc(s.slots, 1)


def ep_pool_table(nc, g, s, pool, n, nt):
    pool.wait_ge(s.slots, n + 1)
    settle(g, pool)
    for t in range(nt):
        pool.indirect_dma_start(out=g.table[:, :], out_offset=bass.IndirectOffsetOnAxis(ap=g.idx_i[:, t:t + 1], axis=0),
                                in_=g.tok_i[:, t:t + 1], in_offset=None, bounds_check=E * STRIDE - 1,
                                oob_is_err=False).then_inc(s.tab, 16)


def attention(nc, g, a, b, s):
    ps = g.ps

    def keys_loop(engine, body, steps):
        cuts = sorted({0, 1, 10} | set(steps))
        for lo, hi in zip(cuts, cuts[1:] + [11]):
            if lo in steps:
                steps[lo]()
            if hi - lo == 1:
                for k in range(min(3, NT - 3 * lo)):
                    body(3 * lo + k, k)
            else:
                with engine.Fori(lo, hi) as r:
                    for k in range(3):
                        body(r * 3 + k, k)

    def before(i, t):
        return i - 1 if isinstance(t, int) and t < 2 else i - 2

    def rounds(engine, one):
        one(0, True, False, None)
        one(1, True, True, 0)
        with engine.Fori(2, NQB) as j:
            one(j, True, True, j - 1)
        one(NQB, False, True, NQB - 1)
        one(NQB + 1, False, False, NQB)

    def size(n):
        return (1, 1) if isinstance(n, int) and n == 0 else (P, SUB)

    with nc.Block() as block:
        @block.sync
        def _(sp):
            def rows(n):
                return bass.ds((n - 1) * QB + 1, QB)

            def load(n):
                sp.wait_ge(s.o, n)
                sp.dma_start(g.hb[:], g.h_res[b, bass.ds((n - 1) * QB, QB), :].rearrange("(t p) d -> p t d", p=P))\
                    .then_inc(s.h_in, 16)

            def store(n):
                sp.wait_ge(s.o, n + 1)
                sp.dma_start(a["out"][b, rows(n), :].rearrange("(t p) d -> p t d", p=P), g.row[:, :, D:2 * D])\
                    .then_inc(s.o_out, 16)
                sp.wait_ge(s.routed, n + 1)
                sp.dma_start(g.rows[bass.ds(b * N + (n - 1) * QB + 1, QB), :].rearrange("(t p) d -> p t d", p=P),
                             g.row[:]).then_inc(s.r_out, 16)

            load(1)
            sp.dma_start(a["out"][b, 0:1, :], g.row[0:1, 0, D:2 * D]).then_inc(s.o_out, 16)
            sp.wait_ge(s.routed, 1)
            sp.dma_start(g.rows[bass.ds(b * N, 1), :], g.row[0:1, 0]).then_inc(s.r_out, 16)
            with sp.Fori(2, NQB + 1) as n:
                load(n)
                store(n - 1)
            sp.wait_ge(s.pv, NQB * NT)
            expert_weights(nc, g, a, sp, 0, s.early)
            for k in range(2):
                load_strip(g, a, sp, (b + 1) % B, k, k, s.early)
            store(NQB)
            sp.wait_ge(s.early, 64)
            sp.wait_ge(s.o_out, 16 * (NQB + 1))
            sp.wait_ge(s.r_out, 16 * (NQB + 1))

        @block.gpsimd
        def _(pool):
            def subtract(j, t):
                x = g.panel[:, t]
                pool.tensor_tensor(x, x, g.m[:], ALU.subtract).then_inc(s.sub, 1)

            def one(j, scores, values, n):
                def bias(m):
                    pool.wait_ge(s.h_in, m * 16)
                    for t in range(SUB):
                        pool.tensor_tensor(g.hb[:, t], g.hb[:, t], g.bv[:], ALU.add)
                    pool.drain().then_inc(s.hb, 1)

                if not values:
                    if n is not None:
                        ep_pool_root(nc, g, s, pool, n, *size(n))
                        ep_pool_table(nc, g, s, pool, n, size(n)[1])
                    return
                pool.wait_ge(s.m, j)
                settle(g, pool)
                body = lambda t, k: subtract(j, t)
                keys_loop(pool, body, {2: lambda: ep_pool_root(nc, g, s, pool, n, *size(n)), 7: lambda: bias(n + 1)})
                ep_pool_table(nc, g, s, pool, n, size(n)[1])

            rounds(pool, one)
            pool.wait_ge(s.tab, s.tab0 + 16 * (SUB * NQB + 1))
            settle(g, pool)

        @block.scalar
        def _(act):
            nc.scalar.activation(g.warm[:], g.ones[:, 0:1], ACT.Exp)

            def weights(j, t, k):
                i = (j - 1) * NT + t
                act.wait_ge(s.sub, i + 1)
                x = g.panel[:, t]
                nc.scalar.activation(x, x, ACT.Exp, scale=g.score[:])
                act.drain()
                if not (isinstance(i, int) and i <= 2):
                    act.wait_ge(s.pv, before(i, t))
                    settle(g, act)
                nc.scalar.activation(g.ph[:, k], x, ACT.Copy, scale=P_SCALE).then_inc(s.p_hi2, 1)

            def keep(j, t, k):
                act.wait_ge(s.qk, j * NT + t + 1)
                if not (isinstance(j, int) and j == 0):
                    act.wait_ge(s.p_lo2, (j - 1) * NT + t + 1)
                settle(g, act)
                nc.scalar.activation(g.panel[:, t], ps[:, 4 + k], ACT.Copy).then_inc(s.kept, 1)

            def one(j, scores, values, n):
                if values:
                    weights(j, 0, 0)

                def body(t, k):
                    if values and not (isinstance(t, int) and t == NT - 1):
                        weights(j, t + 1, (k + 1) % 3)
                    if scores:
                        keep(j, t, k)

                if n is None:
                    steps = {5: lambda: cls_weights(nc, g, s, act)}
                else:
                    steps = {4: lambda: ep_columns(nc, g, s, act, n, 0, *size(n)),
                             6: lambda: ep_columns(nc, g, s, act, n, 1, *size(n)),
                             8: lambda: ep_exp(nc, g, s, act, n, *size(n))}
                if scores or values:
                    keys_loop(act, body, steps)
                else:
                    for step in steps.values():
                        step()
                if scores:
                    act.wait_ge(s.m_ps, j + 1)
                    nc.scalar.activation(g.m[:], ps[:, 7], ACT.Copy).then_inc(s.m, 1)
                    act.wait_ge(s.ck_sub, j + 1)
                    nc.scalar.activation(g.ck_new[:], g.ck_d[:], ACT.Exp, scale=g.score[:]).then_inc(s.ck_exp, 1)

            rounds(act, one)

        @block.vector
        def _(dve):
            def low(j, t, k):
                dve.wait_ge(s.p_hi2, (j - 1) * NT + t + 1)
                nc.vector.scalar_tensor_tensor(out=g.pl[:, k], in0=g.panel[:, t], scalar=P_SCALE, in1=g.ph[:, k],
                                               op0=ALU.mult, op1=ALU.subtract).then_inc(s.p_lo2, 1)

            def largest(j, t):
                dve.wait_ge(s.kept, j * NT + t + 1)
                nc.vector.tensor_tensor(g.r[:], g.r[:], g.panel[:, t], ALU.max)
                dve.drain().then_inc(s.maxed, 1)

            def one(j, scores, values, n):
                if n is None:
                    cls_largest(nc, g, s, dve)
                elif isinstance(n, int) and n == 0:
                    dve.wait_ge(s.c_pv, 1)
                else:
                    dve.wait_ge(s.pv, n * NT)
                if n is not None:
                    ep_evacuate(nc, g, s, dve, n, *size(n))
                if values:
                    low(j, 0, 0)
                    dve.wait_ge(s.ck_exp, j)
                    nc.vector.tensor_copy(g.ck_w[:], g.ck_new[:])
                if scores:
                    wait(dve, s.r_t, j)
                    nc.vector.memset(g.r[:], -3.0e38)
                    dve.drain()

                def body(t, k):
                    if values and not (isinstance(t, int) and t == NT - 1):
                        low(j, t + 1, (k + 1) % 3)
                    if scores:
                        largest(j, t)

                if n is None:
                    steps = {1: lambda: cls_top(nc, g, s, dve), 4: lambda: cls_subtract(nc, g, s, dve),
                             6: lambda: cls_low(nc, g, s, dve)}
                else:
                    steps = {1: lambda: (ep_class_value(nc, g, s, dve, n, *size(n)),
                                         ep_stats(nc, g, s, dve, n, *size(n))),
                             2: lambda: ep_norm(nc, g, s, dve, n, *size(n)),
                             8: lambda: ep_route(nc, g, s, dve, n, *size(n)),
                             10: lambda: ep_slots(nc, g, s, dve, n, *size(n))}
                if scores or values:
                    keys_loop(dve, body, steps)
                else:
                    for step in steps.values():
                        step()
                if scores:
                    dve.wait_ge(s.ck_made, j + 1)
                    nc.vector.reduce_sum(g.ck_s[:], ps[:, 7, KEYED:KEYED + 2 * SUB].rearrange("p (u h) -> p u h", h=2),
                                         axis=AX.X)
                    dve.drain().then_inc(s.ck_read, 1)
                    dve.wait_ge(s.r_t, j + 1)
                    nc.vector.reduce_max(g.mq[:], ps[:, 7].rearrange("p (t q) -> p t q", q=P), axis=AX.X)
                    dve.drain()
                    nc.vector.tensor_tensor(g.mq[:], g.mq[:], g.ck_s[:], ALU.max)
                    dve.drain()
                    for t in range(SUB):
                        nc.vector.tensor_scalar(g.diag[:, t * P:(t + 1) * P], g.ident[:], g.mq[:, t:t + 1], None,
                                                ALU.mult)
                    dve.drain().then_inc(s.diag, 1)
                    nc.vector.tensor_tensor(g.ck_d[:], g.ck_s[:], g.mq[:], ALU.subtract).then_inc(s.ck_sub, 1)

            rounds(dve, one)

        @block.tensor
        def _(pe):
            def score(j, t, k):
                i = j * NT + t
                queries, keys = bass.ds(j * QB, QB), bass.ds(t * P, P)
                wait(pe, s.kept, before(i, t))
                products(nc, ps[:, 4 + k], [(g.k_hi[:, c, keys], g.k_lo[:, c, keys], g.q_hi[:, c, queries],
                                             g.q_lo[:, c, queries]) for c in range(DC)]).then_inc(s.qk, 1)

            def class_key(j):
                for u in range(SUB):
                    out, m = ps[:, 7, KEYED + 2 * u:KEYED + 2 * u + 2], 0
                    for c in range(DC):
                        for part in (g.q_hi, g.q_lo):
                            mm = nc.tensor.matmul(out, part[:, c, bass.ds(j * QB + u * P, P)], g.c_k[:, c],
                                                  start=m == 0, stop=m == 2 * DC - 1)
                            m += 1
                mm.then_inc(s.ck_made, 1)

            def value(j, t, k):
                i = (j - 1) * NT + t
                first, last = isinstance(t, int) and t == 0, isinstance(t, int) and t == NT - 1
                pe.wait_ge(s.p_lo2, i + 1)
                if first:
                    pe.wait_ge(s.freed, j)
                v, vl = g.v_hi[:, t], g.v_lo[:, t]
                for u in range(SUB):
                    q = slice(u * P, (u + 1) * P)
                    nc.tensor.matmul(ps[:, u, 0:VW], g.ph[:, k, q], v, start=first, stop=False)
                    nc.tensor.matmul(ps[:, u, 0:D], g.ph[:, k, q], vl, start=False, stop=False)
                    mm = nc.tensor.matmul(ps[:, u, 0:VW], g.pl[:, k, q], v, start=False, stop=last)
                mm.then_inc(s.pv, 1)

            def one(j, scores, values, n, next_scores):
                def body(t, k):
                    if values:
                        value(j, t, k)
                    if scores and not (isinstance(t, int) and t + 3 >= NT):
                        score(j, t + 3, k)
                    if scores and isinstance(t, int) and t == NT - 2:
                        pe.wait_ge(s.maxed, (j + 1) * NT)
                        pe.wait_ge(s.ck_read, j + 1)
                        if n is not None:
                            pe.wait_ge(s.slots, n + 1)
                        for u in range(SUB):
                            mm = nc.tensor.transpose(ps[:, 7, u * P:(u + 1) * P], g.r[:, u * P:(u + 1) * P],
                                                     g.ident[:])
                        mm.then_inc(s.r_t, 1)

                if n is None:
                    cls_scores(nc, g, s, pe)
                    for k in range(3):
                        score(j, k, k)
                    steps = {1: lambda: cls_turn(nc, g, s, pe), 3: lambda: cls_spread(nc, g, s, pe),
                             7: lambda: cls_values(nc, g, s, pe), 9: lambda: class_key(j)}
                else:
                    steps = {3: lambda: ep_turn(nc, g, s, pe, n, 0, *size(n)),
                             5: lambda: ep_turn(nc, g, s, pe, n, 1, *size(n)),
                             7: lambda: ep_logits(nc, g, s, pe, n, *size(n)),
                             9: lambda: route_end()}

                def route_end():
                    pe.wait_ge(s.routed, n + 1)
                    if scores:
                        class_key(j)
                    ep_prefix(nc, g, s, pe, n, *size(n))

                if scores or values:
                    keys_loop(pe, body, steps)
                else:
                    for step in steps.values():
                        step()
                if next_scores:
                    score(j + 1, 0, 0)
                if scores:
                    pe.wait_ge(s.diag, j + 1)
                    nc.tensor.matmul(ps[:, 7], g.ones[:], g.diag[:], start=True, stop=True).then_inc(s.m_ps, 1)
                if next_scores:
                    score(j + 1, 1, 1)
                    score(j + 1, 2, 2)

            one(0, True, False, None, True)
            one(1, True, True, 0, True)
            with pe.Fori(2, NQB - 1) as j:
                one(j, True, True, j - 1, True)
            one(NQB - 1, True, True, NQB - 2, False)
            one(NQB, False, True, NQB - 1, False)
            one(NQB + 1, False, False, NQB, False)


FIRST = CAP // P // 3 * P
GROUPS = ((0, FIRST), (FIRST, QB), (FIRST + QB, CAP - FIRST - QB))
assert GROUPS[-1][1] <= QB
NG = len(GROUPS)
PAIR = 2
TILES = tuple(-(-w // P) for _, w in GROUPS)
PG = PAIR * NG
ROUNDS = E // PAIR


def expert_weights(nc, g, a, sp, e, sem):
    sp.dma_start(g.w1_raw[:], a["L0_ffn_w1"][e].rearrange("(c p) f -> p c f", p=P)).then_inc(sem, 16)
    sp.dma_start(g.w2_raw[:], a["L0_ffn_w2"][e].rearrange("(c p) d -> p c d", p=P)).then_inc(sem, 16)


def expert_biases(nc, g, a, sp, e, half, sem):
    with nc.allow_non_contiguous_dma(reason="a bias onto the partitions"):
        sp.dma_start(g.b1[:, half], a["L0_ffn_b1"][e].rearrange("(c p) -> p c", p=P)).then_inc(sem, 16)
    sp.dma_start(g.b2[:, half], a["L0_ffn_b2"][e].rearrange("(a n) -> a n", a=1).to_broadcast((P, D)))\
        .then_inc(sem, 16)


def expert_largest(nc, g, dve, half, which):
    if which == 0:
        nc.vector.tensor_reduce(g.f_mx[:, half, 0:1], g.w1_raw[:], axis=AX.XY, op=ALU.max, apply_absolute_value=True)
    else:
        nc.vector.tensor_reduce(g.f_mx[:, half, 1:2], g.w2_raw[:], axis=AX.XY, op=ALU.max, apply_absolute_value=True)
        nc.vector.tensor_reduce(g.f_mx[:, half, 2:3], g.b1[:, half], axis=AX.X, op=ALU.max, apply_absolute_value=True)


def expert_scales(nc, g, dve, half):
    v, m = nc.vector, g.f_mx[:, half]
    sc, isc = g.f_sc[:, half], g.f_isc[:, half]
    v.scalar_tensor_tensor(out=m[:, 2:3], in0=m[:, 0:1], scalar=float(D), in1=m[:, 2:3], op0=ALU.mult, op1=ALU.add)
    dve.drain()
    scale_of(nc, dve, sc, isc, m)
    v.tensor_tensor(g.f_in[:, half], sc[:, 2:3], isc[:, 0:1], ALU.mult)
    v.tensor_tensor(g.f_out[:, half], isc[:, 2:3], isc[:, 1:2], ALU.mult)
    v.tensor_scalar(g.b1[:, half], g.b1[:, half], sc[:, 2:3], None, ALU.mult)
    dve.drain()
    v.tensor_scalar(g.f_in[:, half], g.f_in[:, half], 1.0 / A_SCALE, None, ALU.mult)


def expert_high(nc, g, half, which):
    raw, hi = ((g.w1_raw, g.w1_hi), (g.w2_raw, g.w2_hi))[which]
    return nc.scalar.activation(hi[:, half], raw[:], ACT.Copy, scale=g.f_sc[:, half, which:which + 1])


def expert_low(nc, g, half, which):
    raw, hi, lo = ((g.w1_raw, g.w1_hi, g.w1_lo), (g.w2_raw, g.w2_hi, g.w2_lo))[which]
    return nc.vector.scalar_tensor_tensor(out=lo[:, half], in0=raw[:], scalar=g.f_sc[:, half, which:which + 1],
                                          in1=hi[:, half], op0=ALU.mult, op1=ALU.subtract)


def token_numbers(nc, g, sp, ep, i, sem):
    at = ep * (PAIR * STRIDE) + (i // NG * STRIDE + GROUPS[i % NG][0])
    tiles = TILES[i % NG]
    with nc.allow_non_contiguous_dma(reason="token numbers onto the partitions"):
        sp.dma_start(g.ids[:, i, 0:tiles], g.table[bass.ds(at, tiles * P), 0].rearrange("(t p) -> p t", p=P))\
            .then_inc(sem, 16)


def gather_rows(g, pool, i, sem):
    for t in range(TILES[i % NG]):
        pool.indirect_dma_start(out=g.tok[:, i % 3, t], out_offset=None, in_=g.rows[:, :],
                                in_offset=bass.IndirectOffsetOnAxis(ap=g.ids[:, i, t:t + 1], axis=0))\
            .then_inc(sem, 16)


def first_expert(nc, g, a, f):
    s = Names()
    s.f0_in, s.f0_max, s.f0_red, s.f0_sc, s.f0_hi = semaphores(nc, "f0_in f0_max f0_red f0_sc f0_hi")
    with nc.Block() as block:
        @block.sync
        def _(sp):
            token_numbers(nc, g, sp, 0, 0, f.ids[0])
            expert_biases(nc, g, a, sp, 0, 0, s.f0_in)
            for i in range(1, PG):
                token_numbers(nc, g, sp, 0, i, f.ids[i])

        @block.vector
        def _(dve):
            expert_largest(nc, g, dve, 0, 0)
            dve.wait_ge(s.f0_in, 32)
            expert_largest(nc, g, dve, 0, 1)
            dve.drain().then_inc(s.f0_max, 1)
            nc.vector.memset(g.y[:], 0.0)
            dve.wait_ge(s.f0_red, 1)
            expert_scales(nc, g, dve, 0)
            dve.drain().then_inc(s.f0_sc, 1)
            for which in range(2):
                dve.wait_ge(s.f0_hi, which + 1)
                expert_low(nc, g, 0, which)

        @block.gpsimd
        def _(pool):
            pool.wait_ge(f.ids[0], 16)
            gather_rows(g, pool, 0, f.got[0])
            pool.wait_ge(s.f0_max, 1)
            pool.partition_all_reduce(g.f_mx[:, 0], g.f_mx[:, 0], P, bass.bass_isa.ReduceOp.max).then_inc(s.f0_red, 1)
            for i in (1, 2):
                pool.wait_ge(f.ids[i], 16)
                gather_rows(g, pool, i, f.got[i])

        @block.scalar
        def _(act):
            act.wait_ge(s.f0_sc, 1)
            for which in range(2):
                expert_high(nc, g, 0, which).then_inc(s.f0_hi, 1)


def experts(nc, g, a, s):
    ps = g.ps
    out = a["out"].rearrange("b n d -> (b n) d")

    def width(i):
        return GROUPS[i % NG][1]

    def tiles(i):
        return TILES[i % NG]

    def rows_of(i, t):
        return min(P, width(i) - t * P)

    def later(ep, i, by):
        i += by
        if i >= PG:
            ep, i = ep + i // PG, i % PG
        return None if isinstance(ep, int) and ep >= ROUNDS else (ep, i)

    def count(ep, i):
        return ep * PG + i

    def got(ep, i):
        return (ep * PAIR + (i // NG + 1)) * (16 * tiles(i))

    def put(ep, i):
        whole, part = (sum(tiles(n) for n in range(i % 2, end, 2)) for end in (PG, i + 1))
        return ep * (16 * whole) + 16 * part

    def prepared(ep, i):
        q = ep * PAIR + i // NG
        return None if isinstance(q, int) and q == E - 1 else q

    def rounds(engine, group):
        group(0, 0)
        with engine.Fori(0, ROUNDS - 1) as ep:
            for i in range(1, PG):
                group(ep, i)
            group(ep + 1, 0)
        for i in range(1, PG):
            group(ROUNDS - 1, i)

    with nc.Block() as block:
        @block.sync
        def _(sp):
            expert_weights(nc, g, a, sp, 1, s.f_w)
            expert_biases(nc, g, a, sp, 1, 1, s.f_w)
            with sp.Fori(0, ROUNDS - 1) as ep:
                for i in range(PG):
                    if i % NG == NG - 1:
                        sp.wait_ge(s.w_low, (ep * PAIR + (i // NG + 1)) * 2)
                        settle(g, sp)
                        expert_weights(nc, g, a, sp, ep * PAIR + (i // NG + 2), s.f_w)
                        sp.wait_ge(s.y_made, count(ep, i) + 1)
                        settle(g, sp)
                        expert_biases(nc, g, a, sp, ep * PAIR + (i // NG + 2), i // NG, s.f_w)
                    sp.wait_ge(s.put[i % 2], put(ep, i))
                    settle(g, sp)
                    token_numbers(nc, g, sp, ep + 1, i, s.ids[i])

        @block.gpsimd
        def _(pool):
            def gather(ep, i):
                pool.wait_ge(s.ids[i], ep * 16 + 16)
                settle(g, pool)
                gather_rows(g, pool, i, s.got[i % 3])

            def scatter(ep, i):
                for t in range(tiles(i)):
                    pool.indirect_dma_start(out=out, out_offset=bass.IndirectOffsetOnAxis(ap=g.ids[:, i, t:t + 1],
                                                                                          axis=0),
                                            in_=g.res[:, i % 2, t], in_offset=None, bounds_check=T - 1,
                                            oob_is_err=False).then_inc(s.put[i % 2], 16)

            def low(q, half, which):
                pool.wait_ge(s.w_high, q * 2 + which + 1)
                settle(g, pool)
                raw, hi, lo = ((g.w1_raw, g.w1_hi, g.w1_lo), (g.w2_raw, g.w2_hi, g.w2_lo))[which]
                pool.tensor_tensor(lo[:, half], raw[:], hi[:, half], ALU.subtract).then_inc(s.w_low, 1)

            def group(ep, i):
                q = prepared(ep, i)
                half = i // NG
                prepare = i % NG == 1 and q is not None
                if prepare:
                    pool.wait_ge(s.w_max, q + 1)
                    settle(g, pool)
                    pool.partition_all_reduce(g.f_mx[:, 1 - half], g.f_mx[:, 1 - half], P,
                                              bass.bass_isa.ReduceOp.max).then_inc(s.w_red, 1)
                if not (isinstance(ep, int) and ep == 0 and i == 0):
                    before = (ep, i - 1) if i else (ep - 1, PG - 1)
                    pool.wait_ge(s.y_done, count(*before) + 1)
                    settle(g, pool)
                    if later(ep, i, 2):
                        gather(*later(ep, i, 2))
                    if prepare:
                        low(q, 1 - half, 0)
                    scatter(*before)
                    if prepare:
                        low(q, 1 - half, 1)

            rounds(pool, group)
            pool.wait_ge(s.y_done, ROUNDS * PG)
            scatter(ROUNDS - 1, PG - 1)
            for i in (PG - 2, PG - 1):
                pool.wait_ge(s.put[i % 2], put(ROUNDS - 1, i))

        @block.scalar
        def _(act):
            nc.scalar.activation(g.warm[:], g.ones[:, 0:1], ACT.Exp)

            def high(ep, i, c):
                act.wait_ge(s.turned, count(ep, i) * DC + (c + 1))
                w = tiles(i) * P
                nc.scalar.activation(g.x_hi[:, i % 2, c, 0:w], ps[:, 7, 0:w], ACT.Copy, scale=A_SCALE)\
                    .then_inc(s.x_high, 1)

            def group(ep, i):
                w, half = width(i), i // NG
                for f in range(FC):
                    n = count(ep, i) * FC + f
                    bank, k = (i * FC + f) % 3, (i * FC + f) % 3
                    if f in (4, 6) and later(ep, i, 1):
                        high(*later(ep, i, 1), f // 2 - 2)
                    act.wait_ge(s.l1, n + 1)
                    wait(act, s.h_low, n - 2)
                    nc.scalar.activation(g.hf[:, k, 0:w], ps[:, 4 + bank, 0:w], ACT.Relu,
                                         scale=g.f_in[:, half], bias=g.b1[:, half, f:f + 1])
                    act.drain().then_inc(s.relu, 1)
                    wait(act, s.l2, n - 2)
                    nc.scalar.activation(g.hh[:, k, 0:w], g.hf[:, k, 0:w], ACT.Copy).then_inc(s.h_high, 1)
                    q = prepared(ep, i)
                    step = (i % NG - 1) * FC + f - 4
                    if 0 <= step < 8 and q is not None:
                        which, part = step // 4, step % 2
                        raw, hi = ((g.w1_raw, g.w1_hi), (g.w2_raw, g.w2_hi))[which]
                        chunks = (DC, FC)[which] // 2
                        at = slice(part * chunks, (part + 1) * chunks)
                        if step % 4 < 2:
                            act.wait_ge(s.w_sc, q + 1)
                            nc.scalar.activation(raw[:, at], raw[:, at], ACT.Copy,
                                                 scale=g.f_sc[:, 1 - half, which:which + 1])
                        else:
                            if part == 0:
                                act.drain()
                            nc.scalar.activation(hi[:, 1 - half, at], raw[:, at], ACT.Copy)
                        if step % 4 == 3:
                            act.drain().then_inc(s.w_high, 1)

            for c in range(DC):
                high(0, 0, c)
            rounds(act, group)

        @block.vector
        def _(dve):
            v = nc.vector

            def low(ep, i, c):
                dve.wait_ge(s.x_high, count(ep, i) * DC + (c + 1))
                w = tiles(i) * P
                v.scalar_tensor_tensor(out=g.x_lo[:, i % 2, c, 0:w], in0=ps[:, 7, 0:w], scalar=A_SCALE,
                                       in1=g.x_hi[:, i % 2, c, 0:w], op0=ALU.mult, op1=ALU.subtract)\
                    .then_inc(s.x_low, 1)

            def collect(ep, i):
                half = i // NG
                dve.wait_ge(s.l2, (count(ep, i) + 1) * FC)
                for t in range(tiles(i)):
                    m = rows_of(i, t)
                    v.scalar_tensor_tensor(out=g.y[0:m, t], in0=ps[0:m, i % 2 * 2 + t // 2, t % 2 * D:(t % 2 + 1) * D],
                                           scalar=g.f_out[0:m, half], in1=g.b2[0:m, half],
                                           op0=ALU.mult, op1=ALU.add)
                dve.drain().then_inc(s.y_made, 1)

            def finish(ep, i, stage):
                w = tiles(i)
                y, sign, finite, res = g.y[:, 0:w], g.sign[:, 0:w], g.finite[:, 0:w], g.res[:, i % 2, 0:w]
                z = g.tok[:, i % 3, 0:w, D:2 * D]
                if stage == 0:
                    dve.wait_ge(s.got[i % 3], got(ep, i))
                    for t in range(w):
                        v.tensor_scalar(g.y[:, t], g.y[:, t], g.tok[:, i % 3, t, 2 * D:ROW], None, ALU.mult)
                    dve.drain()
                    v.tensor_scalar(sign, y, float("inf"), None, ALU.is_equal)
                    v.tensor_scalar(finite, y, 0.0, 0.0, ALU.mult, ALU.is_equal)
                if stage == 1:
                    v.scalar_tensor_tensor(out=sign, in0=y, scalar=float("-inf"), in1=sign,
                                           op0=ALU.is_equal, op1=ALU.subtract)
                if stage == 2:
                    before = (ep, i - 2) if i >= 2 else (ep - 1, i + PG - 2)
                    if not (isinstance(before[0], int) and before[0] < 0):
                        dve.wait_ge(s.put[i % 2], put(*before))
                        settle(g, dve)
                    v.scalar_tensor_tensor(out=res, in0=sign, scalar=-10000.0, in1=z, op0=ALU.mult, op1=ALU.add)
                if stage == 3:
                    v.tensor_tensor(y, y, z, ALU.add)
                if stage == 4:
                    v.copy_predicated(res, finite, y)
                dve.drain()
                if stage == 4:
                    dve.sem_inc(s.y_done, 1)

            def group(ep, i):
                w, half = width(i), i // NG
                started = not (isinstance(ep, int) and ep == 0 and i == 0)
                before = (ep, i - 1) if i else (ep - 1, PG - 1)
                q = prepared(ep, i)
                for f in range(FC):
                    n, k = count(ep, i) * FC + f, (i * FC + f) % 3
                    if f in (4, 6) and later(ep, i, 1):
                        low(*later(ep, i, 1), f // 2 - 2)
                    dve.wait_ge(s.h_high, n + 1)
                    v.tensor_tensor(g.hl[:, k, 0:w], g.hf[:, k, 0:w], g.hh[:, k, 0:w], ALU.subtract)\
                        .then_inc(s.h_low, 1)
                    if f == 1 and started:
                        collect(*before)
                    if f >= 2 and f - 2 < 5 and started:
                        finish(*before, f - 2)
                    if q is not None and (i % NG, f) == (0, FC - 1):
                        dve.wait_ge(s.f_w, q * 64 + 64)
                        expert_largest(nc, g, dve, 1 - half, 0)
                    if q is not None and (i % NG, f) == (1, 0):
                        expert_largest(nc, g, dve, 1 - half, 1)
                        dve.drain().then_inc(s.w_max, 1)
                    if q is not None and (i % NG, f) == (1, 3):
                        dve.wait_ge(s.w_red, q + 1)
                        expert_scales(nc, g, dve, 1 - half)
                        dve.drain().then_inc(s.w_sc, 1)

            for c in range(DC):
                low(0, 0, c)
            rounds(dve, group)
            collect(ROUNDS - 1, PG - 1)
            for stage in range(5):
                finish(ROUNDS - 1, PG - 1, stage)

        @block.tensor
        def _(pe):
            def turn(ep, i, c):
                if c == 0:
                    pe.wait_ge(s.got[i % 3], got(ep, i))
                wait(pe, s.x_low, count(ep, i) * DC + c)
                for t in range(tiles(i)):
                    last = nc.tensor.transpose(ps[:, 7, t * P:(t + 1) * P],
                                               g.tok[:, i % 3, t, c * P:(c + 1) * P], g.ident[:])
                last.then_inc(s.turned, 1)

            def hidden(ep, i, f):
                half, w, n = i // NG, width(i), count(ep, i) * FC + f
                if f == 0:
                    pe.wait_ge(s.x_low, (count(ep, i) + 1) * DC)
                    if i % NG == 0:
                        wait(pe, s.w_low, (ep * PAIR + half) * 2)
                wait(pe, s.relu, n - 2)
                k, cols = (i * FC + f) % 3, slice(f * P, (f + 1) * P)
                products(nc, ps[:, 4 + k, 0:w], [(g.w1_hi[:, half, c, cols], g.w1_lo[:, half, c, cols],
                                                  g.x_hi[:, i % 2, c, 0:w], g.x_lo[:, i % 2, c, 0:w])
                                                 for c in range(DC)]).then_inc(s.l1, 1)

            def output(ep, i, f):
                half, n, k = i // NG, count(ep, i) * FC + f, (i * FC + f) % 3
                pe.wait_ge(s.h_low, n + 1)
                if f == 0:
                    wait(pe, s.y_made, count(ep, i) - 1)
                for t in reversed(range(tiles(i))) if f == FC - 1 else range(tiles(i)):
                    m = rows_of(i, t)
                    at = slice(t * P, t * P + m)
                    last = products(nc, ps[0:m, i % 2 * 2 + t // 2, t % 2 * D:(t % 2 + 1) * D],
                                    [(g.hh[:, k, at], g.hl[:, k, at], g.w2_hi[:, half, f], g.w2_lo[:, half, f])],
                                    start=f == 0 and t % 2 == 0,
                                    stop=f == FC - 1 and t % 2 == 0)
                last.then_inc(s.l2, 1)

            def group(ep, i):
                for f in range(FC):
                    if f in (3, 5) and later(ep, i, 1):
                        turn(*later(ep, i, 1), f // 2 - 1)
                    ahead = (ep, i) if f < FC - 2 else later(ep, i, 1)
                    if ahead:
                        hidden(*ahead, (f + 2) % FC)
                    output(ep, i, f)

            turn(0, 0, 0)
            turn(0, 0, 1)
            hidden(0, 0, 0)
            hidden(0, 0, 1)
            rounds(pe, group)


class Arena:

    def __init__(self, words, at):
        self.words, self.at = words, at

    def take(self, shape, dt):
        n = 1
        for x in shape[1:]:
            n *= x
        n = n if dt != F16 else n // 2
        view = self.words[:, self.at:self.at + n]
        self.at += n
        if dt != F32:
            view = view.bitcast(dt)
        if len(shape) == 3:
            view = view.rearrange("p (a b) -> p a b", b=shape[2])
        if len(shape) == 4:
            view = view.rearrange("p (a b c) -> p a b c", b=shape[2], c=shape[3])
        return view


def tower(nc, a):
    g = Names()
    g.w_hi = nc.alloc_sbuf_tensor("w_hi", [P, 3, DC, D], F16)
    g.w_lo = nc.alloc_sbuf_tensor("w_lo", [P, 3, DC, D], F16)
    g.lin_t = nc.alloc_sbuf_tensor("lin_t", [P, DC, D], F32)
    g.gate_w = nc.alloc_sbuf_tensor("gate_w", [P, DC, E], F32)
    g.taps = nc.alloc_sbuf_tensor("taps", [P, DC, 9], F32)
    g.vecs = nc.alloc_sbuf_tensor("vecs", [P, 8, DC], F32)
    g.lin_b = nc.alloc_sbuf_tensor("lin_b", [P, D], F32)
    g.bv = nc.alloc_sbuf_tensor("bv", [P, D], F32)
    g.gate_b = nc.alloc_sbuf_tensor("gate_b", [P, E], F32)
    g.mx = nc.alloc_sbuf_tensor("mx", [P, 6], F32)
    g.sc = nc.alloc_sbuf_tensor("sc", [P, 6], F32)
    g.isc = nc.alloc_sbuf_tensor("isc", [P, 6], F32)
    g.ratio = nc.alloc_sbuf_tensor("ratio", [P, 3], F32)
    g.score = nc.alloc_sbuf_tensor("score", [P, 1], F32)
    g.bqk = nc.alloc_sbuf_tensor("bqk", [P, 2, DC], F32)
    g.bn_v = nc.alloc_sbuf_tensor("bn_v", [P, DC], F32)
    g.bn_r = nc.alloc_sbuf_tensor("bn_r", [P, DC], F32)
    g.bn_s = nc.alloc_sbuf_tensor("bn_s", [P, DC], F32)
    g.bn_h = nc.alloc_sbuf_tensor("bn_h", [P, DC], F32)
    g.ones = nc.alloc_sbuf_tensor("ones", [P, P], F32)
    g.ones16 = nc.alloc_sbuf_tensor("ones16", [P, P], F16)
    g.upper = nc.alloc_sbuf_tensor("upper", [P, P], F16)
    g.ident = nc.alloc_sbuf_tensor("ident", [P, P], F32)
    g.expo = nc.alloc_sbuf_tensor("expo", [P, SUB], F32)
    g.carry = nc.alloc_sbuf_tensor("carry", [P, E], F32)
    g.t_diag = nc.alloc_sbuf_tensor("t_diag", [P, DC, UPPER, P], F32)
    g.warm = nc.alloc_sbuf_tensor("warm", [P, 1], F32)
    g.tok_f = nc.alloc_sbuf_tensor("tok_f", [P, SUB], F32)
    g.tok_i = nc.alloc_sbuf_tensor("tok_i", [P, SUB], I32)
    g.weight = nc.alloc_sbuf_tensor("weight", [P, SUB, E], F32)
    g.slot0 = nc.alloc_sbuf_tensor("slot0", [P, SUB, E], F32)
    g.st = nc.alloc_sbuf_tensor("st", [P, SUB, 6], F32)
    g.mv = nc.alloc_sbuf_tensor("mv", [P, SUB, 2], F32)
    g.var = nc.alloc_sbuf_tensor("var", [P, SUB], F32)
    g.rstd = nc.alloc_sbuf_tensor("rstd", [P, SUB], F32)
    g.rs = nc.alloc_sbuf_tensor("rs", [P, SUB], F32)
    g.r_l = nc.alloc_sbuf_tensor("r_l", [P, SUB, E], F32)
    g.r_e = nc.alloc_sbuf_tensor("r_e", [P, SUB, E], F32)
    g.r_k = nc.alloc_sbuf_tensor("r_k", [P, SUB, E], F32)
    g.r_oh = nc.alloc_sbuf_tensor("r_oh", [P, SUB, E], F16)
    g.r_m = nc.alloc_sbuf_tensor("r_m", [P, SUB], F32)
    g.r_d = nc.alloc_sbuf_tensor("r_d", [P, SUB], F32)
    g.r_x = nc.alloc_sbuf_tensor("r_x", [P, SUB], F32)
    g.idx_f = nc.alloc_sbuf_tensor("idx_f", [P, SUB], F32)
    g.idx_i = nc.alloc_sbuf_tensor("idx_i", [P, SUB], I32)
    g.c_m = nc.alloc_sbuf_tensor("c_m", [P, 1], F32)
    g.c_m1 = nc.alloc_sbuf_tensor("c_m1", [P, 1], F32)
    g.c_hb = nc.alloc_sbuf_tensor("c_hb", [P, 1, D], F32)
    g.c_q = nc.alloc_sbuf_tensor("c_q", [P, DC, 2], F16)
    g.c_k = nc.alloc_sbuf_tensor("c_k", [P, DC, 2], F16)
    g.c_v = nc.alloc_sbuf_tensor("c_v", [P, D], F32)
    g.ck_s = nc.alloc_sbuf_tensor("ck_s", [P, SUB], F32)
    g.ck_d = nc.alloc_sbuf_tensor("ck_d", [P, SUB], F32)
    g.ck_new = nc.alloc_sbuf_tensor("ck_new", [P, SUB], F32)
    g.ck_w = nc.alloc_sbuf_tensor("ck_w", [P, SUB], F32)
    g.ck_c = nc.alloc_sbuf_tensor("ck_c", [P, SUB], F32)
    g.c_s = nc.alloc_sbuf_tensor("c_s", [P, KT], F32)
    g.c_hi = nc.alloc_sbuf_tensor("c_hi", [P, KT + 1], F16)
    g.c_lo = nc.alloc_sbuf_tensor("c_lo", [P, KT + 1], F16)
    g.mq = nc.alloc_sbuf_tensor("mq", [P, SUB], F32)
    words = 48300
    g.arena = nc.alloc_sbuf_tensor("arena", [P, words], F32)
    g.ps = nc.alloc_psum_tensor("ps", [P, 8, 512], F32)

    kept = Arena(g.arena, 0)
    g.q_hi = kept.take([P, DC, N + 7], F16)
    g.q_lo = kept.take([P, DC, N + 7], F16)
    g.k_hi = kept.take([P, DC, N + 7], F16)
    g.k_lo = kept.take([P, DC, N + 7], F16)
    g.v_hi = kept.take([P, KT, VW + 3], F16)
    g.v_lo = kept.take([P, KT, D], F16)
    g.v_hi = g.v_hi[:, :, 0:VW]
    g.row = kept.take([P, SUB, ROW], F32)
    g.hb = kept.take([P, SUB, D], F32)
    strips = Arena(g.arena, kept.at)
    g.xp = strips.take([P, DC, PW, PW], F32)
    g.x_in = strips.take([P, 2, DC, QB], F32)
    g.y_t = strips.take([P, 2, DC, QB], F32)
    g.h = strips.take([P, SUB, D], F32)
    g.a = strips.take([P, SUB, D], F32)
    g.a_hi = strips.take([P, 2, DC, QB], F16)
    g.a_lo = strips.take([P, 2, DC, QB], F16)
    g.p_f = strips.take([P, 2, QB], F32)
    blocks = Arena(g.arena, kept.at)
    g.panel = blocks.take([P, NT, QB], F32)
    g.ph = blocks.take([P, 3, QB], F16)
    g.pl = blocks.take([P, 3, QB], F16)
    g.r = blocks.take([P, QB], F32)
    g.m = blocks.take([P, QB], F32)
    g.z_t = blocks.take([P, DC, QB], F32)
    g.diag = g.z_t[:, 0]
    mixture = Arena(g.arena, 0)
    g.w1_raw = mixture.take([P, DC, F], F32)
    g.w2_raw = mixture.take([P, FC, D], F32)
    g.w1_hi = mixture.take([P, PAIR, DC, F], F16)
    g.w1_lo = mixture.take([P, PAIR, DC, F], F16)
    g.w2_hi = mixture.take([P, PAIR, FC, D], F16)
    g.w2_lo = mixture.take([P, PAIR, FC, D], F16)
    g.b1 = mixture.take([P, PAIR, FC], F32)
    g.b2 = mixture.take([P, PAIR, D], F32)
    g.tok = mixture.take([P, 3, SUB, ROW], F32)
    g.x_hi = mixture.take([P, 2, DC, QB], F16)
    g.x_lo = mixture.take([P, 2, DC, QB], F16)
    g.hf = mixture.take([P, 3, QB], F32)
    g.hh = mixture.take([P, 3, QB], F16)
    g.hl = mixture.take([P, 3, QB], F16)
    g.y = mixture.take([P, SUB, D], F32)
    g.sign = mixture.take([P, SUB, D], F32)
    g.finite = mixture.take([P, SUB, D], I32)
    g.res = mixture.take([P, 2, SUB, D], F32)
    g.ids = mixture.take([P, PAIR * NG, SUB], I32)
    g.f_mx = mixture.take([P, PAIR, 3], F32)
    g.f_sc = mixture.take([P, PAIR, 3], F32)
    g.f_isc = mixture.take([P, PAIR, 3], F32)
    g.f_in = mixture.take([P, PAIR, 1], F32)
    g.f_out = mixture.take([P, PAIR, 1], F32)
    first = Arena(g.arena, strips.at)
    g.w_raw = first.take([P, 3, DC, D], F32)
    g.zrow = first.take([P, ROW], F32)
    g.iota_i = first.take([P, SUB], I32)
    g.weight_i = first.take([P, SUB, E], I32)
    g.base_i = first.take([P, SUB, E], I32)
    g.none_f = first.take([P, E * STRIDE // P], F32)
    g.none_i = first.take([P, E * STRIDE // P], I32)
    assert max(first.at, blocks.at, mixture.at) <= words

    g.table = nc.dram_tensor("slot_tokens", [E * STRIDE, 1], I32, kind="Internal").ap()
    g.rows = nc.dram_tensor("token_rows", [T + 1, ROW], F32, kind="Internal").ap()
    g.h_res = nc.dram_tensor("residual_rows", [B, NP, D], F32, kind="Internal").ap()

    setup(nc, g, a)
    class_row(nc, g, a)
    s = Names()
    (s.cleared, s.x_in0, s.x_in1, s.xn, s.y_t, s.lin, s.h_made, s.h_out, s.var, s.rstd, s.a, s.aT, s.a_hi,
     s.a_lo, s.proj, s.p_f, s.p_hi, s.p_lo, s.early, s.upper, s.started, s.hb, s.o, s.var2, s.rstd2, s.z, s.zT,
     s.z_t, s.logits, s.l_sub, s.l_exp, s.routed, s.prefix, s.slots, s.o_out, s.r_out, s.h_in, s.sub, s.m,
     s.m_ps, s.p_hi2, s.p_lo2, s.pv, s.qk, s.kept, s.maxed, s.r_t, s.diag, s.settled, s.c_qk, s.c_maxed,
     s.c_turned, s.c_top, s.c_spread, s.c_sub, s.c_high, s.c_low, s.c_pv, s.freed, s.ck_made, s.ck_read,
     s.ck_sub, s.ck_exp) = s.handles = semaphores(
        nc, "cleared x_in0 x_in1 xn y_t lin h_made h_out var rstd a aT a_hi a_lo proj p_f p_hi p_lo early upper "
            "started hb o var2 rstd2 z zT z_t logits l_sub l_exp routed prefix slots o_out r_out h_in sub m m_ps "
            "p_hi2 p_lo2 pv qk kept maxed r_t diag settled c_qk c_maxed c_turned c_top c_spread c_sub c_high "
            "c_low c_pv freed ck_made ck_read ck_sub ck_exp")
    s.x_in, g.settled = (s.x_in0, s.x_in1), s.settled
    s.tab, = semaphores(nc, "tab")
    with nc.Fori(0, B) as b:
        clear(nc, s)
        s.tab0 = b * (16 * (SUB * NQB + 1))
        tokenizer(nc, g, a, b, s)
        attention(nc, g, a, b, s)
    f = Names()
    (f.f_w, f.w_max, f.w_red, f.w_sc, f.w_high, f.w_low, f.turned, f.x_high, f.x_low, f.l1, f.relu, f.h_high,
     f.h_low, f.l2, f.y_made, f.y_done) = semaphores(
        nc, "f_w w_max w_red w_sc w_high w_low turned x_high x_low l1 relu h_high h_low l2 y_made y_done")
    f.ids = semaphores(nc, "ids0 ids1 ids2 ids3 ids4 ids5")
    f.got, f.put = semaphores(nc, "got0 got1 got2"), semaphores(nc, "put0 put1")
    first_expert(nc, g, a, f)
    experts(nc, g, a, f)


_INS = ["xT", "cls_tok", "L0_tok_bn_gamma", "L0_tok_bn_beta", "L0_tok_bn_mean", "L0_tok_bn_var", "conv_taps",
        "L0_tok_conv_b", "lin_wT", "L0_tok_lin_b", "L0_attn_Wq", "L0_attn_bq", "L0_attn_Wk", "L0_attn_bk",
        "L0_attn_Wv", "L0_attn_bv", "L0_ffn_gate_w", "L0_ffn_gate_b", "L0_ffn_w1", "L0_ffn_b1", "L0_ffn_w2",
        "L0_ffn_b2"]


def kernel(**inputs):
    import numpy as _np
    import concourse.bacc as _bacc
    from concourse.bass_utils import run_bass_kernel_spmd as _run

    laid = {k: _np.asarray(v) for k, v in inputs.items()}
    laid["xT"] = laid["x"].reshape(B, NP, D).transpose(0, 2, 1)
    laid["conv_taps"] = laid["L0_tok_conv_w"].reshape(D, 9)
    laid["lin_wT"] = laid["L0_tok_lin_w"].T
    nc = _bacc.Bacc("TRN2", target_bir_lowering=False, num_devices=1)
    arrays, a = {}, {}
    for name in _INS:
        arrays[f"in_{name}"] = _np.ascontiguousarray(laid[name])
        a[name] = nc.dram_tensor(f"in_{name}", arrays[f"in_{name}"].shape, F32, kind="ExternalInput").ap()
    a["out"] = nc.dram_tensor("out_tokens", (B, N, D), F32, kind="ExternalOutput").ap()
    tower(nc, a)
    r = _run(nc, [arrays], core_ids=[0])
    return r.results[0]["out_tokens"]
```
